# Optimizing a Trainium2 kernel written in Bass

```python
import numpy as np
import jax
import jax.numpy as jnp

def _softmax(x, axis=-1):
    return jax.nn.softmax(x, axis=axis)

def _gelu(x):
    return jax.nn.gelu(x, approximate=True)

def _silu(x):
    return jax.nn.silu(x)

def _sigmoid(x):
    return jax.nn.sigmoid(x)

def _layernorm(x, axis=-1, eps=1e-05):
    m = jnp.mean(x, axis=axis, keepdims=True)
    v = jnp.var(x, axis=axis, keepdims=True)
    return (x - m) / jnp.sqrt(v + eps)

def _scatter_add(tgt, idx, src, axis=0):
    return tgt.at[idx].add(src)

def _segment_sum(src, seg, n):
    return jax.ops.segment_sum(src, seg, n)
kernel_name = 'mk_flamingo_gated_d1_seqx_r4_63adb7'

def setup_inputs(seed: int=0):
    np.random.seed(seed)
    _w = jnp.asarray

    def _rec_inputs():
        import jax
        import jax.numpy as jnp
        _rk = jax.random.key(seed)
        x = 7.22e-05 + 1 * jax.random.normal(jax.random.fold_in(_rk, 1), (4, 512, 256), jnp.float32)
        _lenS = 512 - jax.random.randint(jax.random.fold_in(_rk, 7), (4,), 0, max(1, 512 // 4) + 1, jnp.int32)
        _lenS2 = 512 - jax.random.randint(jax.random.fold_in(_rk, 8), (4,), 0, max(1, 512 // 4) + 1, jnp.int32)
        _ctx_1024P = jax.random.normal(jax.random.fold_in(_rk, 11), (4, 16, 256), jnp.float32)
        _ctx_1024c = jax.random.dirichlet(jax.random.fold_in(_rk, 511), 0.3 * jnp.ones((16,), jnp.float32), (4, 512))
        _ctx_1024t = jnp.einsum('bsk,bkd->bsd', _ctx_1024c, _ctx_1024P)
        _ctx_1024t = _ctx_1024t * jax.lax.rsqrt(jnp.mean(jnp.square(_ctx_1024t)) + 1e-12) * 0.953939
        ctx_1024 = 4.13588e-05 + 0.999923 * (_ctx_1024t + 0.3 * jax.random.normal(jax.random.fold_in(_rk, 611), (4, 512, 256), jnp.float32))
        _g = jax.random.normal(jax.random.fold_in(_rk, 9001), (2, 1), jnp.float32)
        _g = jnp.sign(_g) * jnp.maximum(jnp.abs(_g), 1.0) + (_g == 0) * 1.0
        g_xattn = _g[0]
        g_ffn = _g[1]
        return (x, ctx_1024, g_xattn, g_ffn)
    x, ctx_1024, g_xattn, g_ffn = _rec_inputs()

    def _L0_xattn_setup():
        import jax, jax.numpy as jnp
        import numpy as np
        B, T, D, H = (4, 512, 256, 1024)
        S = 64
        EPS = 1e-05

        def _layer_norm(x, gamma, beta):
            mu = jnp.mean(x, axis=-1, keepdims=True)
            var = jnp.mean(jnp.square(x - mu), axis=-1, keepdims=True)
            return (x - mu) * jax.lax.rsqrt(var + EPS) * gamma + beta

        def _aft_local(emb, wq, bq, wk, bk, wv, bv, wo, bo, pos_bias):
            q = emb @ wq + bq
            k = emb @ wk + bk
            v = emb @ wv + bv
            idx = jnp.arange(T)
            mask = (jnp.abs(idx[:, None] - idx[None, :]) < S).astype(pos_bias.dtype)
            w = pos_bias * mask
            max_k = jnp.max(k, axis=1, keepdims=True)
            max_w = jnp.max(w, axis=1, keepdims=True)
            ek = jnp.exp(k - max_k)
            ew = jnp.exp(w - max_w)
            num = jnp.einsum('tj,bjd->btd', ew, ek * v)
            den = jnp.einsum('tj,bjd->btd', ew, ek)
            y = jax.nn.sigmoid(q) * num / den
            return y @ wo + bo
        key = jax.random.key(seed)
        ks = jax.random.split(key, 16)
        sd = 0.02
        return {'x': jax.random.normal(ks[0], (B, T, D), jnp.float32), 'pos_encod': jax.random.normal(ks[1], (B, T, D), jnp.float32), 'wq': jax.random.normal(ks[2], (D, D), jnp.float32) * sd, 'bq': jnp.zeros((D,), jnp.float32), 'wk': jax.random.normal(ks[3], (D, D), jnp.float32) * sd, 'bk': jnp.zeros((D,), jnp.float32), 'wv': jax.random.normal(ks[4], (D, D), jnp.float32) * sd, 'bv': jnp.zeros((D,), jnp.float32), 'wo': jax.random.normal(ks[5], (D, D), jnp.float32) * sd, 'bo': jnp.zeros((D,), jnp.float32), 'pos_bias': jax.random.normal(ks[6], (T, T), jnp.float32) * sd, 'gamma': jnp.ones((D,), jnp.float32), 'beta': jnp.zeros((D,), jnp.float32), 'w1': jax.random.normal(ks[7], (D, H), jnp.float32) * sd, 'b1': jnp.zeros((H,), jnp.float32), 'w2': jax.random.normal(ks[8], (H, D), jnp.float32) * sd, 'b2': jnp.zeros((D,), jnp.float32)}
    _L0_xattn_all = _L0_xattn_setup()
    _L0_xattn_in = {k: v for k, v in _L0_xattn_all.items() if k in ('wq', 'bq', 'wk', 'bk', 'wv', 'bv', 'wo', 'bo', 'pos_bias', 'gamma', 'beta', 'w1', 'b1', 'w2', 'b2')}
    del _L0_xattn_all

    def _L0_ffn_setup():
        import jax, jax.numpy as jnp
        import numpy as np
        B, S, D, H, M, E, K = (4, 256, 256, 16, 2, 8, 2)
        KD = D // H
        F = 2 * D
        EPS = 1e-06

        def _ln(x, g, b):
            m = jnp.mean(x, axis=-1, keepdims=True)
            v = jnp.mean(jnp.square(x - m), axis=-1, keepdims=True)
            return (x - m) * jax.lax.rsqrt(v + EPS) * g + b
        key = jax.random.key(seed)
        ks = jax.random.split(key, 12)
        r = lambda i, shape: jax.random.normal(ks[i], shape, jnp.float32) * 0.02
        return {'x': jax.random.normal(ks[0], (B, S, D), jnp.float32), 'ln1_g': jnp.ones((D,), jnp.float32), 'ln1_b': jnp.zeros((D,), jnp.float32), 'ln2_g': jnp.ones((D,), jnp.float32), 'ln2_b': jnp.zeros((D,), jnp.float32), 'mha_wq': r(1, (M, D, H, KD)), 'mha_bq': jnp.zeros((M, H, KD), jnp.float32), 'mha_wk': r(2, (M, D, H, KD)), 'mha_bk': jnp.zeros((M, H, KD), jnp.float32), 'mha_wv': r(3, (M, D, H, KD)), 'mha_bv': jnp.zeros((M, H, KD), jnp.float32), 'mha_wo': r(4, (M, H, KD, D)), 'mha_bo': jnp.zeros((M, D), jnp.float32), 'mha_rw': r(5, (D, M)), 'mha_rb': jnp.zeros((M,), jnp.float32), 'ffn_rw': r(6, (D, E)), 'ffn_rb': jnp.zeros((E,), jnp.float32), 'fw1': r(7, (E, D, F)), 'fw2': r(8, (E, F, D))}
    _L0_ffn_all = _L0_ffn_setup()
    _L0_ffn_in = {k: v for k, v in _L0_ffn_all.items() if k in ('ln1_g', 'ln1_b', 'ln2_g', 'ln2_b', 'mha_wq', 'mha_bq', 'mha_wk', 'mha_bk', 'mha_wv', 'mha_bv', 'mha_wo', 'mha_bo', 'mha_rw', 'mha_rb', 'ffn_rw', 'ffn_rb', 'fw1', 'fw2')}
    del _L0_ffn_all
    return {'x': x, 'ctx_1024': ctx_1024, 'g_xattn': g_xattn, 'g_ffn': g_ffn, 'L0_xattn_wq': _L0_xattn_in['wq'], 'L0_xattn_bq': _L0_xattn_in['bq'], 'L0_xattn_wk': _L0_xattn_in['wk'], 'L0_xattn_bk': _L0_xattn_in['bk'], 'L0_xattn_wv': _L0_xattn_in['wv'], 'L0_xattn_bv': _L0_xattn_in['bv'], 'L0_xattn_wo': _L0_xattn_in['wo'], 'L0_xattn_bo': _L0_xattn_in['bo'], 'L0_xattn_pos_bias': _L0_xattn_in['pos_bias'], 'L0_xattn_gamma': _L0_xattn_in['gamma'], 'L0_xattn_beta': _L0_xattn_in['beta'], 'L0_xattn_w1': _L0_xattn_in['w1'], 'L0_xattn_b1': _L0_xattn_in['b1'], 'L0_xattn_w2': _L0_xattn_in['w2'], 'L0_xattn_b2': _L0_xattn_in['b2'], 'L0_ffn_ln1_g': _L0_ffn_in['ln1_g'], 'L0_ffn_ln1_b': _L0_ffn_in['ln1_b'], 'L0_ffn_ln2_g': _L0_ffn_in['ln2_g'], 'L0_ffn_ln2_b': _L0_ffn_in['ln2_b'], 'L0_ffn_mha_wq': _L0_ffn_in['mha_wq'], 'L0_ffn_mha_bq': _L0_ffn_in['mha_bq'], 'L0_ffn_mha_wk': _L0_ffn_in['mha_wk'], 'L0_ffn_mha_bk': _L0_ffn_in['mha_bk'], 'L0_ffn_mha_wv': _L0_ffn_in['mha_wv'], 'L0_ffn_mha_bv': _L0_ffn_in['mha_bv'], 'L0_ffn_mha_wo': _L0_ffn_in['mha_wo'], 'L0_ffn_mha_bo': _L0_ffn_in['mha_bo'], 'L0_ffn_mha_rw': _L0_ffn_in['mha_rw'], 'L0_ffn_mha_rb': _L0_ffn_in['mha_rb'], 'L0_ffn_ffn_rw': _L0_ffn_in['ffn_rw'], 'L0_ffn_ffn_rb': _L0_ffn_in['ffn_rb'], 'L0_ffn_fw1': _L0_ffn_in['fw1'], 'L0_ffn_fw2': _L0_ffn_in['fw2']}

def reference(x, ctx_1024, g_xattn, g_ffn, L0_xattn_wq, L0_xattn_bq, L0_xattn_wk, L0_xattn_bk, L0_xattn_wv, L0_xattn_bv, L0_xattn_wo, L0_xattn_bo, L0_xattn_pos_bias, L0_xattn_gamma, L0_xattn_beta, L0_xattn_w1, L0_xattn_b1, L0_xattn_w2, L0_xattn_b2, L0_ffn_ln1_g, L0_ffn_ln1_b, L0_ffn_ln2_g, L0_ffn_ln2_b, L0_ffn_mha_wq, L0_ffn_mha_bq, L0_ffn_mha_wk, L0_ffn_mha_bk, L0_ffn_mha_wv, L0_ffn_mha_bv, L0_ffn_mha_wo, L0_ffn_mha_bo, L0_ffn_mha_rw, L0_ffn_mha_rb, L0_ffn_ffn_rw, L0_ffn_ffn_rb, L0_ffn_fw1, L0_ffn_fw2):
    import jax
    import jax.numpy as jnp

    def _L0_xattn_ref(x, pos_encod, wq, bq, wk, bk, wv, bv, wo, bo, pos_bias, gamma, beta, w1, b1, w2, b2):
        import jax, jax.numpy as jnp
        import numpy as np
        B, T, D, H = (4, 512, 256, 1024)
        S = 64
        EPS = 1e-05

        def _layer_norm(x, gamma, beta):
            mu = jnp.mean(x, axis=-1, keepdims=True)
            var = jnp.mean(jnp.square(x - mu), axis=-1, keepdims=True)
            return (x - mu) * jax.lax.rsqrt(var + EPS) * gamma + beta

        def _aft_local(emb, wq, bq, wk, bk, wv, bv, wo, bo, pos_bias):
            q = emb @ wq + bq
            k = emb @ wk + bk
            v = emb @ wv + bv
            idx = jnp.arange(T)
            mask = (jnp.abs(idx[:, None] - idx[None, :]) < S).astype(pos_bias.dtype)
            w = pos_bias * mask
            max_k = jnp.max(k, axis=1, keepdims=True)
            max_w = jnp.max(w, axis=1, keepdims=True)
            ek = jnp.exp(k - max_k)
            ew = jnp.exp(w - max_w)
            num = jnp.einsum('tj,bjd->btd', ew, ek * v)
            den = jnp.einsum('tj,bjd->btd', ew, ek)
            y = jax.nn.sigmoid(q) * num / den
            return y @ wo + bo
        emb = x + pos_encod
        attn = _aft_local(emb, wq, bq, wk, bk, wv, bv, wo, bo, pos_bias)
        a = _layer_norm(attn + emb, gamma, beta)
        ff = jax.nn.relu(a @ w1 + b1) @ w2 + b2
        return _layer_norm(ff + a, gamma, beta)

    def _L0_ffn_ref(x, ln1_g, ln1_b, ln2_g, ln2_b, mha_wq, mha_bq, mha_wk, mha_bk, mha_wv, mha_bv, mha_wo, mha_bo, mha_rw, mha_rb, ffn_rw, ffn_rb, fw1, fw2):
        import jax, jax.numpy as jnp
        import numpy as np
        B, S, D, H, M, E, K = (4, 256, 256, 16, 2, 8, 2)
        KD = D // H
        F = 2 * D
        EPS = 1e-06

        def _ln(x, g, b):
            m = jnp.mean(x, axis=-1, keepdims=True)
            v = jnp.mean(jnp.square(x - m), axis=-1, keepdims=True)
            return (x - m) * jax.lax.rsqrt(v + EPS) * g + b
        n1 = _ln(x, ln1_g, ln1_b)
        mha_probs = jax.nn.softmax(jnp.mean(n1, axis=1) @ mha_rw + mha_rb, axis=-1)
        q = jnp.einsum('btd,mdhk->mbhtk', n1, mha_wq) + mha_bq[:, None, :, None, :]
        kk = jnp.einsum('btd,mdhk->mbhtk', n1, mha_wk) + mha_bk[:, None, :, None, :]
        v = jnp.einsum('btd,mdhk->mbhtk', n1, mha_wv) + mha_bv[:, None, :, None, :]
        scores = jnp.einsum('mbhtk,mbhsk->mbhts', q, kk) / jnp.sqrt(jnp.float32(KD))
        attn = jax.nn.softmax(scores, axis=-1)
        ctx = jnp.einsum('mbhts,mbhsk->mbthk', attn, v)
        mha_out = jnp.einsum('mbthk,mhkd->mbtd', ctx, mha_wo) + mha_bo[:, None, None, :]
        x = x + jnp.einsum('mbtd,bm->btd', mha_out, mha_probs)
        n2 = _ln(x, ln2_g, ln2_b)
        ffn_probs = jax.nn.softmax(jnp.mean(n2, axis=1) @ ffn_rw + ffn_rb, axis=-1)
        topk_p, topk_i = jax.lax.top_k(ffn_probs, K)
        topk_p = topk_p / jnp.sum(topk_p, axis=-1, keepdims=True)
        sw1 = fw1[topk_i]
        sw2 = fw2[topk_i]
        h = jax.nn.gelu(jnp.einsum('btd,bkdf->bktf', n2, sw1), approximate=False)
        eo = jnp.einsum('bktf,bkfd->bktd', h, sw2)
        return x + jnp.einsum('bktd,bk->btd', eo, topk_p)
    x = x + jnp.tanh(g_xattn[0]) * _L0_xattn_ref(_layernorm(x, axis=-1), ctx_1024, L0_xattn_wq, L0_xattn_bq, L0_xattn_wk, L0_xattn_bk, L0_xattn_wv, L0_xattn_bv, L0_xattn_wo, L0_xattn_bo, L0_xattn_pos_bias, L0_xattn_gamma, L0_xattn_beta, L0_xattn_w1, L0_xattn_b1, L0_xattn_w2, L0_xattn_b2)
    x = x + jnp.tanh(g_ffn[0]) * _L0_ffn_ref(_layernorm(x, axis=-1), L0_ffn_ln1_g, L0_ffn_ln1_b, L0_ffn_ln2_g, L0_ffn_ln2_b, L0_ffn_mha_wq, L0_ffn_mha_bq, L0_ffn_mha_wk, L0_ffn_mha_bk, L0_ffn_mha_wv, L0_ffn_mha_bv, L0_ffn_mha_wo, L0_ffn_mha_bo, L0_ffn_mha_rw, L0_ffn_mha_rb, L0_ffn_ffn_rw, L0_ffn_ffn_rb, L0_ffn_fw1, L0_ffn_fw2)
    return x

_drawn_inputs = setup_inputs


def setup_inputs(seed=0):
    import zlib

    import numpy as np

    out = dict(_drawn_inputs(seed))
    spreads = {'L0_xattn_bq': (0.0, 0.8),
     'L0_xattn_bk': (0.0, 2.0),
     'L0_xattn_bv': (0.0, 0.8),
     'L0_xattn_bo': (0.0, 0.357),
     'L0_xattn_gamma': (1.0, 0.2),
     'L0_xattn_beta': (0.0, 0.1),
     'L0_xattn_b1': (0.0, 0.343),
     'L0_xattn_b2': (0.0, 0.1),
     'L0_ffn_ln1_g': (1.0, 0.6),
     'L0_ffn_ln1_b': (0.0, 0.753),
     'L0_ffn_ln2_g': (1.0, 0.6),
     'L0_ffn_ln2_b': (0.0, 0.8),
     'L0_ffn_mha_bq': (0.0, 0.8),
     'L0_ffn_mha_bk': (0.0, 2.0),
     'L0_ffn_mha_bv': (0.0, 0.1),
     'L0_ffn_mha_bo': (0.0, 0.1),
     'L0_ffn_mha_rb': (0.0, 0.8),
     'L0_ffn_ffn_rb': (0.0, 0.1)}
    factors = {'L0_xattn_wq': 8.0,
     'L0_xattn_wk': 8.0,
     'L0_xattn_wv': 6.136,
     'L0_xattn_wo': 5.152,
     'L0_xattn_pos_bias': 26.15,
     'L0_ffn_mha_wq': 8.0,
     'L0_ffn_mha_wk': 8.0}
    for name, (base, spread) in spreads.items():
        noise = np.random.default_rng([zlib.crc32(name.encode()), seed]).standard_normal(out[name].shape)
        drawn = base * np.exp(spread * noise) if base else spread * noise
        out[name] = jnp.asarray(drawn.astype(out[name].dtype))
    for name, factor in factors.items():
        out[name] = (out[name] * factor).astype(out[name].dtype)
    return out
```

```python
from contextlib import ExitStack

import concourse.bass as bass
from concourse import mybir

ALU = mybir.AluOpType
ACT = mybir.ActivationFunctionType
AX = mybir.AxisListType
F32 = mybir.dt.float32
F32R = mybir.dt.float32r
U32 = mybir.dt.uint32

P = 128
B, T, D, H = 4, 512, 256, 1024
BAND = 64
NT = T // P
ND = D // P
NH = H // P
M, HEADS, KD = 2, 16, 16
NJ = M * D // P
HT = P // KD
E, TOP, F = 8, 2, 512
NF = F // P
EPS_XATTN, EPS_FFN = 1e-5, 1e-6
QUAD = 32

ROW_PARTS = 32
ROW_MAX = ROW_PARTS + 4 * KD
ROWS = ROW_MAX + 2
RING = 3

STEPS = HT * NJ * 2
PER_ROUND = NJ * 2
LEAD = PER_ROUND + 3
LAST_STEP = STEPS + PER_ROUND

VECTORS = [("bq", ND), ("bk", ND), ("bv", ND), ("gamma", ND), ("beta", ND), ("b1", NH),
           ("ln1_g", ND), ("ln1_b", ND), ("ln2_g", ND), ("ln2_b", ND),
           ("mbq", NJ), ("mbk", NJ), ("mbv", NJ)]
COL = {}
for _name, _n in VECTORS:
    COL[_name] = sum(n for _, n in VECTORS[:len(COL)])
NCOLS = sum(n for _, n in VECTORS)

DVE_LINKS = 52
POOL_LINKS = 1


class Count:

    def __init__(self, sem, per):
        self.sem, self.per = sem, per

    def at(self, b, n):
        return b * self.per + n


def build(nc, x, ctx_in, g_xattn, g_ffn, wq, bq, wk, bk, wv, bv, wo, bo, pos_bias, gamma, beta, w1, b1,
          w2, b2, ln1_g, ln1_b, ln2_g, ln2_b, mha_wq, mha_bq, mha_wk, mha_bk, mha_wv, mha_bv, mha_wo,
          mha_bo, mha_rw, mha_rb, ffn_rw, ffn_rb, fw1, fw2, out):
    stack = ExitStack()
    with stack:
        place = [(nc.sbuf_base + 31) // 32 * 32]

        def at(name, offset, shape, dt=F32):
            return nc.alloc_sbuf_tensor_at(name, shape, dt, offset=offset)

        def sb(name, shape, dt=F32):
            size = 4
            for n in shape[1:]:
                size *= n
            offset = place[0]
            place[0] += (size + 31) // 32 * 32
            return at(name, offset, shape, dt)

        def region(size):
            offset = place[0]
            place[0] += size
            return offset

        WQ = sb("WQ", [P, ND, D])
        WK = sb("WK", [P, ND, D])
        WV = sb("WV", [P, ND, D])
        WO = sb("WO", [P, ND, D])
        W1 = sb("W1", [P, ND, H])
        W2 = sb("W2", [P, NH, D])
        MWQ = sb("MWQ", [P, M, ND, D])
        MWK = sb("MWK", [P, M, ND, D])
        MWV = sb("MWV", [P, ND, M, D])
        MWO = sb("MWO", [P, NJ, D])
        RW = sb("RW", [P, ND, M])
        RB = sb("RB", [P, M])
        FRW = sb("FRW", [P, ND, E])
        FRB = sb("FRB", [P, E])
        EWT = sb("EWT", [P, NT, T])
        bo_row = sb("bo_row", [P, D])
        gamma_row = sb("gamma_row", [P, D])
        beta_b2_row = sb("beta_b2_row", [P, D])
        gated_gamma_row = sb("gated_gamma_row", [P, D])
        gated_beta_row = sb("gated_beta_row", [P, D])
        mbo_row = sb("mbo_row", [P, M, D])
        ident = sb("ident", [P, P])
        ones = sb("ones", [P, P])
        COLS = sb("COLS", [P, NCOLS])
        neg_bq = sb("neg_bq", [P, ND])
        gates = sb("gates", [P, 2])
        minus_half = sb("minus_half", [P, NT])

        stats = sb("stats", [P, NT, 6])
        mean_var = sb("mean_var", [P, NT, 2])
        var_eps = sb("var_eps", [P, NT])
        rstd = sb("rstd", [P, NT])
        k_max = sb("k_max", [P, ND])
        k_shift = sb("k_shift", [P, ND])
        token_sum = sb("token_sum", [P, ND])
        sum_wide = sb("sum_wide", [P, ND, P])
        logits = sb("logits", [P, E])
        small = sb("small", [P, 8])
        mprob = sb("mprob", [P, M])
        mix_bo = sb("mix_bo", [P, D])
        eprob = sb("eprob", [P, E])
        top_p = sb("top_p", [P, 8])
        top_i = sb("top_i", [P, 8], U32)
        out_w = sb("out_w", [P, TOP])
        neg_max = sb("neg_max", [P, 2, NT * NJ])
        max_parts = sb("max_parts", [P, 2, 2 * NT * NJ])
        max_rows = sb("max_rows", [2 * NT * NJ, 2, P])
        denom = sb("denom", [P, NT, NJ])

        xs = sb("xs", [P, NT, D])
        emb = sb("emb", [P, NT, D])
        res = sb("res", [P, NT, D])
        rn = region(NT * NJ * P * 4)
        nat = at("nat", rn, [P, NT, D])
        OUT = at("OUT", rn + 4096, [P, NT, D])
        CN = at("CN", rn, [P, NT, NJ * P])

        ra = region(4 * NJ * T * 4)
        embT = at("embT", ra, [P, ND, T])
        q_exp = at("q_exp", ra + 4096, [P, ND, T])
        ekT = at("ekT", ra + 8192, [P, ND, T])
        EK = at("EK", ra + 12288, [P, NT, D])
        EKV = at("EKV", ra + 16384, [P, NT, D])
        den = at("den", ra + 20480, [P, ND, T])
        yT = at("yT", ra + 24576, [P, ND, T])
        y_den = at("y_den", ra + 28672, [P, ND, T])
        q_hi = at("q_hi", ra, [P, NJ, T], F32R)
        q_lo = at("q_lo", ra + 8192, [P, NJ, T], F32R)
        k_hi = at("k_hi", ra + 16384, [P, NJ, T], F32R)
        k_lo = at("k_lo", ra + 24576, [P, NJ, T], F32R)
        V = sb("V", [P, NT, NJ * HT, KD + 1])
        rb = region(2 * NJ * 2 * T * 4)
        hT = at("hT", rb, [P, NH, T])
        PROB = at("PROB", rb, [P, 2, NJ, 2, T])
        geluT = at("geluT", rb, [P, TOP, NF, T])
        actT = at("actT", rb + 4 * NH * T, [P, ND, T])
        C = sb("C", [P, 2, T])
        QS = sb("QS", [P, RING, NJ, T], F32R)
        KS = sb("KS", [P, RING, NJ, T], F32R)
        EW1 = at("EW1", ra, [P, TOP, ND, F])
        EW2 = at("EW2", ra + 8192, [P, TOP, NF, D])
        ctxT = at("ctxT", ra + 16384, [P, NJ, T])
        POS = at("POS", ra, [P, NT, T])
        EWN = at("EWN", ra + 8192, [P, NT, T])
        pos_max = sb("pos_max", [P, NT])
        vec_rows = at("vec_rows", ra + 16384, [NCOLS, P])
        beta_row = at("beta_row", ra + 20480, [P, D])
        assert place[0] <= nc.sbuf_top, (place[0], nc.sbuf_top)

        PS = stack.enter_context(nc.psum_tensor("PS", [P, 8, 512], F32))

        def sem(name):
            return stack.enter_context(nc.semaphore(name))

        def count(name, per):
            return Count(sem(name), per)

        rows_loaded = sem("rows_loaded")
        vectors_loaded = sem("vectors_loaded")
        xattn_loaded = sem("xattn_loaded")
        pos_loaded = sem("pos_loaded")
        mlp_loaded = sem("mlp_loaded")
        mha_loaded = sem("mha_loaded")
        gates_loaded = sem("gates_loaded")
        consts_made = sem("consts_made")
        ident_made = sem("ident_made")
        pos_masked = sem("pos_masked")
        pos_max_made = sem("pos_max_made")
        pos_exp_made = sem("pos_exp_made")
        pos_turned = sem("pos_turned")
        pos_copied = sem("pos_copied")
        vectors_turned = sem("vectors_turned")
        vectors_copied = sem("vectors_copied")
        gates_made = sem("gates_made")
        rows_made = sem("rows_made")
        setup_link = sem("setup_link")
        wait_carrier = sem("wait_carrier")

        x_loaded = count("x_loaded", 32)
        var_made = count("var_made", 6)
        rstd_made = count("rstd_made", 6)
        emb_made = count("emb_made", 1)
        emb_bo_made = count("emb_bo_made", 1)
        xs_beta_made = count("xs_beta_made", 1)
        z_made = count("z_made", 3)
        turned = count("turned", 4)
        actT_made = count("actT_made", 4)
        q_done = count("q_done", ND)
        k_done = count("k_done", ND)
        v_done = count("v_done", 2)
        k_max_made = count("k_max_made", ND)
        q_exp_made = count("q_exp_made", ND)
        ekT_made = count("ekT_made", ND)
        ek_turned = count("ek_turned", 2)
        ek_copied = count("ek_copied", 2)
        ekv_made = count("ekv_made", 2)
        den_done = count("den_done", ND)
        num_done = count("num_done", ND)
        den_copied = count("den_copied", ND)
        y_made = count("y_made", ND)
        attn_done = count("attn_done", 2)
        attn_added = count("attn_added", 2)
        a_res_made = count("a_res_made", 1)
        h_done = count("h_done", NH)
        h_even = count("h_even", NH // 2)
        h_odd = count("h_odd", NH // 2)
        ff_done = count("ff_done", 2)
        ff_added = count("ff_added", 2)
        x1_made = count("x1_made", 1)
        xf_made = count("xf_made", 1)
        sum_wide_made = count("sum_wide_made", 2)
        route_done = count("route_done", 2)
        logits_made = count("logits_made", 2)
        probs_exp = count("probs_exp", 2)
        mprob_made = count("mprob_made", 1)
        res2_made = count("res2_made", 1)
        mix_bo_made = count("mix_bo_made", 1)
        qk_done = count("qk_done", 2 * NJ)
        qk_hi = count("qk_hi", 2 * NJ)
        qk_lo = count("qk_lo", 2 * NJ)
        mv_done = count("mv_done", NT)
        mv_copied = count("mv_copied", NT)
        stacked = [count(f"stacked{s}", 8 * 16 * len(range(s, HT, RING))) for s in range(RING)]
        max_mm = count("max_mm", 2 * STEPS)
        max_red = count("max_red", 2 * STEPS)
        max_split = count("max_split", HT)
        max_turned = count("max_turned", HT)
        max_copied = count("max_copied", HT)
        max_stacked = [count(f"max_stacked{s}", 2 * 16 * len(range(s, HT, 2))) for s in range(2)]
        scored = count("scored", STEPS)
        exped = count("exped", STEPS)
        pv_done = count("pv_done", 2 * HT)
        c_copied = count("c_copied", HT)
        c_turned = count("c_turned", HT)
        cn_made = count("cn_made", HT)
        cn_turned = count("cn_turned", NJ)
        ctxT_made = count("ctxT_made", NJ)
        mo_done = count("mo_done", 2)
        mo_added = count("mo_added", 2)
        x12_made = count("x12_made", 1)
        chosen = count("chosen", 1)
        experts_loaded = count("experts_loaded", 4 * 16)
        eh_done = count("eh_done", TOP * NF)
        gelu_made = count("gelu_made", TOP * NF)
        eo_done = count("eo_done", 2 * TOP)
        eo_added = count("eo_added", 2 * TOP)
        stored = count("stored", 16)
        link = count("dve_link", DVE_LINKS)
        pool_link = count("pool_link", POOL_LINKS)

        x_v = x.rearrange("b (n p) d -> b p n d", p=P)
        c_v = ctx_in.rearrange("b (n p) d -> b p n d", p=P)
        o_v = out.rearrange("b (n p) d -> b p n d", p=P)
        fw1_v = fw1.rearrange("e (k p) f -> e p k f", p=P)
        fw2_v = fw2.rearrange("e (k p) d -> e p k d", p=P)

        def row(v):
            return v.rearrange("(a d) -> a d", a=1)

        block = stack.enter_context(nc.Block())

        @block.sync
        def _(sp):
            vecs = {"bq": bq, "bk": bk, "bv": bv, "gamma": gamma, "beta": beta, "b1": b1,
                    "ln1_g": ln1_g, "ln1_b": ln1_b, "ln2_g": ln2_g, "ln2_b": ln2_b}
            mvecs = {"mbq": mha_bq, "mbk": mha_bk, "mbv": mha_bv}
            for name, n in VECTORS:
                if name in vecs:
                    src = vecs[name].rearrange("(k p) -> k p", p=P)
                else:
                    src = mvecs[name].rearrange("m h k -> (m h k)").rearrange("(j p) -> j p", p=P)
                sp.dma_start(vec_rows[COL[name]:COL[name] + n, :], src).then_inc(vectors_loaded, 16)
            sp.dma_start(POS[:, :, :], pos_bias.rearrange("(n p) j -> p n j", p=P)).then_inc(pos_loaded, 16)
            for dst, src in ((WQ, wq), (WK, wk), (WV, wv), (WO, wo)):
                sp.dma_start(dst[:, :, :], src.rearrange("(k p) n -> p k n", p=P)).then_inc(xattn_loaded, 16)
            for dst, src in ((bo_row, row(bo)), (gamma_row, row(gamma)), (beta_row, row(beta)),
                             (beta_b2_row, row(b2)), (RB, row(mha_rb)), (FRB, row(ffn_rb))):
                sp.dma_start(dst[:, :], src.broadcast_to([P, src.shape[1]])).then_inc(rows_loaded, 16)
            for m in range(M):
                sp.dma_start(mbo_row[:, m, :], mha_bo[m:m + 1, :].broadcast_to([P, D])).then_inc(rows_loaded, 16)
            for n, g in enumerate((g_xattn, g_ffn)):
                sp.dma_start(gates[:, n:n + 1], row(g).broadcast_to([P, 1])).then_inc(gates_loaded, 16)
            sp.dma_start(W1[:, :, :], w1.rearrange("(k p) n -> p k n", p=P)).then_inc(mlp_loaded, 16)
            sp.dma_start(W2[:, :, :], w2.rearrange("(k p) n -> p k n", p=P)).then_inc(mlp_loaded, 16)
            for m in range(M):
                for dst, src in ((MWQ[:, m, :, :], mha_wq), (MWK[:, m, :, :], mha_wk), (MWV[:, :, m, :], mha_wv)):
                    v = src.rearrange("m (k p) h d -> m p k (h d)", p=P)
                    sp.dma_start(dst, v[m, :, :, :]).then_inc(mha_loaded, 16)
            sp.dma_start(MWO[:, :, :], mha_wo.rearrange("m h k d -> (m h k) d")
                         .rearrange("(j p) d -> p j d", p=P)).then_inc(mha_loaded, 16)
            sp.dma_start(RW[:, :, :], mha_rw.rearrange("(k p) m -> p k m", p=P)).then_inc(mha_loaded, 16)
            sp.dma_start(FRW[:, :, :], ffn_rw.rearrange("(k p) m -> p k m", p=P)).then_inc(mha_loaded, 16)
            with sp.Fori(0, B) as b:
                sp.dma_start(xs[:, :, :], x_v[b, :, :, :]).then_inc(x_loaded.sem, 16)
                sp.dma_start(emb[:, :, :], c_v[b, :, :, :]).then_inc(x_loaded.sem, 16)

                def stack_round(r):
                    s = r % RING
                    for n, (dst, src) in enumerate(((QS, q_hi), (QS, q_hi), (QS, q_lo), (QS, q_lo),
                                                    (KS, k_hi), (KS, k_lo), (KS, k_hi), (KS, k_lo))):
                        at0 = ROW_PARTS + KD * (n % 4)
                        sp.dma_start(dst[at0:at0 + KD, s, :, :].bitcast(F32),
                                     src[KD * r:KD * r + KD, :, :].bitcast(F32)).then_inc(stacked[s].sem, 16)

                def stack_max(r):
                    s = r % RING
                    sp.wait_ge(max_copied.sem, max_copied.at(b, r + 1))
                    for part in range(2):
                        n = NT * NJ
                        dst = QS[ROW_MAX + part:ROW_MAX + part + 1, s, :, :].bitcast(F32)
                        sp.dma_start(dst.rearrange("a j (n c) -> a (j n) c", c=P),
                                     max_rows[part * n:part * n + n, r % 2, :]).then_inc(max_stacked[r % 2].sem, 16)

                sp.wait_ge(qk_lo.sem, qk_lo.at(b, 2 * NJ))
                sp.wait_ge(qk_hi.sem, qk_hi.at(b, 2 * NJ))
                for r in range(RING):
                    stack_round(r)
                for r in range(HT):
                    stack_max(r)
                    if r + 2 >= RING and r + 2 < HT:
                        sp.wait_ge(scored.sem, scored.at(b, PER_ROUND * (r + 3 - RING)))
                        stack_round(r + 2)
                sp.wait_ge(chosen.sem, chosen.at(b, 1))
                sp.sem_inc(wait_carrier, 1)
                for e in range(TOP):
                    i = sp.value_load(top_i[0:1, e:e + 1], min_val=0, max_val=E - 1)
                    sp.dma_start(EW1[:, e, :, :], fw1_v[i, :, :, :]).then_inc(experts_loaded.sem, 16)
                    sp.dma_start(EW2[:, e, :, :], fw2_v[i, :, :, :]).then_inc(experts_loaded.sem, 16)
                sp.wait_ge(eo_added.sem, eo_added.at(b, 2 * TOP))
                sp.dma_start(o_v[b, :, :, :], OUT[:, :, :]).then_inc(stored.sem, 16)
                sp.wait_ge(stored.sem, stored.at(b, 16))
                sp.sem_inc(wait_carrier, 1)

        @block.gpsimd
        def _(pool):
            nc.gpsimd.memset(ident[:, :], 0.0).then_inc(ident_made, 1)
            pool.wait_ge(ident_made, 1)
            nc.gpsimd.affine_select(out=ident[:, :], in_=ident[:, :], compare_op=ALU.not_equal, fill=1.0,
                                    base=0, pattern=[[-1, P]], channel_multiplier=1).then_inc(ident_made, 1)
            nc.gpsimd.memset(minus_half[:, :], -0.5).then_inc(consts_made, 1)
            pool.wait_ge(pos_loaded, 16)
            for n in range(NT):
                nc.gpsimd.affine_select(out=POS[:, n, :], in_=POS[:, n, :], compare_op=ALU.is_ge, fill=0.0,
                                        base=BAND - 1 - n * P, pattern=[[1, T]],
                                        channel_multiplier=-1).then_inc(pos_masked, 1)
            pool.wait_ge(pos_masked, NT)
            for n in range(NT):
                nc.gpsimd.affine_select(out=POS[:, n, :], in_=POS[:, n, :], compare_op=ALU.is_ge, fill=0.0,
                                        base=BAND - 1 + n * P, pattern=[[-1, T]],
                                        channel_multiplier=1).then_inc(pos_masked, 1)
            pool.wait_ge(rows_loaded, 16 * 8)
            nc.gpsimd.tensor_tensor(beta_b2_row[:, :], beta_b2_row[:, :], beta_row[:, :], ALU.add).then_inc(rows_made, 1)
            pool.wait_ge(gates_made, 1)
            nc.gpsimd.tensor_scalar(gated_gamma_row[:, :], gamma_row[:, :], gates[:, 0:1], None, ALU.mult).then_inc(rows_made, 1)
            nc.gpsimd.tensor_scalar(gated_beta_row[:, :], beta_row[:, :], gates[:, 0:1], None, ALU.mult).then_inc(rows_made, 1)
            pool.wait_ge(rows_made, 3)
            pool.wait_ge(consts_made, 1)

            with pool.Fori(0, B) as b:
                def root(n):
                    pool.wait_ge(var_made.sem, var_made.at(b, n + 1))
                    nc.gpsimd.tensor_tensor(rstd[:, :], var_eps[:, :], minus_half[:, :], ALU.pow).then_inc(rstd_made.sem, 1)

                def wide(v):
                    return v[:, :].rearrange("p (a d) -> p a d", a=1).broadcast_to([P, NT, D])

                root(0)
                pool.wait_ge(x_loaded.sem, x_loaded.at(b, 32))
                pool.wait_ge(emb_made.sem, emb_made.at(b, 1))
                nc.gpsimd.tensor_tensor(res[:, :, :], emb[:, :, :], wide(bo_row), ALU.add).then_inc(emb_bo_made.sem, 1)
                nc.gpsimd.tensor_tensor(xs[:, :, :], xs[:, :, :], wide(gated_beta_row), ALU.add).then_inc(xs_beta_made.sem, 1)
                root(1)
                pool.wait_ge(z_made.sem, z_made.at(b, 1))
                pool.wait_ge(attn_added.sem, attn_added.at(b, 2))
                nc.gpsimd.tensor_tensor(res[:, :, :], nat[:, :, :], wide(gamma_row), ALU.mult).then_inc(pool_link.sem, 1)
                pool.wait_ge(pool_link.sem, pool_link.at(b, 1))
                nc.gpsimd.tensor_tensor(res[:, :, :], res[:, :, :], wide(beta_b2_row), ALU.add).then_inc(a_res_made.sem, 1)
                root(2)
                root(3)
                root(4)
                pool.wait_ge(mix_bo_made.sem, mix_bo_made.at(b, 1))
                nc.gpsimd.tensor_tensor(res[:, :, :], emb[:, :, :], wide(mix_bo), ALU.add).then_inc(res2_made.sem, 1)
                root(5)
                pool.wait_ge(eo_added.sem, eo_added.at(b, 2 * TOP))

        @block.scalar
        def _(act):
            act.wait_ge(gates_loaded, 32)
            nc.scalar.activation(gates[:, :], gates[:, :], ACT.Tanh).then_inc(gates_made, 1)
            act.wait_ge(pos_max_made, 1)
            for n in range(NT):
                nc.scalar.activation(EWN[:, n, :], POS[:, n, :], ACT.Exp, bias=pos_max[:, n:n + 1]).then_inc(pos_exp_made, 1)
            act.wait_ge(vectors_copied, 2)

            with act.Fori(0, B) as b:
                act.wait_ge(turned.sem, turned.at(b, 1))
                act.activation(embT[:, :, :], PS[:, 0:2, :], ACT.Copy).then_inc(actT_made.sem, 1)
                for i in range(ND):
                    act.wait_ge(q_done.sem, q_done.at(b, i + 1))
                    act.activation(q_exp[:, i, :], PS[:, 2 + i, :], ACT.Exp, bias=neg_bq[:, i:i + 1],
                                   scale=-1.0).then_inc(q_exp_made.sem, 1)
                for i in range(ND):
                    act.wait_ge(k_max_made.sem, k_max_made.at(b, i + 1))
                    act.activation(ekT[:, i, :], PS[:, 4 + i, :], ACT.Exp, bias=k_shift[:, i:i + 1]).then_inc(ekT_made.sem, 1)
                for i in range(2):
                    act.wait_ge(ek_turned.sem, ek_turned.at(b, i + 1))
                    act.activation(EK[:, 2 * i:2 * i + 2, :].rearrange("p a d -> p (a d)"), PS[:, i, :],
                                   ACT.Copy).then_inc(ek_copied.sem, 1)
                for i in range(ND):
                    act.wait_ge(den_done.sem, den_done.at(b, i + 1))
                    act.activation(den[:, i, :], PS[:, 2 + i, :], ACT.Copy).then_inc(den_copied.sem, 1)
                act.wait_ge(turned.sem, turned.at(b, 2))
                for i in range(ND):
                    a = act.activation(actT[:, i, :], PS[:, 2 + i, :], ACT.Identity,
                                       scale=COLS[:, COL["gamma"] + i:COL["gamma"] + i + 1],
                                       bias=COLS[:, COL["beta"] + i:COL["beta"] + i + 1])
                a.then_inc(actT_made.sem, 1)
                for i in range(0, NH, 2):
                    act.wait_ge(h_done.sem, h_done.at(b, i + 1))
                    act.activation(hT[:, i, :], PS[:, (4 + i) % 8, :], ACT.Relu,
                                   bias=COLS[:, COL["b1"] + i:COL["b1"] + i + 1]).then_inc(h_even.sem, 1)
                act.wait_ge(turned.sem, turned.at(b, 3))
                for i in range(ND):
                    a = act.activation(actT[:, i, :], PS[:, i, :], ACT.Identity,
                                       scale=COLS[:, COL["ln1_g"] + i:COL["ln1_g"] + i + 1],
                                       bias=COLS[:, COL["ln1_b"] + i:COL["ln1_b"] + i + 1],
                                       accum_out=token_sum[:, i:i + 1])
                a.then_inc(actT_made.sem, 1)
                for n in range(2 * NJ):
                    j, bias, dst = n // 2, ("mbq", "mbk")[n % 2], (q_hi, k_hi)[n % 2]
                    act.wait_ge(qk_done.sem, qk_done.at(b, n + 1))
                    act.activation(dst[:, j, :], PS[:, 2 + n % 4, :], ACT.Identity,
                                   bias=COLS[:, COL[bias] + j:COL[bias] + j + 1]).then_inc(qk_hi.sem, 1)
                act.wait_ge(logits_made.sem, logits_made.at(b, 1))
                act.activation(mprob[:, :], logits[:, 0:M], ACT.Exp, bias=small[:, 0:1],
                               accum_out=small[:, 1:2]).then_inc(probs_exp.sem, 1)

                for s in range(STEPS + PER_ROUND):
                    r, i = s // PER_ROUND, s % PER_ROUND
                    if s < STEPS:
                        act.wait_ge(scored.sem, scored.at(b, s + 1))
                        blk = s // NJ
                        if blk >= 2:
                            act.wait_ge(pv_done.sem, pv_done.at(b, blk - 1))
                        act.activation(PROB[:, blk % 2, s % NJ, :, :], PS[:, 2 + 2 * (s % 2):4 + 2 * (s % 2), :],
                                       ACT.Exp, scale=KD ** -0.5).then_inc(exped.sem, 1)
                    if i == 4 and r >= 1:
                        act.wait_ge(pv_done.sem, pv_done.at(b, 2 * r))
                        if r >= 3:
                            act.wait_ge(c_turned.sem, c_turned.at(b, r - 2))
                        act.activation(C[:, (r - 1) % 2, :], PS[:, 6, :], ACT.Copy).then_inc(c_copied.sem, 1)

                act.wait_ge(turned.sem, turned.at(b, 4))
                for i in range(ND):
                    a = act.activation(actT[:, i, :], PS[:, 6 + i, :], ACT.Identity,
                                       scale=COLS[:, COL["ln2_g"] + i:COL["ln2_g"] + i + 1],
                                       bias=COLS[:, COL["ln2_b"] + i:COL["ln2_b"] + i + 1],
                                       accum_out=token_sum[:, i:i + 1])
                a.then_inc(actT_made.sem, 1)
                act.wait_ge(logits_made.sem, logits_made.at(b, 2))
                act.activation(eprob[:, :], logits[:, :], ACT.Exp, bias=small[:, 0:1],
                               accum_out=small[:, 1:2]).then_inc(probs_exp.sem, 1)
                for n in range(TOP * NF):
                    act.wait_ge(eh_done.sem, eh_done.at(b, n + 1))
                    act.activation(geluT[:, n // NF, n % NF, :], PS[:, n % 4, :], ACT.Gelu).then_inc(gelu_made.sem, 1)
                act.wait_ge(eo_added.sem, eo_added.at(b, 2 * TOP))

        @block.vector
        def _(dve):
            nc.vector.memset(ones[:, :], 1.0).then_inc(consts_made, 1)
            nc.vector.memset(QS[:, :, :, :].bitcast(F32), 0.0).then_inc(setup_link, 1)
            nc.vector.memset(KS[:, :, :, :].bitcast(F32), 0.0).then_inc(setup_link, 1)
            dve.wait_ge(setup_link, 2)
            nc.vector.memset(V[:, :, :, KD:KD + 1], 1.0).then_inc(consts_made, 1)
            for s in range(RING):
                nc.vector.memset(KS[ROW_MAX:ROWS, s, :, :].bitcast(F32), 1.0).then_inc(consts_made, 1)
            dve.wait_ge(vectors_turned, 1)
            nc.vector.tensor_copy(COLS[:, :], PS[:, 7, 0:NCOLS]).then_inc(vectors_copied, 1)
            dve.wait_ge(vectors_copied, 1)
            nc.vector.tensor_scalar(neg_bq[:, :], COLS[:, COL["bq"]:COL["bq"] + ND], -1.0, None,
                                    ALU.mult).then_inc(vectors_copied, 1)
            dve.wait_ge(pos_masked, 2 * NT)
            nc.vector.tensor_reduce(pos_max[:, :], POS[:, :, :], AX.X, ALU.max, negate=True).then_inc(pos_max_made, 1)
            for n in range(NT):
                dve.wait_ge(pos_turned, n + 1)
                nc.vector.tensor_copy(EWT[:, n, :], PS[:, n, :]).then_inc(pos_copied, 1)
            dve.wait_ge(rows_made, 3)
            dve.wait_ge(pos_copied, NT)
            dve.wait_ge(vectors_copied, 2)

            with dve.Fori(0, B) as b:
                links = [0]

                def linked(ins, alone=False):
                    links[0] += 1
                    ins.then_inc(link.sem, 1)
                    dve.wait_ge(link.sem, link.at(b, links[0]))
                    if alone:
                        dve.sem_inc(wait_carrier, 1)

                def layer_norm(n, src, dst, eps):
                    for t in range(NT):
                        a = nc.vector.bn_stats(stats[:, t, :], src[:, t, :])
                    linked(a, alone=True)
                    for t in range(NT):
                        a = nc.vector.bn_aggr(mean_var[:, t, :], stats[:, t, :])
                    linked(a)
                    nc.vector.tensor_scalar(var_eps[:, :], mean_var[:, :, 1], eps, None, ALU.add).then_inc(var_made.sem, 1)
                    dve.wait_ge(rstd_made.sem, rstd_made.at(b, n + 1))
                    for t in range(NT):
                        a = nc.vector.tensor_scalar(dst[:, t, :], src[:, t, :], mean_var[:, t, 0:1], rstd[:, t:t + 1],
                                                    ALU.subtract, ALU.mult)
                    return a

                def wide(v):
                    return v[:, :].rearrange("p (a d) -> p a d", a=1).broadcast_to([P, NT, D])

                def spread_sum():
                    for i in range(ND):
                        a = nc.vector.tensor_scalar(sum_wide[:, i, :], ones[:, :], token_sum[:, i:i + 1], None, ALU.mult)
                    a.then_inc(sum_wide_made.sem, 1)

                dve.wait_ge(x_loaded.sem, x_loaded.at(b, 32))
                linked(layer_norm(0, xs, nat, EPS_XATTN))
                nc.vector.tensor_tensor(emb[:, :, :], emb[:, :, :], nat[:, :, :], ALU.add).then_inc(emb_made.sem, 1)
                for i in range(ND):
                    bk_i = COLS[:, COL["bk"] + i:COL["bk"] + i + 1]
                    dve.wait_ge(k_done.sem, k_done.at(b, i + 1))
                    linked(nc.vector.tensor_reduce(k_max[:, i:i + 1], PS[:, 4 + i, :], AX.X, ALU.max))
                    linked(nc.vector.tensor_scalar(k_max[:, i:i + 1], k_max[:, i:i + 1], bk_i, None, ALU.add))
                    nc.vector.tensor_tensor(k_shift[:, i:i + 1], bk_i, k_max[:, i:i + 1], ALU.subtract).then_inc(k_max_made.sem, 1)
                for i in range(2):
                    dve.wait_ge(v_done.sem, v_done.at(b, i + 1))
                    dve.wait_ge(ek_copied.sem, ek_copied.at(b, i + 1))
                    nc.vector.tensor_tensor(EKV[:, 2 * i:2 * i + 2, :], PS[:, 6 + i, :].rearrange("p (a d) -> p a d", a=2),
                                            EK[:, 2 * i:2 * i + 2, :], ALU.mult).then_inc(ekv_made.sem, 1)
                for i in range(ND):
                    dve.wait_ge(den_copied.sem, den_copied.at(b, i + 1))
                    dve.wait_ge(q_exp_made.sem, q_exp_made.at(b, i + 1))
                    linked(nc.vector.scalar_tensor_tensor(y_den[:, i, :], q_exp[:, i, :], 1.0, den[:, i, :], ALU.add, ALU.mult))
                    nc.vector.reciprocal(y_den[:, i, :], y_den[:, i, :])
                    dve.wait_ge(num_done.sem, num_done.at(b, i + 1))
                    linked(nc.vector.scalar_tensor_tensor(yT[:, i, :], den[:, i, :], COLS[:, COL["bv"] + i:COL["bv"] + i + 1],
                                                          PS[:, 4 + i, :], ALU.mult, ALU.add))
                    nc.vector.tensor_tensor(yT[:, i, :], yT[:, i, :], y_den[:, i, :], ALU.mult).then_inc(y_made.sem, 1)
                dve.wait_ge(emb_bo_made.sem, emb_bo_made.at(b, 1))
                for i in range(2):
                    dve.wait_ge(attn_done.sem, attn_done.at(b, i + 1))
                    nc.vector.tensor_tensor(nat[:, 2 * i:2 * i + 2, :], PS[:, i, :].rearrange("p (a d) -> p a d", a=2),
                                            res[:, 2 * i:2 * i + 2, :], ALU.add).then_inc(attn_added.sem, 1)
                dve.wait_ge(attn_added.sem, attn_added.at(b, 2))
                layer_norm(1, nat, nat, EPS_XATTN).then_inc(z_made.sem, 1)
                for i in range(1, NH, 2):
                    dve.wait_ge(h_done.sem, h_done.at(b, i + 1))
                    nc.vector.tensor_scalar(hT[:, i, :], PS[:, (4 + i) % 8, :], COLS[:, COL["b1"] + i:COL["b1"] + i + 1],
                                            0.0, ALU.add, ALU.max).then_inc(h_odd.sem, 1)
                dve.wait_ge(a_res_made.sem, a_res_made.at(b, 1))
                for i in range(2):
                    dve.wait_ge(ff_done.sem, ff_done.at(b, i + 1))
                    nc.vector.tensor_tensor(nat[:, 2 * i:2 * i + 2, :], PS[:, 4 + i, :].rearrange("p (a d) -> p a d", a=2),
                                            res[:, 2 * i:2 * i + 2, :], ALU.add).then_inc(ff_added.sem, 1)
                dve.wait_ge(ff_added.sem, ff_added.at(b, 2))
                linked(layer_norm(2, nat, nat, EPS_XATTN))
                linked(nc.vector.tensor_tensor(nat[:, :, :], nat[:, :, :], wide(gated_gamma_row), ALU.mult))
                dve.wait_ge(xs_beta_made.sem, xs_beta_made.at(b, 1))
                linked(nc.vector.tensor_tensor(xs[:, :, :], xs[:, :, :], nat[:, :, :], ALU.add))
                linked(layer_norm(3, xs, emb, EPS_XATTN))
                layer_norm(4, emb, nat, EPS_FFN).then_inc(z_made.sem, 1)
                dve.wait_ge(actT_made.sem, actT_made.at(b, 3))
                spread_sum()

                def softmax_shift(n, width, bias):
                    dve.wait_ge(route_done.sem, route_done.at(b, n + 1))
                    linked(nc.vector.scalar_tensor_tensor(logits[:, 0:width], PS[:, (7, 5)[n], 0:width], 1.0 / T, bias[:, :],
                                                          ALU.mult, ALU.add))
                    nc.vector.tensor_reduce(small[:, 0:1], logits[:, 0:width], AX.X, ALU.max,
                                            negate=True).then_inc(logits_made.sem, 1)

                def low_part(n):
                    j, bias, hi, dst = n // 2, ("mbq", "mbk")[n % 2], (q_hi, k_hi)[n % 2], (q_lo, k_lo)[n % 2]
                    dve.wait_ge(qk_hi.sem, qk_hi.at(b, n + 1))
                    nc.vector.scalar_tensor_tensor(dst[:, j, :], PS[:, 2 + n % 4, :], COLS[:, COL[bias] + j:COL[bias] + j + 1],
                                                   hi[:, j, :].bitcast(F32), ALU.add, ALU.subtract).then_inc(qk_lo.sem, 1)

                for n in range(2 * NJ):
                    low_part(n)
                for t in range(NT):
                    dve.wait_ge(mv_done.sem, mv_done.at(b, t + 1))
                    nc.vector.tensor_copy(V[:, t, :, 0:KD],
                                          PS[:, 6 + t % 2, :].rearrange("p (h k) -> p h k", k=KD)).then_inc(mv_copied.sem, 1)
                softmax_shift(0, M, RB)
                dve.wait_ge(probs_exp.sem, probs_exp.at(b, 1))
                linked(nc.vector.reciprocal(small[:, 2:3], small[:, 1:2]))
                linked(nc.vector.tensor_scalar(mprob[:, :], mprob[:, :], small[:, 2:3], None, ALU.mult))
                linked(nc.vector.tensor_scalar(mix_bo[:, :], mbo_row[:, 0, :], mprob[:, 0:1], None, ALU.mult))
                nc.vector.scalar_tensor_tensor(mix_bo[:, :], mbo_row[:, 1, :], mprob[:, 1:2], mix_bo[:, :],
                                               ALU.mult, ALU.add).then_inc(mix_bo_made.sem, 1)

                for s in range(-LEAD, LAST_STEP + 1):
                    m = s + LEAD
                    g, i = m // PER_ROUND, m % PER_ROUND
                    if m < STEPS:
                        for half in range(2):
                            n = 2 * m + half
                            col = (i // 2) * NT + 2 * (i % 2) + half
                            dve.wait_ge(max_mm.sem, max_mm.at(b, n + 1))
                            a = nc.vector.tensor_reduce(neg_max[:, g % 2, col:col + 1], PS[:, n % 2, :], AX.X, ALU.max,
                                                        negate=True)
                            a.then_inc(max_red.sem, 1)
                        if i == PER_ROUND - 1:
                            w = NT * NJ
                            dve.wait_ge(max_red.sem, max_red.at(b, 2 * m + 2))
                            if g >= 2:
                                dve.wait_ge(max_turned.sem, max_turned.at(b, g - 1))
                            linked(nc.vector.tensor_copy(max_parts[:, g % 2, 0:w].bitcast(F32R), neg_max[:, g % 2, :]))
                            nc.vector.tensor_tensor(max_parts[:, g % 2, w:2 * w].bitcast(F32R), neg_max[:, g % 2, :],
                                                    max_parts[:, g % 2, 0:w], ALU.subtract).then_inc(max_split.sem, 1)
                    if i == 1 and 1 <= g <= HT:
                        dve.wait_ge(max_turned.sem, max_turned.at(b, g))
                        if g >= 3:
                            dve.wait_ge(max_stacked[(g - 3) % 2].sem, max_stacked[(g - 3) % 2].at(b, 32 * ((g - 3) // 2 + 1)))
                        nc.vector.tensor_copy(max_rows[:, (g - 1) % 2, :], PS[0:2 * NT * NJ, 7, 0:P]).then_inc(max_copied.sem, 1)
                    r = s // PER_ROUND - 2
                    if s % PER_ROUND == 0 and 0 <= r < HT:
                        ct = PS[:, 7, :].rearrange("p (t j c) -> p t j c", t=NT, c=QUAD)
                        dve.wait_ge(c_turned.sem, c_turned.at(b, r + 1))
                        linked(nc.vector.reciprocal(denom[:, :, :], ct[:, :, :, KD]))
                        cn = CN[:, :, :].rearrange("p t (j c) -> p t j c", c=P)[:, :, :, KD * r:KD * r + KD]
                        dn = denom[:, :, :].rearrange("p t (j a) -> p t j a", a=1).broadcast_to([P, NT, NJ, KD])
                        nc.vector.tensor_tensor(cn, ct[:, :, :, 0:KD], dn, ALU.mult).then_inc(cn_made.sem, 1)

                for j in range(NJ):
                    dve.wait_ge(cn_turned.sem, cn_turned.at(b, j + 1))
                    g = j // (NJ // M)
                    nc.vector.tensor_scalar(ctxT[:, j, :], PS[:, j, :], COLS[:, COL["mbv"] + j:COL["mbv"] + j + 1],
                                            mprob[:, g:g + 1], ALU.add, ALU.mult).then_inc(ctxT_made.sem, 1)
                dve.wait_ge(res2_made.sem, res2_made.at(b, 1))
                for i in range(2):
                    dve.wait_ge(mo_done.sem, mo_done.at(b, i + 1))
                    nc.vector.tensor_tensor(res[:, 2 * i:2 * i + 2, :], PS[:, 4 + i, :].rearrange("p (a d) -> p a d", a=2),
                                            res[:, 2 * i:2 * i + 2, :], ALU.add).then_inc(mo_added.sem, 1)
                dve.wait_ge(mo_added.sem, mo_added.at(b, 2))
                layer_norm(5, res, nat, EPS_FFN).then_inc(z_made.sem, 1)
                nc.vector.scalar_tensor_tensor(xs[:, :, :], res[:, :, :], gates[:, 1:2], xs[:, :, :], ALU.mult,
                                               ALU.add).then_inc(x12_made.sem, 1)
                dve.wait_ge(actT_made.sem, actT_made.at(b, 4))
                spread_sum()
                softmax_shift(1, E, FRB)
                dve.wait_ge(probs_exp.sem, probs_exp.at(b, 2))
                linked(nc.vector.reciprocal(small[:, 2:3], small[:, 1:2]))
                linked(nc.vector.tensor_scalar(eprob[:, :], eprob[:, :], small[:, 2:3], None, ALU.mult), alone=True)
                linked(nc.vector.max(top_p[:, :], eprob[:, :]), alone=True)
                nc.vector.max_index(top_i[:, :], top_p[:, :], eprob[:, :]).then_inc(chosen.sem, 1)
                linked(nc.vector.tensor_tensor(small[:, 3:4], top_p[:, 0:1], top_p[:, 1:2], ALU.add))
                linked(nc.vector.reciprocal(small[:, 4:5], small[:, 3:4]))
                linked(nc.vector.tensor_scalar(out_w[:, :], top_p[:, 0:TOP], small[:, 4:5], gates[:, 1:2], ALU.mult, ALU.mult))
                dve.wait_ge(x12_made.sem, x12_made.at(b, 1))
                for e in range(TOP):
                    for i in range(2):
                        dve.wait_ge(eo_done.sem, eo_done.at(b, 2 * e + i + 1))
                        if e == 1:
                            dve.wait_ge(eo_added.sem, eo_added.at(b, i + 1))
                        rows = slice(2 * i, 2 * i + 2)
                        nc.vector.scalar_tensor_tensor(OUT[:, rows, :],
                                                       PS[:, 4 + 2 * e + i, :].rearrange("p (a d) -> p a d", a=2),
                                                       out_w[:, e:e + 1], (xs if e == 0 else OUT)[:, rows, :],
                                                       ALU.mult, ALU.add).then_inc(eo_added.sem, 1)
                dve.wait_ge(eo_added.sem, eo_added.at(b, 2 * TOP))
                dve.wait_ge(stored.sem, stored.at(b, 16))
                assert links[0] == DVE_LINKS, links[0]

        @block.tensor
        def _(pe):
            pe.wait_ge(ident_made, 2)
            pe.wait_ge(vectors_loaded, 16 * len(VECTORS))
            pe.transpose(PS[:, 7, 0:NCOLS], vec_rows[:, :], ident[0:NCOLS, 0:NCOLS]).then_inc(vectors_turned, 1)
            pe.wait_ge(pos_exp_made, NT)
            for j in range(NT):
                for n in range(NT):
                    a = pe.transpose(PS[:, j, n * P:(n + 1) * P], EWN[:, n, j * P:(j + 1) * P], ident[:, :])
                a.then_inc(pos_turned, 1)
            pe.wait_ge(pos_copied, NT)
            pe.wait_ge(vectors_copied, 1)
            pe.wait_ge(xattn_loaded, 4 * 16)
            pe.wait_ge(mlp_loaded, 2 * 16)
            pe.wait_ge(mha_loaded, 9 * 16)
            pe.wait_ge(consts_made, 3 + RING)

            with pe.Fori(0, B) as b:
                def turn(bank, src):
                    for k in range(ND):
                        for t in range(NT):
                            a = pe.transpose(PS[:, bank + k, t * P:(t + 1) * P], src[:, t, k * P:(k + 1) * P], ident[:, :])
                    a.then_inc(turned.sem, 1)

                def product(dst, lhs, rhs, n):
                    for k in range(n):
                        a = pe.matmul(dst, lhs(k), rhs(k), start=(k == 0), stop=(k == n - 1))
                    return a

                pe.wait_ge(emb_made.sem, emb_made.at(b, 1))
                turn(0, emb)
                pe.wait_ge(actT_made.sem, actT_made.at(b, 1))
                for i in range(ND):
                    product(PS[:, 4 + i, :], lambda k: WK[:, k, i * P:(i + 1) * P], lambda k: embT[:, k, :],
                            ND).then_inc(k_done.sem, 1)
                for i in range(ND):
                    product(PS[:, 2 + i, :], lambda k: WQ[:, k, i * P:(i + 1) * P], lambda k: embT[:, k, :],
                            ND).then_inc(q_done.sem, 1)
                for t in range(NT):
                    a = product(PS[:, 6 + t // 2, (t % 2) * D:(t % 2) * D + D],
                                lambda k: embT[:, k, t * P:(t + 1) * P], lambda k: WV[:, k, :], ND)
                    if t % 2:
                        a.then_inc(v_done.sem, 1)
                pe.wait_ge(ekT_made.sem, ekT_made.at(b, ND))
                for t in range(NT):
                    for k in range(ND):
                        at0 = (t % 2) * D + k * P
                        a = pe.transpose(PS[:, t // 2, at0:at0 + P], ekT[:, k, t * P:(t + 1) * P], ident[:, :])
                    if t % 2:
                        a.then_inc(ek_turned.sem, 1)
                pe.wait_ge(ek_copied.sem, ek_copied.at(b, 2))
                pe.wait_ge(q_exp_made.sem, q_exp_made.at(b, ND))
                for i in range(ND):
                    product(PS[:, 2 + i, :], lambda k: EK[:, k, i * P:(i + 1) * P], lambda k: EWT[:, k, :],
                            NT).then_inc(den_done.sem, 1)
                pe.wait_ge(ekv_made.sem, ekv_made.at(b, 2))
                for i in range(ND):
                    product(PS[:, 4 + i, :], lambda k: EKV[:, k, i * P:(i + 1) * P], lambda k: EWT[:, k, :],
                            NT).then_inc(num_done.sem, 1)
                pe.wait_ge(y_made.sem, y_made.at(b, ND))
                for t in range(NT):
                    a = product(PS[:, t // 2, (t % 2) * D:(t % 2) * D + D],
                                lambda k: yT[:, k, t * P:(t + 1) * P], lambda k: WO[:, k, :], ND)
                    if t % 2:
                        a.then_inc(attn_done.sem, 1)
                pe.wait_ge(z_made.sem, z_made.at(b, 1))
                turn(2, nat)
                pe.wait_ge(actT_made.sem, actT_made.at(b, 2))
                for i in range(NH):
                    product(PS[:, (4 + i) % 8, :], lambda k: W1[:, k, i * P:(i + 1) * P], lambda k: actT[:, k, :],
                            ND).then_inc(h_done.sem, 1)
                pe.wait_ge(h_even.sem, h_even.at(b, NH // 2))
                pe.wait_ge(h_odd.sem, h_odd.at(b, NH // 2))
                for t in range(NT):
                    a = product(PS[:, 4 + t // 2, (t % 2) * D:(t % 2) * D + D],
                                lambda k: hT[:, k, t * P:(t + 1) * P], lambda k: W2[:, k, :], NH)
                    if t % 2:
                        a.then_inc(ff_done.sem, 1)
                pe.wait_ge(z_made.sem, z_made.at(b, 2))
                turn(0, nat)
                pe.wait_ge(actT_made.sem, actT_made.at(b, 3))
                for n in range(2 * NJ):
                    j, w = n // 2, (MWQ, MWK)[n % 2]
                    m, half = j // (NJ // M), j % (NJ // M)
                    if n >= 4:
                        pe.wait_ge(qk_lo.sem, qk_lo.at(b, n - 3))
                    product(PS[:, 2 + n % 4, :], lambda k: w[:, m, k, half * P:(half + 1) * P], lambda k: actT[:, k, :],
                            ND).then_inc(qk_done.sem, 1)
                for t in range(NT):
                    if t >= 2:
                        pe.wait_ge(mv_copied.sem, mv_copied.at(b, t - 1))
                    product(PS[:, 6 + t % 2, :], lambda k: actT[:, k, t * P:(t + 1) * P],
                            lambda k: MWV[:, k, :, :].rearrange("p m d -> p (m d)"), ND).then_inc(mv_done.sem, 1)
                pe.wait_ge(mv_copied.sem, mv_copied.at(b, NT))
                pe.wait_ge(sum_wide_made.sem, sum_wide_made.at(b, 1))
                product(PS[:, 7, 0:M], lambda k: sum_wide[:, k, :], lambda k: RW[:, k, :], ND).then_inc(route_done.sem, 1)
                pe.wait_ge(logits_made.sem, logits_made.at(b, 1))
                pe.wait_ge(qk_lo.sem, qk_lo.at(b, 2 * NJ))

                for s in range(-LEAD, LAST_STEP):
                    m = s + LEAD
                    g, i = m // PER_ROUND, m % PER_ROUND
                    if m < STEPS:
                        if i == 0:
                            pe.wait_ge(stacked[g % RING].sem, stacked[g % RING].at(b, 8 * 16 * (g // RING + 1)))
                        j, slot = i // 2, g % RING
                        for half in range(2):
                            n, t = 2 * m + half, 2 * (i % 2) + half
                            if n >= 2:
                                pe.wait_ge(max_red.sem, max_red.at(b, n - 1))
                            pe.matmul(PS[:, n % 2, :], QS[0:ROW_MAX, slot, j, t * P:(t + 1) * P], KS[0:ROW_MAX, slot, j, :],
                                      start=True, stop=True).then_inc(max_mm.sem, 1)
                    r = s // PER_ROUND
                    if 0 <= s < STEPS:
                        step = s % PER_ROUND
                        j, slot = step % NJ, r % RING
                        if step == 0:
                            pe.wait_ge(max_stacked[r % 2].sem, max_stacked[r % 2].at(b, 32 * (r // 2 + 1)))
                        if s >= 2:
                            pe.wait_ge(exped.sem, exped.at(b, s - 1))
                        for half in range(2):
                            st = 2 * (step // NJ) + half
                            a = pe.matmul(PS[:, 2 + 2 * (s % 2) + half, :], KS[0:ROWS, slot, j, st * P:(st + 1) * P],
                                          QS[0:ROWS, slot, j, :], start=True, stop=True)
                        a.then_inc(scored.sem, 1)
                    blk = s // NJ - 1
                    if s % 2 == 1 and 0 <= blk < 2 * HT:
                        half, st = (s % NJ) // 2, 2 * (blk % 2) + (s % NJ) // 2
                        if half == 0:
                            pe.wait_ge(exped.sem, exped.at(b, NJ * (blk + 1)))
                            if blk % 2 == 0 and blk >= 2:
                                pe.wait_ge(c_copied.sem, c_copied.at(b, blk // 2))
                        for j in range(NJ):
                            a = pe.matmul(PS[QUAD * j:QUAD * j + KD + 1, 6, :], V[:, st, HT * j + blk // 2, :],
                                          PROB[:, blk % 2, j, half, :], start=(st == 0), stop=(st == NT - 1))
                        if half == 1:
                            a.then_inc(pv_done.sem, 1)
                    if i == 0 and 1 <= g <= HT:
                        pe.wait_ge(max_split.sem, max_split.at(b, g))
                        if r >= 2:
                            pe.wait_ge(cn_made.sem, cn_made.at(b, r - 1))
                        pe.transpose(PS[0:2 * NT * NJ, 7, 0:P], max_parts[:, (g - 1) % 2, :], ident[:, :]).then_inc(max_turned.sem, 1)
                    if s % PER_ROUND == PER_ROUND - 1 and r >= 1:
                        pe.wait_ge(c_copied.sem, c_copied.at(b, r))
                        if r + 1 <= HT:
                            pe.wait_ge(max_copied.sem, max_copied.at(b, min(r + 2, HT)))
                        if r >= 2:
                            pe.wait_ge(cn_made.sem, cn_made.at(b, r - 1))
                        for t in range(NT):
                            a = pe.transpose(PS[:, 7, t * P:(t + 1) * P], C[:, (r - 1) % 2, t * P:(t + 1) * P], ident[:, :])
                        a.then_inc(c_turned.sem, 1)

                pe.wait_ge(cn_made.sem, cn_made.at(b, HT))
                for j in range(NJ):
                    for t in range(NT):
                        a = pe.transpose(PS[:, j, t * P:(t + 1) * P], CN[:, t, j * P:(j + 1) * P], ident[:, :])
                    a.then_inc(cn_turned.sem, 1)
                pe.wait_ge(ctxT_made.sem, ctxT_made.at(b, NJ))
                for t in range(NT):
                    a = product(PS[:, 4 + t // 2, (t % 2) * D:(t % 2) * D + D],
                                lambda k: ctxT[:, k, t * P:(t + 1) * P], lambda k: MWO[:, k, :], NJ)
                    if t % 2:
                        a.then_inc(mo_done.sem, 1)
                pe.wait_ge(z_made.sem, z_made.at(b, 3))
                turn(6, nat)
                pe.wait_ge(sum_wide_made.sem, sum_wide_made.at(b, 2))
                product(PS[:, 5, 0:E], lambda k: sum_wide[:, k, :], lambda k: FRW[:, k, :], ND).then_inc(route_done.sem, 1)
                pe.wait_ge(experts_loaded.sem, experts_loaded.at(b, 4 * 16))
                for e in range(TOP):
                    for i in range(NF):
                        n = e * NF + i
                        if n >= 4:
                            pe.wait_ge(gelu_made.sem, gelu_made.at(b, n - 3))
                        product(PS[:, n % 4, :], lambda k: EW1[:, e, k, i * P:(i + 1) * P], lambda k: actT[:, k, :],
                                ND).then_inc(eh_done.sem, 1)
                for e in range(TOP):
                    pe.wait_ge(gelu_made.sem, gelu_made.at(b, NF * (e + 1)))
                    for t in range(NT):
                        a = product(PS[:, 4 + 2 * e + t // 2, (t % 2) * D:(t % 2) * D + D],
                                    lambda k: geluT[:, e, k, t * P:(t + 1) * P], lambda k: EW2[:, e, k, :], NF)
                        if t % 2:
                            a.then_inc(eo_done.sem, 1)
                pe.wait_ge(eo_added.sem, eo_added.at(b, 2 * TOP))


_INS = ["x", "ctx_1024", "g_xattn", "g_ffn", "L0_xattn_wq", "L0_xattn_bq", "L0_xattn_wk", "L0_xattn_bk",
        "L0_xattn_wv", "L0_xattn_bv", "L0_xattn_wo", "L0_xattn_bo", "L0_xattn_pos_bias", "L0_xattn_gamma",
        "L0_xattn_beta", "L0_xattn_w1", "L0_xattn_b1", "L0_xattn_w2", "L0_xattn_b2", "L0_ffn_ln1_g",
        "L0_ffn_ln1_b", "L0_ffn_ln2_g", "L0_ffn_ln2_b", "L0_ffn_mha_wq", "L0_ffn_mha_bq", "L0_ffn_mha_wk",
        "L0_ffn_mha_bk", "L0_ffn_mha_wv", "L0_ffn_mha_bv", "L0_ffn_mha_wo", "L0_ffn_mha_bo", "L0_ffn_mha_rw",
        "L0_ffn_mha_rb", "L0_ffn_ffn_rw", "L0_ffn_ffn_rb", "L0_ffn_fw1", "L0_ffn_fw2"]


def kernel(**inputs):
    import numpy as _np
    import concourse.bacc as _bacc
    from concourse import mybir as _mybir
    from concourse.bass_utils import run_bass_kernel_spmd as _run

    nc = _bacc.Bacc("TRN2", target_bir_lowering=False, num_devices=1)
    arrays, args = {}, []
    for name in _INS:
        a = _np.ascontiguousarray(inputs[name])
        arrays[f"in_{name}"] = a
        args.append(nc.dram_tensor(f"in_{name}", a.shape, _mybir.dt.from_np(a.dtype), kind="ExternalInput").ap())
    out = nc.dram_tensor("out_0", (B, T, D), _mybir.dt.float32, kind="ExternalOutput").ap()
    build(nc, *args, out)
    r = _run(nc, [arrays], core_ids=[0])
    return r.results[0]["out_0"]
```

```python
from contextlib import ExitStack

import concourse.bass as bass
from concourse import mybir

ALU = mybir.AluOpType
ACT = mybir.ActivationFunctionType
AX = mybir.AxisListType
F32 = mybir.dt.float32
F32R = mybir.dt.float32r
U32 = mybir.dt.uint32

P = 128
B, T, D, H = 4, 512, 256, 1024
BAND = 64
NT = T // P
ND = D // P
NH = H // P
M, HEADS, KD = 2, 16, 16
NJ = M * D // P
HT = P // KD
E, TOP, F = 8, 2, 512
NF = F // P
EPS_XATTN, EPS_FFN = 1e-5, 1e-6
QUAD = 32

ROW_PARTS = 32
ROW_MAX = ROW_PARTS + 4 * KD
ROWS = ROW_MAX + 2
MAX_BANKS = 3
SCORE_BANK, SCORE_BANKS = 3, 3
RING = 3

STEPS = HT * NJ * 2
PER_ROUND = NJ * 2
LEAD = PER_ROUND + 3
LAST_STEP = STEPS + PER_ROUND
ROUTE_STEP = 6

VECTORS = [("bq", ND), ("bk", ND), ("bv", ND), ("gamma", ND), ("beta", ND), ("b1", NH),
           ("ln1_g", ND), ("ln1_b", ND), ("ln2_g", ND), ("ln2_b", ND),
           ("mbq", NJ), ("mbk", NJ), ("mbv", NJ)]
COL = {}
for _name, _n in VECTORS:
    COL[_name] = sum(n for _, n in VECTORS[:len(COL)])
NCOLS = sum(n for _, n in VECTORS)

DVE_LINKS = 63
POOL_LINKS = 1


class Count:

    def __init__(self, sem, per):
        self.sem, self.per = sem, per

    def at(self, b, n):
        return b * self.per + n


def build(nc, x, ctx_in, g_xattn, g_ffn, wq, bq, wk, bk, wv, bv, wo, bo, pos_bias, gamma, beta, w1, b1,
          w2, b2, ln1_g, ln1_b, ln2_g, ln2_b, mha_wq, mha_bq, mha_wk, mha_bk, mha_wv, mha_bv, mha_wo,
          mha_bo, mha_rw, mha_rb, ffn_rw, ffn_rb, fw1, fw2, out):
    stack = ExitStack()
    with stack:
        place = [(nc.sbuf_base + 31) // 32 * 32]

        def at(name, offset, shape, dt=F32):
            return nc.alloc_sbuf_tensor_at(name, shape, dt, offset=offset)

        def sb(name, shape, dt=F32):
            size = 4
            for n in shape[1:]:
                size *= n
            offset = place[0]
            place[0] += (size + 31) // 32 * 32
            return at(name, offset, shape, dt)

        def region(size):
            offset = place[0]
            place[0] += size
            return offset

        WQ = sb("WQ", [P, ND, D])
        WK = sb("WK", [P, ND, D])
        WV = sb("WV", [P, ND, D])
        WO = sb("WO", [P, ND, D])
        W1 = sb("W1", [P, ND, H])
        W2 = sb("W2", [P, NH, D])
        MWQ = sb("MWQ", [P, M, ND, D])
        MWK = sb("MWK", [P, M, ND, D])
        MWV = sb("MWV", [P, ND, M, D])
        MWO = sb("MWO", [P, NJ, D])
        RW = sb("RW", [P, ND, M])
        RB = sb("RB", [P, M])
        FRW = sb("FRW", [P, ND, E])
        FRB = sb("FRB", [P, E])
        EWT = sb("EWT", [P, NT, T])
        bo_row = sb("bo_row", [P, D])
        gamma_row = sb("gamma_row", [P, D])
        beta_b2_row = sb("beta_b2_row", [P, D])
        gated_gamma_row = sb("gated_gamma_row", [P, D])
        gated_beta_row = sb("gated_beta_row", [P, D])
        mbo_row = sb("mbo_row", [P, M, D])
        ident = sb("ident", [P, P])
        ones = sb("ones", [P, P])
        COLS = sb("COLS", [P, NCOLS])
        neg_bq = sb("neg_bq", [P, ND])
        gates = sb("gates", [P, 2])
        minus_half = sb("minus_half", [P, 4])

        stats = sb("stats", [P, NT, 6])
        mean_var = sb("mean_var", [P, NT, 2])
        var_eps = sb("var_eps", [P, 2, 4])
        rstd = sb("rstd", [P, 2, 4])
        token_sum = sb("token_sum", [P, ND])
        half_sum = sb("half_sum", [P, ND, 2])
        logits = sb("logits", [P, E])
        small = sb("small", [P, 8])
        mprob = sb("mprob", [P, M])
        mix_bo = sb("mix_bo", [P, D])
        eprob = sb("eprob", [P, E])
        top_p = sb("top_p", [P, 8])
        top_i = sb("top_i", [P, 8], U32)
        out_w = sb("out_w", [P, TOP])
        neg_max = sb("neg_max", [P, 2, NT * NJ])
        max_parts = sb("max_parts", [P, 2, 2 * NT * NJ])
        rm = region(2 * P * 4)
        max_rows = at("max_rows", rm, [2 * NT * NJ, 2, P])
        sum_wide = at("sum_wide", rm, [P, ND, P])
        denom = sb("denom", [P, NT, NJ])

        xs = sb("xs", [P, NT, D])
        emb = sb("emb", [P, NT, D])
        res = sb("res", [P, NT, D])
        rn = region(NT * NJ * P * 4)
        nat = at("nat", rn, [P, NT, D])
        CN = at("CN", rn, [P, NT, NJ * P])

        X12 = sb("X12", [P, NT, D])
        ra = region(4 * NJ * T * 4)
        embT = at("embT", ra, [P, ND, T])
        q_exp = at("q_exp", ra + 4096, [P, ND, T])
        ekT = at("ekT", ra + 8192, [P, ND, T])
        EK = at("EK", ra + 12288, [P, NT, D])
        EKV = at("EKV", ra + 16384, [P, NT, D])
        den = at("den", ra + 20480, [P, ND, T])
        k_max = at("k_max", ra + 24576, [P, ND])
        k_shift = at("k_shift", ra + 24608, [P, ND])
        yT = at("yT", ra + 24576, [P, ND, T])
        y_den = at("y_den", ra + 28672, [P, ND, T])
        q_hi = at("q_hi", ra, [P, NJ, T], F32R)
        q_lo = at("q_lo", ra + 8192, [P, NJ, T], F32R)
        k_hi = at("k_hi", ra + 16384, [P, NJ, T], F32R)
        k_lo = at("k_lo", ra + 24576, [P, NJ, T], F32R)
        rv = region(NT * NJ * HT * (KD + 1) * 4)
        V = at("V", rv, [P, NT, NJ * HT, KD + 1])
        rb = region(2 * NJ * 2 * T * 4)
        hT = at("hT", rb, [P, NH, T])
        PROB = at("PROB", rb, [P, 2, NJ, 2, T])
        n2T = at("n2T", rb + 20480, [P, ND, T])
        geluT = at("geluT", rb + 24576, [P, NF, T])
        actT = at("actT", rb + 4 * NH * T, [P, ND, T])
        rc = region(2 * T * 4)
        C = at("C", rc, [P, 2, T])
        QS = sb("QS", [P, RING, NJ, T], F32R)
        KS = sb("KS", [P, RING, NJ, T], F32R)
        EW1 = [at("EW1a", rv, [P, ND, F]), at("EW1b", rv + 4096, [P, ND, F])]
        EW2 = [at("EW2a", rc, [P, NF, D]), at("EW2b", rn + 4096, [P, NF, D])]
        ctxT = at("ctxT", ra + 16384, [P, NJ, T])
        POS = at("POS", ra, [P, NT, T])
        EWN = at("EWN", ra + 8192, [P, NT, T])
        pos_max = at("pos_max", ra + 24576, [P, NT])
        vec_rows = at("vec_rows", ra + 16384, [NCOLS, P])
        beta_row = at("beta_row", ra + 20480, [P, D])
        assert place[0] <= nc.sbuf_top, (place[0], nc.sbuf_top)

        PS = stack.enter_context(nc.psum_tensor("PS", [P, 8, 512], F32))

        def sem(name):
            return stack.enter_context(nc.semaphore(name))

        def count(name, per):
            return Count(sem(name), per)

        rows_loaded = sem("rows_loaded")
        vectors_loaded = sem("vectors_loaded")
        xattn_loaded = sem("xattn_loaded")
        pos_loaded = sem("pos_loaded")
        mlp_loaded = sem("mlp_loaded")
        mha_loaded = sem("mha_loaded")
        gates_loaded = sem("gates_loaded")
        consts_made = sem("consts_made")
        ident_made = sem("ident_made")
        pos_masked = sem("pos_masked")
        pos_max_made = sem("pos_max_made")
        pos_exp_made = sem("pos_exp_made")
        pos_turned = sem("pos_turned")
        pos_copied = sem("pos_copied")
        vectors_turned = sem("vectors_turned")
        vectors_copied = sem("vectors_copied")
        gates_made = sem("gates_made")
        rows_made = sem("rows_made")
        setup_link = sem("setup_link")
        wait_carrier = sem("wait_carrier")

        x_loaded = count("x_loaded", 32)
        var_made = count("var_made", 10)
        rstd_made = count("rstd_made", 10)
        emb_made = count("emb_made", 2)
        emb_bo_made = count("emb_bo_made", 1)
        xs_beta_made = count("xs_beta_made", 1)
        z_made = count("z_made", 6)
        turned = count("turned", 8)
        actT_made = count("actT_made", 4)
        q_done = count("q_done", ND)
        k_done = count("k_done", ND)
        v_done = count("v_done", 2)
        k_max_made = count("k_max_made", ND)
        q_exp_made = count("q_exp_made", ND)
        ekT_made = count("ekT_made", ND)
        ek_turned = count("ek_turned", 2)
        ek_copied = count("ek_copied", 2)
        ekv_made = count("ekv_made", 2)
        den_done = count("den_done", ND)
        num_done = count("num_done", ND)
        den_copied = count("den_copied", ND)
        y_made = count("y_made", ND)
        attn_done = count("attn_done", 2)
        attn_added = count("attn_added", 2)
        a_res_made = count("a_res_made", 1)
        h_done = count("h_done", NH)
        h_even = count("h_even", NH // 2)
        h_odd = count("h_odd", NH // 2)
        ff_done = count("ff_done", 2)
        ff_added = count("ff_added", 2)
        x1_made = count("x1_made", 1)
        xf_made = count("xf_made", 2)
        sum_wide_made = count("sum_wide_made", 2)
        route_done = count("route_done", 2)
        logits_made = count("logits_made", 2)
        probs_exp = count("probs_exp", 2)
        mprob_made = count("mprob_made", 1)
        res2_made = count("res2_made", 1)
        mix_bo_made = count("mix_bo_made", 1)
        qk_done = count("qk_done", 2 * NJ)
        qk_hi = count("qk_hi", 2 * NJ)
        qk_lo = count("qk_lo", 2 * NJ)
        mv_done = count("mv_done", NT)
        mv_copied = count("mv_copied", NT)
        v_ones = count("v_ones", 1)
        stacked = [count(f"stacked{s}", 8 * 16 * len(range(s, HT, RING))) for s in range(RING)]
        max_mm = count("max_mm", 2 * STEPS)
        max_red = count("max_red", 2 * STEPS)
        max_split = count("max_split", HT)
        max_turned = count("max_turned", HT)
        max_copied = count("max_copied", HT)
        max_stacked = [count(f"max_stacked{s}", 2 * 16 * len(range(s, HT, 2))) for s in range(2)]
        scored = count("scored", 2 * STEPS)
        exped = count("exped", 2 * STEPS)
        pv_done = count("pv_done", 2 * HT)
        c_copied = count("c_copied", HT)
        c_turned = count("c_turned", HT)
        cn_made = count("cn_made", HT)
        cn_turned = count("cn_turned", NJ)
        ctxT_made = count("ctxT_made", NJ)
        mo_done = count("mo_done", 2)
        mo_added = count("mo_added", 2)
        x12_made = count("x12_made", 1)
        chosen = count("chosen", 1)
        experts_loaded = count("experts_loaded", 4 * 16)
        eh_done = count("eh_done", TOP * NF)
        gelu_made = count("gelu_made", TOP * NF)
        eo_done = count("eo_done", 2 * TOP)
        eo_added = count("eo_added", 2 * TOP)
        stored = count("stored", 16)
        link = count("dve_link", DVE_LINKS)
        pool_link = count("pool_link", POOL_LINKS)

        x_v = x.rearrange("b (n p) d -> b p n d", p=P)
        c_v = ctx_in.rearrange("b (n p) d -> b p n d", p=P)
        o_v = out.rearrange("b (n p) d -> b p n d", p=P)
        fw1_v = fw1.rearrange("e (k p) f -> e p k f", p=P)
        fw2_v = fw2.rearrange("e (k p) d -> e p k d", p=P)

        def row(v):
            return v.rearrange("(a d) -> a d", a=1)

        block = stack.enter_context(nc.Block())

        HALVES = ((0, 2), (2, 4))
        HW = 2 * P

        def col(name, i):
            return COLS[:, COL[name] + i:COL[name] + i + 1]

        @block.sync
        def _(sp):
            vecs = {"bq": bq, "bk": bk, "bv": bv, "gamma": gamma, "beta": beta, "b1": b1,
                    "ln1_g": ln1_g, "ln1_b": ln1_b, "ln2_g": ln2_g, "ln2_b": ln2_b}
            mvecs = {"mbq": mha_bq, "mbk": mha_bk, "mbv": mha_bv}

            def load_x(b):
                sp.dma_start(xs[:, :, :], x_v[b, :, :, :]).then_inc(x_loaded.sem, 16)
                sp.dma_start(emb[:, :, :], c_v[b, :, :, :]).then_inc(x_loaded.sem, 16)

            def load_experts(b):
                sp.wait_ge(chosen.sem, chosen.at(b, 1))
                sp.sem_inc(wait_carrier, 1)
                for e in range(TOP):
                    i = sp.value_load(top_i[0:1, e:e + 1], min_val=0, max_val=E - 1)
                    sp.dma_start(EW1[e][:, :, :], fw1_v[i, :, :, :]).then_inc(experts_loaded.sem, 16)
                    sp.dma_start(EW2[e][:, :, :], fw2_v[i, :, :, :]).then_inc(experts_loaded.sem, 16)

            def store(b):
                sp.wait_ge(eo_added.sem, eo_added.at(b, 2 * TOP))
                sp.dma_start(o_v[b, :, :, :], X12[:, :, :]).then_inc(stored.sem, 16)

            def stack_rounds(b):
                def stack_round(r):
                    s = r % RING
                    for n, (dst, src) in enumerate(((QS, q_hi), (QS, q_hi), (QS, q_lo), (QS, q_lo),
                                                    (KS, k_hi), (KS, k_lo), (KS, k_hi), (KS, k_lo))):
                        at0 = ROW_PARTS + KD * (n % 4)
                        sp.dma_start(dst[at0:at0 + KD, s, :, :].bitcast(F32),
                                     src[KD * r:KD * r + KD, :, :].bitcast(F32)).then_inc(stacked[s].sem, 16)

                def stack_max(r):
                    s = r % RING
                    sp.wait_ge(max_copied.sem, max_copied.at(b, r + 1))
                    for part in range(2):
                        n = NT * NJ
                        dst = QS[ROW_MAX + part:ROW_MAX + part + 1, s, :, :].bitcast(F32)
                        sp.dma_start(dst.rearrange("a j (n c) -> a (j n) c", c=P),
                                     max_rows[part * n:part * n + n, r % 2, :]).then_inc(max_stacked[r % 2].sem, 16)

                sp.wait_ge(qk_lo.sem, qk_lo.at(b, 2 * NJ))
                sp.wait_ge(qk_hi.sem, qk_hi.at(b, 2 * NJ))
                for r in range(RING):
                    stack_round(r)
                for r in range(HT):
                    stack_max(r)
                    if r + 2 >= RING and r + 2 < HT:
                        sp.wait_ge(scored.sem, scored.at(b, 2 * PER_ROUND * (r + 3 - RING)))
                        stack_round(r + 2)

            load_x(0)
            for name, n in VECTORS:
                if name in vecs:
                    src = vecs[name].rearrange("(k p) -> k p", p=P)
                else:
                    src = mvecs[name].rearrange("m h k -> (m h k)").rearrange("(j p) -> j p", p=P)
                sp.dma_start(vec_rows[COL[name]:COL[name] + n, :], src).then_inc(vectors_loaded, 16)
            sp.dma_start(POS[:, :, :], pos_bias.rearrange("(n p) j -> p n j", p=P)).then_inc(pos_loaded, 16)
            for dst, src in ((WQ, wq), (WK, wk), (WV, wv), (WO, wo)):
                sp.dma_start(dst[:, :, :], src.rearrange("(k p) n -> p k n", p=P)).then_inc(xattn_loaded, 16)
            for dst, src in ((bo_row, row(bo)), (gamma_row, row(gamma)), (beta_row, row(beta)),
                             (beta_b2_row, row(b2)), (RB, row(mha_rb)), (FRB, row(ffn_rb))):
                sp.dma_start(dst[:, :], src.broadcast_to([P, src.shape[1]])).then_inc(rows_loaded, 16)
            for m in range(M):
                sp.dma_start(mbo_row[:, m, :], mha_bo[m:m + 1, :].broadcast_to([P, D])).then_inc(rows_loaded, 16)
            for n, g in enumerate((g_xattn, g_ffn)):
                sp.dma_start(gates[:, n:n + 1], row(g).broadcast_to([P, 1])).then_inc(gates_loaded, 16)
            sp.dma_start(W1[:, :, :], w1.rearrange("(k p) n -> p k n", p=P)).then_inc(mlp_loaded, 16)
            sp.dma_start(W2[:, :, :], w2.rearrange("(k p) n -> p k n", p=P)).then_inc(mlp_loaded, 16)
            for m in range(M):
                for dst, src in ((MWQ[:, m, :, :], mha_wq), (MWK[:, m, :, :], mha_wk), (MWV[:, :, m, :], mha_wv)):
                    v = src.rearrange("m (k p) h d -> m p k (h d)", p=P)
                    sp.dma_start(dst, v[m, :, :, :]).then_inc(mha_loaded, 16)
            sp.dma_start(MWO[:, :, :], mha_wo.rearrange("m h k d -> (m h k) d")
                         .rearrange("(j p) d -> p j d", p=P)).then_inc(mha_loaded, 16)
            sp.dma_start(RW[:, :, :], mha_rw.rearrange("(k p) m -> p k m", p=P)).then_inc(mha_loaded, 16)
            sp.dma_start(FRW[:, :, :], ffn_rw.rearrange("(k p) m -> p k m", p=P)).then_inc(mha_loaded, 16)

            stack_rounds(0)
            with sp.Fori(1, B) as b:
                sp.wait_ge(x12_made.sem, x12_made.at(b - 1, 1))
                sp.wait_ge(res2_made.sem, res2_made.at(b - 1, 1))
                load_x(b)
                load_experts(b - 1)
                store(b - 1)
                stack_rounds(b)
            load_experts(B - 1)
            store(B - 1)
            sp.wait_ge(stored.sem, stored.at(B - 1, 16))

        @block.gpsimd
        def _(pool):
            nc.gpsimd.memset(ident[:, :], 0.0).then_inc(ident_made, 1)
            pool.wait_ge(ident_made, 1)
            nc.gpsimd.affine_select(out=ident[:, :], in_=ident[:, :], compare_op=ALU.not_equal, fill=1.0,
                                    base=0, pattern=[[-1, P]], channel_multiplier=1).then_inc(ident_made, 1)
            nc.gpsimd.memset(minus_half[:, :], -0.5).then_inc(consts_made, 1)
            pool.wait_ge(pos_loaded, 16)
            for n in range(NT):
                nc.gpsimd.affine_select(out=POS[:, n, :], in_=POS[:, n, :], compare_op=ALU.is_ge, fill=0.0,
                                        base=BAND - 1 - n * P, pattern=[[1, T]],
                                        channel_multiplier=-1).then_inc(pos_masked, 1)
            pool.wait_ge(pos_masked, NT)
            for n in range(NT):
                nc.gpsimd.affine_select(out=POS[:, n, :], in_=POS[:, n, :], compare_op=ALU.is_ge, fill=0.0,
                                        base=BAND - 1 + n * P, pattern=[[-1, T]],
                                        channel_multiplier=1).then_inc(pos_masked, 1)
            pool.wait_ge(rows_loaded, 16 * 8)
            nc.gpsimd.tensor_tensor(beta_b2_row[:, :], beta_b2_row[:, :], beta_row[:, :], ALU.add).then_inc(rows_made, 1)
            pool.wait_ge(gates_made, 1)
            nc.gpsimd.tensor_scalar(gated_gamma_row[:, :], gamma_row[:, :], gates[:, 0:1], None, ALU.mult).then_inc(rows_made, 1)
            nc.gpsimd.tensor_scalar(gated_beta_row[:, :], beta_row[:, :], gates[:, 0:1], None, ALU.mult).then_inc(rows_made, 1)
            pool.wait_ge(rows_made, 3)
            pool.wait_ge(consts_made, 1)

            def batch_row(b):
                def roots(n):
                    for h in range(2):
                        pool.wait_ge(var_made.sem, var_made.at(b, 2 * n + h + 1))
                        w = 4 if n == 3 else 2
                        nc.gpsimd.tensor_tensor(rstd[:, h, 0:w], var_eps[:, h, 0:w], minus_half[:, 0:w],
                                                ALU.pow).then_inc(rstd_made.sem, 1)

                def wide(v):
                    return v[:, :].rearrange("p (a d) -> p a d", a=1).broadcast_to([P, NT, D])

                roots(0)
                pool.wait_ge(x_loaded.sem, x_loaded.at(b, 32))
                pool.wait_ge(emb_made.sem, emb_made.at(b, 2))
                nc.gpsimd.tensor_tensor(res[:, :, :], emb[:, :, :], wide(bo_row), ALU.add).then_inc(emb_bo_made.sem, 1)
                nc.gpsimd.tensor_tensor(xs[:, :, :], xs[:, :, :], wide(gated_beta_row), ALU.add).then_inc(xs_beta_made.sem, 1)
                roots(1)
                pool.wait_ge(z_made.sem, z_made.at(b, 2))
                nc.gpsimd.tensor_tensor(res[:, :, :], nat[:, :, :], wide(gamma_row), ALU.mult).then_inc(pool_link.sem, 1)
                pool.wait_ge(pool_link.sem, pool_link.at(b, 1))
                nc.gpsimd.tensor_tensor(res[:, :, :], res[:, :, :], wide(beta_b2_row), ALU.add).then_inc(a_res_made.sem, 1)
                roots(2)
                roots(3)
                pool.wait_ge(mix_bo_made.sem, mix_bo_made.at(b, 1))
                nc.gpsimd.tensor_tensor(res[:, :, :], emb[:, :, :], wide(mix_bo), ALU.add).then_inc(res2_made.sem, 1)
                roots(4)

            batch_row(0)
            with pool.Fori(1, B) as b:
                batch_row(b)

        @block.scalar
        def _(act):
            act.wait_ge(gates_loaded, 32)
            nc.scalar.activation(gates[:, :], gates[:, :], ACT.Tanh).then_inc(gates_made, 1)
            act.wait_ge(pos_max_made, 1)
            for n in range(NT):
                nc.scalar.activation(EWN[:, n, :], POS[:, n, :], ACT.Exp, bias=pos_max[:, n:n + 1]).then_inc(pos_exp_made, 1)
            act.wait_ge(vectors_copied, 2)

            def gelus(b, e, tiles):
                for i in tiles:
                    act.wait_ge(eh_done.sem, eh_done.at(b, e * NF + i + 1))
                    if e > 0 and i == 0:
                        act.wait_ge(eo_done.sem, eo_done.at(b, 2 * e))
                    act.activation(geluT[:, i, :], PS[:, 6 + i % 2, :], ACT.Gelu).then_inc(gelu_made.sem, 1)

            def batch_row(b, before):
                def affine(turn, bank, dst, scale, bias, sums):
                    for h in range(2):
                        act.wait_ge(turned.sem, turned.at(b, 2 * turn + h + 1))
                        for i in range(ND):
                            kw = dict(accum_out=half_sum[:, i, h:h + 1]) if sums else {}
                            a = act.activation(dst[:, i, h * HW:(h + 1) * HW], PS[:, bank + h, i * HW:(i + 1) * HW],
                                               ACT.Identity, scale=col(scale, i), bias=col(bias, i), **kw)
                    a.then_inc(actT_made.sem, 1)

                for h in range(2):
                    act.wait_ge(turned.sem, turned.at(b, h + 1))
                    a = act.activation(embT[:, :, h * HW:(h + 1) * HW], PS[:, h, :].rearrange("p (k t) -> p k t", k=ND), ACT.Copy)
                a.then_inc(actT_made.sem, 1)
                for i in range(ND):
                    act.wait_ge(k_max_made.sem, k_max_made.at(b, i + 1))
                    act.activation(ekT[:, i, :], PS[:, 4 + i, :], ACT.Exp, bias=k_shift[:, i:i + 1]).then_inc(ekT_made.sem, 1)
                for i in range(ND):
                    act.wait_ge(q_done.sem, q_done.at(b, i + 1))
                    act.activation(q_exp[:, i, :], PS[:, 2 + i, :], ACT.Exp, bias=neg_bq[:, i:i + 1],
                                   scale=-1.0).then_inc(q_exp_made.sem, 1)
                for i in range(2):
                    act.wait_ge(ek_turned.sem, ek_turned.at(b, i + 1))
                    act.activation(EK[:, 2 * i:2 * i + 2, :].rearrange("p a d -> p (a d)"), PS[:, 2 + i, :],
                                   ACT.Copy).then_inc(ek_copied.sem, 1)
                for i in range(ND):
                    act.wait_ge(den_done.sem, den_done.at(b, i + 1))
                    act.activation(den[:, i, :], PS[:, 4 + i, :], ACT.Copy).then_inc(den_copied.sem, 1)
                if before is not None:
                    gelus(before, 0, range(NF))
                affine(1, 4, actT, "gamma", "beta", False)
                for i in range(0, NH, 2):
                    act.wait_ge(h_done.sem, h_done.at(b, i + 1))
                    act.activation(hT[:, i, :], PS[:, i % 6, :], ACT.Relu, bias=col("b1", i)).then_inc(h_even.sem, 1)
                if before is not None:
                    gelus(before, 1, range(NF))
                affine(2, 0, actT, "ln1_g", "ln1_b", True)
                for n in range(2 * NJ):
                    j, bias, dst = n // 2, ("mbq", "mbk")[n % 2], (q_hi, k_hi)[n % 2]
                    act.wait_ge(qk_done.sem, qk_done.at(b, n + 1))
                    act.activation(dst[:, j, :], PS[:, 2 + n % 4, :], ACT.Identity, bias=col(bias, j)).then_inc(qk_hi.sem, 1)
                for t in range(NT):
                    act.wait_ge(mv_done.sem, mv_done.at(b, t + 1))
                    act.activation(V[:, t, :, 0:KD], PS[:, 6 + t % 2, :].rearrange("p (h k) -> p h k", k=KD),
                                   ACT.Copy).then_inc(mv_copied.sem, 1)
                act.wait_ge(logits_made.sem, logits_made.at(b, 1))
                act.activation(mprob[:, :], logits[:, 0:M], ACT.Exp, bias=small[:, 0:1],
                               accum_out=small[:, 1:2]).then_inc(probs_exp.sem, 1)

                for s in range(STEPS + PER_ROUND):
                    r, i = s // PER_ROUND, s % PER_ROUND
                    if s < STEPS:
                        blk = s // NJ
                        for half in range(2):
                            u = 2 * s + half
                            act.wait_ge(scored.sem, scored.at(b, u + 1))
                            if blk >= 2 and half == 0 and s % NJ == 0:
                                act.wait_ge(pv_done.sem, pv_done.at(b, blk - 1))
                            act.activation(PROB[:, blk % 2, s % NJ, half, :], PS[:, SCORE_BANK + u % SCORE_BANKS, :],
                                           ACT.Exp, scale=KD ** -0.5).then_inc(exped.sem, 1)
                    if i == 4 and r >= 1:
                        act.wait_ge(pv_done.sem, pv_done.at(b, 2 * r))
                        if r >= 3:
                            act.wait_ge(c_turned.sem, c_turned.at(b, r - 2))
                        act.activation(C[:, (r - 1) % 2, :], PS[:, 6, :], ACT.Copy).then_inc(c_copied.sem, 1)

                affine(3, 6, n2T, "ln2_g", "ln2_b", True)
                act.wait_ge(logits_made.sem, logits_made.at(b, 2))
                act.activation(eprob[:, :], logits[:, :], ACT.Exp, bias=small[:, 0:1],
                               accum_out=small[:, 1:2]).then_inc(probs_exp.sem, 1)

            batch_row(0, None)
            with act.Fori(1, B) as b:
                batch_row(b, b - 1)
            for e in range(TOP):
                gelus(B - 1, e, range(NF))

        @block.vector
        def _(dve):
            nc.vector.memset(ones[:, :], 1.0).then_inc(consts_made, 1)
            nc.vector.memset(QS[:, :, :, :].bitcast(F32), 0.0).then_inc(setup_link, 1)
            nc.vector.memset(KS[:, :, :, :].bitcast(F32), 0.0).then_inc(setup_link, 1)
            dve.wait_ge(setup_link, 2)
            for s in range(RING):
                nc.vector.memset(KS[ROW_MAX:ROWS, s, :, :].bitcast(F32), 1.0).then_inc(consts_made, 1)
            dve.wait_ge(vectors_turned, 1)
            nc.vector.tensor_copy(COLS[:, :], PS[:, 7, 0:NCOLS]).then_inc(vectors_copied, 1)
            dve.wait_ge(vectors_copied, 1)
            nc.vector.tensor_scalar(neg_bq[:, :], COLS[:, COL["bq"]:COL["bq"] + ND], -1.0, None,
                                    ALU.mult).then_inc(vectors_copied, 1)
            dve.wait_ge(pos_masked, 2 * NT)
            nc.vector.tensor_reduce(pos_max[:, :], POS[:, :, :], AX.X, ALU.max, negate=True).then_inc(pos_max_made, 1)
            for n in range(NT):
                dve.wait_ge(pos_turned, n + 1)
                nc.vector.tensor_copy(EWT[:, n, :], PS[:, n, :]).then_inc(pos_copied, 1)
            dve.wait_ge(rows_made, 3)
            dve.wait_ge(pos_copied, NT)
            dve.wait_ge(vectors_copied, 2)

            def expert_out(b, e):
                for i in range(2):
                    dve.wait_ge(eo_done.sem, eo_done.at(b, 2 * e + i + 1))
                    if e == 0:
                        dve.wait_ge(x12_made.sem, x12_made.at(b, 1))
                    else:
                        dve.wait_ge(eo_added.sem, eo_added.at(b, i + 1))
                    rows = slice(2 * i, 2 * i + 2)
                    nc.vector.scalar_tensor_tensor(X12[:, rows, :], PS[:, 6 + i, :].rearrange("p (a d) -> p a d", a=2),
                                                   out_w[:, e:e + 1], X12[:, rows, :], ALU.mult, ALU.add).then_inc(eo_added.sem, 1)

            def batch_row(b, before):
                links = [0]

                def linked(ins, alone=False):
                    links[0] += 1
                    ins.then_inc(link.sem, 1)
                    dve.wait_ge(link.sem, link.at(b, links[0]))
                    if alone:
                        dve.sem_inc(wait_carrier, 1)

                def moments(n, h, src, eps):
                    t0, t1 = HALVES[h]
                    for t in range(t0, t1):
                        a = nc.vector.bn_stats(stats[:, t, :], src[:, t, :])
                    linked(a, alone=True)
                    for t in range(t0, t1):
                        a = nc.vector.bn_aggr(mean_var[:, t, :], stats[:, t, :])
                    linked(a)
                    if n == 3:
                        nc.vector.tensor_scalar(var_eps[:, h, 2:4], mean_var[:, t0:t1, 1], 1 + EPS_FFN, eps * EPS_FFN,
                                                ALU.mult, ALU.add)
                    nc.vector.tensor_scalar(var_eps[:, h, 0:2], mean_var[:, t0:t1, 1], eps, None,
                                            ALU.add).then_inc(var_made.sem, 1)

                def normalized(n, h, src, dst, at0=0):
                    dve.wait_ge(rstd_made.sem, rstd_made.at(b, 2 * n + h + 1))
                    for t in range(*HALVES[h]):
                        c = at0 + t % 2
                        a = nc.vector.tensor_scalar(dst[:, t, :], src[:, t, :], mean_var[:, t, 0:1], rstd[:, h, c:c + 1],
                                                    ALU.subtract, ALU.mult)
                    return a

                def spread_sum():
                    linked(nc.vector.tensor_tensor(token_sum[:, :], half_sum[:, :, 0], half_sum[:, :, 1], ALU.add))
                    for i in range(ND):
                        a = nc.vector.tensor_scalar(sum_wide[:, i, :], ones[:, :], token_sum[:, i:i + 1], None, ALU.mult)
                    a.then_inc(sum_wide_made.sem, 1)

                def softmax_shift(n, width, bias):
                    dve.wait_ge(route_done.sem, route_done.at(b, n + 1))
                    linked(nc.vector.scalar_tensor_tensor(logits[:, 0:width], PS[:, 7, 0:width], 1.0 / T, bias[:, :],
                                                          ALU.mult, ALU.add))
                    nc.vector.tensor_reduce(small[:, 0:1], logits[:, 0:width], AX.X, ALU.max,
                                            negate=True).then_inc(logits_made.sem, 1)

                def half_tiles(v, h):
                    return v[:, HALVES[h][0]:HALVES[h][1], :]

                def pair(bank):
                    return PS[:, bank, :].rearrange("p (a d) -> p a d", a=2)

                dve.wait_ge(x_loaded.sem, x_loaded.at(b, 32))
                for h in range(2):
                    moments(0, h, xs, EPS_XATTN)
                if before is not None:
                    dve.wait_ge(turned.sem, turned.at(before, 8))
                for h in range(2):
                    linked(normalized(0, h, xs, nat))
                    nc.vector.tensor_tensor(half_tiles(emb, h), half_tiles(emb, h), half_tiles(nat, h), ALU.add).then_inc(emb_made.sem, 1)
                for i in range(ND):
                    dve.wait_ge(k_done.sem, k_done.at(b, i + 1))
                    linked(nc.vector.tensor_reduce(k_max[:, i:i + 1], PS[:, 4 + i, :], AX.X, ALU.max))
                    linked(nc.vector.tensor_scalar(k_max[:, i:i + 1], k_max[:, i:i + 1], col("bk", i), None, ALU.add))
                    nc.vector.tensor_tensor(k_shift[:, i:i + 1], col("bk", i), k_max[:, i:i + 1], ALU.subtract).then_inc(k_max_made.sem, 1)
                for i in range(2):
                    dve.wait_ge(v_done.sem, v_done.at(b, i + 1))
                    dve.wait_ge(ek_copied.sem, ek_copied.at(b, i + 1))
                    nc.vector.tensor_tensor(half_tiles(EKV, i), pair(i), half_tiles(EK, i), ALU.mult).then_inc(ekv_made.sem, 1)
                for i in range(ND):
                    dve.wait_ge(den_copied.sem, den_copied.at(b, i + 1))
                    dve.wait_ge(q_exp_made.sem, q_exp_made.at(b, i + 1))
                    linked(nc.vector.scalar_tensor_tensor(y_den[:, i, :], q_exp[:, i, :], 1.0, den[:, i, :], ALU.add, ALU.mult))
                    nc.vector.reciprocal(y_den[:, i, :], y_den[:, i, :])
                for i in range(ND):
                    dve.wait_ge(num_done.sem, num_done.at(b, i + 1))
                    linked(nc.vector.scalar_tensor_tensor(yT[:, i, :], den[:, i, :], col("bv", i), PS[:, 2 + i, :], ALU.mult, ALU.add))
                    nc.vector.tensor_tensor(yT[:, i, :], yT[:, i, :], y_den[:, i, :], ALU.mult).then_inc(y_made.sem, 1)
                dve.wait_ge(emb_bo_made.sem, emb_bo_made.at(b, 1))
                for i in range(2):
                    dve.wait_ge(attn_done.sem, attn_done.at(b, i + 1))
                    nc.vector.tensor_tensor(half_tiles(nat, i), pair(i), half_tiles(res, i), ALU.add).then_inc(attn_added.sem, 1)
                    dve.wait_ge(attn_added.sem, attn_added.at(b, i + 1))
                    moments(1, i, nat, EPS_XATTN)
                for h in range(2):
                    normalized(1, h, nat, nat).then_inc(z_made.sem, 1)
                if before is not None:
                    expert_out(before, 0)
                for i in range(1, NH, 2):
                    dve.wait_ge(h_done.sem, h_done.at(b, i + 1))
                    nc.vector.tensor_scalar(hT[:, i, :], PS[:, i % 6, :], col("b1", i), 0.0, ALU.add, ALU.max).then_inc(h_odd.sem, 1)
                dve.wait_ge(a_res_made.sem, a_res_made.at(b, 1))
                for i in range(2):
                    dve.wait_ge(ff_done.sem, ff_done.at(b, i + 1))
                    nc.vector.tensor_tensor(half_tiles(nat, i), pair(2 + i), half_tiles(res, i), ALU.add).then_inc(ff_added.sem, 1)
                    dve.wait_ge(ff_added.sem, ff_added.at(b, i + 1))
                    moments(2, i, nat, EPS_XATTN)
                dve.wait_ge(xs_beta_made.sem, xs_beta_made.at(b, 1))
                for h in range(2):
                    dve.wait_ge(rstd_made.sem, rstd_made.at(b, 2 * 2 + h + 1))
                    for t in range(*HALVES[h]):
                        a = nc.vector.scalar_tensor_tensor(nat[:, t, :], nat[:, t, :], mean_var[:, t, 0:1], gated_gamma_row[:, :],
                                                           ALU.subtract, ALU.mult)
                    linked(a)
                    for t in range(*HALVES[h]):
                        a = nc.vector.scalar_tensor_tensor(xs[:, t, :], nat[:, t, :], rstd[:, h, t % 2:t % 2 + 1], xs[:, t, :],
                                                           ALU.mult, ALU.add)
                    linked(a)
                    moments(3, h, xs, EPS_XATTN)
                for h in range(2):
                    normalized(3, h, xs, nat, 2).then_inc(z_made.sem, 1)
                for h in range(2):
                    normalized(3, h, xs, emb).then_inc(xf_made.sem, 1)
                if before is not None:
                    expert_out(before, 1)
                dve.wait_ge(actT_made.sem, actT_made.at(b, 3))
                spread_sum()
                for n in range(2 * NJ):
                    j, bias, hi, dst = n // 2, ("mbq", "mbk")[n % 2], (q_hi, k_hi)[n % 2], (q_lo, k_lo)[n % 2]
                    dve.wait_ge(qk_hi.sem, qk_hi.at(b, n + 1))
                    nc.vector.scalar_tensor_tensor(dst[:, j, :], PS[:, 2 + n % 4, :], col(bias, j), hi[:, j, :].bitcast(F32),
                                                   ALU.add, ALU.subtract).then_inc(qk_lo.sem, 1)
                dve.wait_ge(mv_done.sem, mv_done.at(b, 1))
                nc.vector.memset(V[:, :, :, KD:KD + 1], 1.0).then_inc(v_ones.sem, 1)

                for s in range(-LEAD, LAST_STEP + 1):
                    m = s + LEAD
                    g, i = m // PER_ROUND, m % PER_ROUND
                    if m < STEPS:
                        for half in range(2):
                            n = 2 * m + half
                            c = (i // 2) * NT + 2 * (i % 2) + half
                            dve.wait_ge(max_mm.sem, max_mm.at(b, n + 1))
                            nc.vector.tensor_reduce(neg_max[:, g % 2, c:c + 1], PS[:, n % MAX_BANKS, :], AX.X, ALU.max,
                                                    negate=True).then_inc(max_red.sem, 1)
                        if i == PER_ROUND - 1:
                            w = NT * NJ
                            dve.wait_ge(max_red.sem, max_red.at(b, 2 * m + 2))
                            if g >= 2:
                                dve.wait_ge(max_turned.sem, max_turned.at(b, g - 1))
                            linked(nc.vector.tensor_copy(max_parts[:, g % 2, 0:w].bitcast(F32R), neg_max[:, g % 2, :]))
                            nc.vector.tensor_tensor(max_parts[:, g % 2, w:2 * w].bitcast(F32R), neg_max[:, g % 2, :],
                                                    max_parts[:, g % 2, 0:w], ALU.subtract).then_inc(max_split.sem, 1)
                    if m == ROUTE_STEP + 1:
                        softmax_shift(0, M, RB)
                        dve.wait_ge(probs_exp.sem, probs_exp.at(b, 1))
                        linked(nc.vector.reciprocal(small[:, 2:3], small[:, 1:2]))
                        linked(nc.vector.tensor_scalar(mprob[:, :], mprob[:, :], small[:, 2:3], None, ALU.mult))
                        linked(nc.vector.tensor_scalar(mix_bo[:, :], mbo_row[:, 0, :], mprob[:, 0:1], None, ALU.mult))
                        nc.vector.scalar_tensor_tensor(mix_bo[:, :], mbo_row[:, 1, :], mprob[:, 1:2], mix_bo[:, :],
                                                       ALU.mult, ALU.add).then_inc(mix_bo_made.sem, 1)
                    if i == 1 and 1 <= g <= HT:
                        dve.wait_ge(max_turned.sem, max_turned.at(b, g))
                        if g >= 3:
                            q = (g - 3) % 2
                            dve.wait_ge(max_stacked[q].sem, max_stacked[q].at(b, 32 * ((g - 3) // 2 + 1)))
                        nc.vector.tensor_copy(max_rows[:, (g - 1) % 2, :], PS[0:2 * NT * NJ, 7, 0:P]).then_inc(max_copied.sem, 1)
                    r = s // PER_ROUND - 2
                    if s % PER_ROUND == 0 and 0 <= r < HT:
                        ct = PS[:, 7, :].rearrange("p (t j c) -> p t j c", t=NT, c=QUAD)
                        dve.wait_ge(c_turned.sem, c_turned.at(b, r + 1))
                        linked(nc.vector.reciprocal(denom[:, :, :], ct[:, :, :, KD]))
                        cn = CN[:, :, :].rearrange("p t (j c) -> p t j c", c=P)[:, :, :, KD * r:KD * r + KD]
                        dn = denom[:, :, :].rearrange("p t (j a) -> p t j a", a=1).broadcast_to([P, NT, NJ, KD])
                        nc.vector.tensor_tensor(cn, ct[:, :, :, 0:KD], dn, ALU.mult).then_inc(cn_made.sem, 1)

                for j in range(NJ):
                    dve.wait_ge(cn_turned.sem, cn_turned.at(b, j + 1))
                    g = j // (NJ // M)
                    nc.vector.tensor_scalar(ctxT[:, j, :], PS[:, j, :], col("mbv", j),
                                            mprob[:, g:g + 1], ALU.add, ALU.mult).then_inc(ctxT_made.sem, 1)
                dve.wait_ge(res2_made.sem, res2_made.at(b, 1))
                for i in range(2):
                    dve.wait_ge(mo_done.sem, mo_done.at(b, i + 1))
                    nc.vector.tensor_tensor(half_tiles(res, i), pair(4 + i), half_tiles(res, i), ALU.add).then_inc(mo_added.sem, 1)
                    dve.wait_ge(mo_added.sem, mo_added.at(b, i + 1))
                    moments(4, i, res, EPS_FFN)
                for h in range(2):
                    normalized(4, h, res, nat).then_inc(z_made.sem, 1)
                if before is not None:
                    dve.wait_ge(stored.sem, stored.at(before, 16))
                nc.vector.scalar_tensor_tensor(X12[:, :, :], res[:, :, :], gates[:, 1:2], xs[:, :, :], ALU.mult,
                                               ALU.add).then_inc(x12_made.sem, 1)
                dve.wait_ge(actT_made.sem, actT_made.at(b, 4))
                spread_sum()
                softmax_shift(1, E, FRB)
                dve.wait_ge(probs_exp.sem, probs_exp.at(b, 2))
                linked(nc.vector.reciprocal(small[:, 2:3], small[:, 1:2]))
                linked(nc.vector.tensor_scalar(eprob[:, :], eprob[:, :], small[:, 2:3], None, ALU.mult), alone=True)
                linked(nc.vector.max(top_p[:, :], eprob[:, :]), alone=True)
                nc.vector.max_index(top_i[:, :], top_p[:, :], eprob[:, :]).then_inc(chosen.sem, 1)
                linked(nc.vector.tensor_tensor(small[:, 3:4], top_p[:, 0:1], top_p[:, 1:2], ALU.add))
                linked(nc.vector.reciprocal(small[:, 4:5], small[:, 3:4]))
                linked(nc.vector.tensor_scalar(out_w[:, :], top_p[:, 0:TOP], small[:, 4:5], gates[:, 1:2], ALU.mult, ALU.mult))
                assert links[0] == DVE_LINKS, links[0]

            batch_row(0, None)
            with dve.Fori(1, B) as b:
                batch_row(b, b - 1)
            for e in range(TOP):
                expert_out(B - 1, e)

        @block.tensor
        def _(pe):
            pe.wait_ge(ident_made, 2)
            pe.wait_ge(vectors_loaded, 16 * len(VECTORS))
            pe.transpose(PS[:, 7, 0:NCOLS], vec_rows[:, :], ident[0:NCOLS, 0:NCOLS]).then_inc(vectors_turned, 1)
            pe.wait_ge(pos_exp_made, NT)
            for j in range(NT):
                for n in range(NT):
                    a = pe.transpose(PS[:, j, n * P:(n + 1) * P], EWN[:, n, j * P:(j + 1) * P], ident[:, :])
                a.then_inc(pos_turned, 1)
            pe.wait_ge(pos_copied, NT)
            pe.wait_ge(vectors_copied, 1)
            pe.wait_ge(xattn_loaded, 4 * 16)
            pe.wait_ge(mlp_loaded, 2 * 16)
            pe.wait_ge(mha_loaded, 9 * 16)
            pe.wait_ge(consts_made, 2 + RING)

            def product(dst, lhs, rhs, n):
                for k in range(n):
                    a = pe.matmul(dst, lhs(k), rhs(k), start=(k == 0), stop=(k == n - 1))
                return a

            def tile_out(bank, t):
                return PS[:, bank + t // 2, (t % 2) * D:(t % 2) * D + D]

            def expert_hidden(b, e, tiles):
                if e == 0 and 0 in tiles:
                    pe.wait_ge(experts_loaded.sem, experts_loaded.at(b, 4 * 16))
                    pe.wait_ge(logits_made.sem, logits_made.at(b, 2))
                for i in tiles:
                    n = e * NF + i
                    if i >= 2:
                        pe.wait_ge(gelu_made.sem, gelu_made.at(b, n - 1))
                    elif e > 0:
                        pe.wait_ge(eo_added.sem, eo_added.at(b, 2 * (e - 1) + i + 1))
                    product(PS[:, 6 + i % 2, :], lambda k: EW1[e][:, k, i * P:(i + 1) * P], lambda k: n2T[:, k, :],
                            ND).then_inc(eh_done.sem, 1)

            def expert_product(b, e, tiles):
                pe.wait_ge(gelu_made.sem, gelu_made.at(b, NF * (e + 1)))
                for t in tiles:
                    a = product(tile_out(6, t), lambda k: geluT[:, k, t * P:(t + 1) * P], lambda k: EW2[e][:, k, :], NF)
                    if t % 2:
                        a.then_inc(eo_done.sem, 1)

            def batch_row(b, before):
                def turn(bank, src, made):
                    for h in range(2):
                        pe.wait_ge(made[0].sem, made[0].at(b, made[1] + h))
                        for k in range(ND):
                            for t in range(*HALVES[h]):
                                at0 = k * HW + (t % 2) * P
                                a = pe.transpose(PS[:, bank + h, at0:at0 + P], src[:, t, k * P:(k + 1) * P], ident[:, :])
                        a.then_inc(turned.sem, 1)

                turn(0, emb, (emb_made, 1))
                pe.wait_ge(actT_made.sem, actT_made.at(b, 1))
                for i in range(ND):
                    product(PS[:, 4 + i, :], lambda k: WK[:, k, i * P:(i + 1) * P], lambda k: embT[:, k, :],
                            ND).then_inc(k_done.sem, 1)
                for i in range(ND):
                    product(PS[:, 2 + i, :], lambda k: WQ[:, k, i * P:(i + 1) * P], lambda k: embT[:, k, :],
                            ND).then_inc(q_done.sem, 1)
                for t in range(NT):
                    a = product(tile_out(0, t), lambda k: embT[:, k, t * P:(t + 1) * P], lambda k: WV[:, k, :], ND)
                    if t % 2:
                        a.then_inc(v_done.sem, 1)
                pe.wait_ge(ekT_made.sem, ekT_made.at(b, ND))
                pe.wait_ge(q_exp_made.sem, q_exp_made.at(b, ND))
                for t in range(NT):
                    for k in range(ND):
                        at0 = (t % 2) * D + k * P
                        a = pe.transpose(PS[:, 2 + t // 2, at0:at0 + P], ekT[:, k, t * P:(t + 1) * P], ident[:, :])
                    if t % 2:
                        a.then_inc(ek_turned.sem, 1)
                pe.wait_ge(ek_copied.sem, ek_copied.at(b, 2))
                for i in range(ND):
                    product(PS[:, 4 + i, :], lambda k: EK[:, k, i * P:(i + 1) * P], lambda k: EWT[:, k, :],
                            NT).then_inc(den_done.sem, 1)
                pe.wait_ge(ekv_made.sem, ekv_made.at(b, 2))
                for i in range(ND):
                    product(PS[:, 2 + i, :], lambda k: EKV[:, k, i * P:(i + 1) * P], lambda k: EWT[:, k, :],
                            NT).then_inc(num_done.sem, 1)
                if before is not None:
                    expert_hidden(before, 0, range(2))
                pe.wait_ge(y_made.sem, y_made.at(b, ND))
                for t in range(NT):
                    a = product(tile_out(0, t), lambda k: yT[:, k, t * P:(t + 1) * P], lambda k: WO[:, k, :], ND)
                    if t % 2:
                        a.then_inc(attn_done.sem, 1)
                if before is not None:
                    expert_hidden(before, 0, range(2, NF))
                turn(4, nat, (z_made, 1))
                if before is not None:
                    expert_product(before, 0, range(NT))
                pe.wait_ge(actT_made.sem, actT_made.at(b, 2))
                for i in range(NH):
                    if i >= 6:
                        done = (h_even, h_odd)[i % 2]
                        pe.wait_ge(done.sem, done.at(b, (i - 6) // 2 + 1))
                    product(PS[:, i % 6, :], lambda k: W1[:, k, i * P:(i + 1) * P], lambda k: actT[:, k, :],
                            ND).then_inc(h_done.sem, 1)
                pe.wait_ge(h_even.sem, h_even.at(b, NH // 2))
                pe.wait_ge(h_odd.sem, h_odd.at(b, NH // 2))
                for t in range(NT):
                    a = product(tile_out(2, t), lambda k: hT[:, k, t * P:(t + 1) * P], lambda k: W2[:, k, :], NH)
                    if t % 2:
                        a.then_inc(ff_done.sem, 1)
                if before is not None:
                    expert_hidden(before, 1, range(NF))
                    expert_product(before, 1, range(2))
                turn(0, nat, (z_made, 3))
                if before is not None:
                    expert_product(before, 1, range(2, NT))
                pe.wait_ge(actT_made.sem, actT_made.at(b, 3))
                for n in range(2 * NJ):
                    j, w = n // 2, (MWQ, MWK)[n % 2]
                    m, half = j // (NJ // M), j % (NJ // M)
                    if n >= 4:
                        pe.wait_ge(qk_lo.sem, qk_lo.at(b, n - 3))
                    product(PS[:, 2 + n % 4, :], lambda k: w[:, m, k, half * P:(half + 1) * P], lambda k: actT[:, k, :],
                            ND).then_inc(qk_done.sem, 1)
                if before is not None:
                    pe.wait_ge(eo_added.sem, eo_added.at(before, 2 * TOP))

                def values(t):
                    if t >= 2:
                        pe.wait_ge(mv_copied.sem, mv_copied.at(b, t - 1))
                    product(PS[:, 6 + t % 2, :], lambda k: actT[:, k, t * P:(t + 1) * P],
                            lambda k: MWV[:, k, :, :].rearrange("p m d -> p (m d)"), ND).then_inc(mv_done.sem, 1)

                values(0)
                values(1)
                pe.wait_ge(qk_lo.sem, qk_lo.at(b, 2 * NJ))

                def score_for_max(m, half):
                    g, i = m // PER_ROUND, m % PER_ROUND
                    n, t, j, slot = 2 * m + half, 2 * (i % 2) + half, i // 2, g % RING
                    if n >= MAX_BANKS:
                        pe.wait_ge(max_red.sem, max_red.at(b, n - MAX_BANKS + 1))
                    pe.matmul(PS[:, n % MAX_BANKS, :], QS[0:ROW_MAX, slot, j, t * P:(t + 1) * P], KS[0:ROW_MAX, slot, j, :],
                              start=True, stop=True).then_inc(max_mm.sem, 1)

                def score(s, half):
                    r, step, u = s // PER_ROUND, s % PER_ROUND, 2 * s + half
                    j, slot, st = step % NJ, r % RING, 2 * (step // NJ) + half
                    if u >= SCORE_BANKS:
                        pe.wait_ge(exped.sem, exped.at(b, u - SCORE_BANKS + 1))
                    pe.matmul(PS[:, SCORE_BANK + u % SCORE_BANKS, :], KS[0:ROWS, slot, j, st * P:(st + 1) * P],
                              QS[0:ROWS, slot, j, :], start=True, stop=True).then_inc(scored.sem, 1)

                for s in range(-LEAD, LAST_STEP):
                    m, r = s + LEAD, s // PER_ROUND
                    g, i = m // PER_ROUND, m % PER_ROUND
                    if m < STEPS and i == 0:
                        pe.wait_ge(stacked[g % RING].sem, stacked[g % RING].at(b, 8 * 16 * (g // RING + 1)))
                    if 0 <= s < STEPS and s % PER_ROUND == 0:
                        pe.wait_ge(max_stacked[r % 2].sem, max_stacked[r % 2].at(b, 32 * (r // 2 + 1)))
                    for half in range(2):
                        if m < STEPS:
                            score_for_max(m, half)
                        if 0 <= s < STEPS:
                            score(s, half)
                    if m in (1, 3):
                        values(2 + m // 2)
                    if m == ROUTE_STEP:
                        pe.wait_ge(mv_copied.sem, mv_copied.at(b, NT))
                        pe.wait_ge(sum_wide_made.sem, sum_wide_made.at(b, 1))
                        product(PS[:, 7, 0:M], lambda k: sum_wide[:, k, :], lambda k: RW[:, k, :], ND).then_inc(route_done.sem, 1)
                    blk = s // NJ - 1
                    if s % 2 == 1 and 0 <= blk < 2 * HT:
                        half, st = (s % NJ) // 2, 2 * (blk % 2) + (s % NJ) // 2
                        if half == 0:
                            pe.wait_ge(exped.sem, exped.at(b, 2 * NJ * (blk + 1)))
                            if blk == 0:
                                pe.wait_ge(v_ones.sem, v_ones.at(b, 1))
                            if blk % 2 == 0 and blk >= 2:
                                pe.wait_ge(c_copied.sem, c_copied.at(b, blk // 2))
                        for j in range(NJ):
                            a = pe.matmul(PS[QUAD * j:QUAD * j + KD + 1, 6, :], V[:, st, HT * j + blk // 2, :],
                                          PROB[:, blk % 2, j, half, :], start=(st == 0), stop=(st == NT - 1))
                        if half == 1:
                            a.then_inc(pv_done.sem, 1)
                    if i == 0 and 1 <= g <= HT:
                        pe.wait_ge(max_split.sem, max_split.at(b, g))
                        if g == 1:
                            pe.wait_ge(logits_made.sem, logits_made.at(b, 1))
                        if r >= 2:
                            pe.wait_ge(cn_made.sem, cn_made.at(b, r - 1))
                        pe.transpose(PS[0:2 * NT * NJ, 7, 0:P], max_parts[:, (g - 1) % 2, :], ident[:, :]).then_inc(max_turned.sem, 1)
                    if s % PER_ROUND == PER_ROUND - 1 and r >= 1:
                        pe.wait_ge(c_copied.sem, c_copied.at(b, r))
                        if r + 1 <= HT:
                            pe.wait_ge(max_copied.sem, max_copied.at(b, min(r + 2, HT)))
                        if r >= 2:
                            pe.wait_ge(cn_made.sem, cn_made.at(b, r - 1))
                        for t in range(NT):
                            a = pe.transpose(PS[:, 7, t * P:(t + 1) * P], C[:, (r - 1) % 2, t * P:(t + 1) * P], ident[:, :])
                        a.then_inc(c_turned.sem, 1)

                pe.wait_ge(cn_made.sem, cn_made.at(b, HT))
                for j in range(NJ):
                    for t in range(NT):
                        a = pe.transpose(PS[:, j, t * P:(t + 1) * P], CN[:, t, j * P:(j + 1) * P], ident[:, :])
                    a.then_inc(cn_turned.sem, 1)
                pe.wait_ge(ctxT_made.sem, ctxT_made.at(b, NJ))
                for t in range(NT):
                    a = product(tile_out(4, t), lambda k: ctxT[:, k, t * P:(t + 1) * P], lambda k: MWO[:, k, :], NJ)
                    if t % 2:
                        a.then_inc(mo_done.sem, 1)
                turn(6, nat, (z_made, 5))
                pe.wait_ge(sum_wide_made.sem, sum_wide_made.at(b, 2))
                product(PS[:, 7, 0:E], lambda k: sum_wide[:, k, :], lambda k: FRW[:, k, :], ND).then_inc(route_done.sem, 1)

            batch_row(0, None)
            with pe.Fori(1, B) as b:
                batch_row(b, b - 1)
            for e in range(TOP):
                expert_hidden(B - 1, e, range(NF))
                expert_product(B - 1, e, range(NT))


_INS = ["x", "ctx_1024", "g_xattn", "g_ffn", "L0_xattn_wq", "L0_xattn_bq", "L0_xattn_wk", "L0_xattn_bk",
        "L0_xattn_wv", "L0_xattn_bv", "L0_xattn_wo", "L0_xattn_bo", "L0_xattn_pos_bias", "L0_xattn_gamma",
        "L0_xattn_beta", "L0_xattn_w1", "L0_xattn_b1", "L0_xattn_w2", "L0_xattn_b2", "L0_ffn_ln1_g",
        "L0_ffn_ln1_b", "L0_ffn_ln2_g", "L0_ffn_ln2_b", "L0_ffn_mha_wq", "L0_ffn_mha_bq", "L0_ffn_mha_wk",
        "L0_ffn_mha_bk", "L0_ffn_mha_wv", "L0_ffn_mha_bv", "L0_ffn_mha_wo", "L0_ffn_mha_bo", "L0_ffn_mha_rw",
        "L0_ffn_mha_rb", "L0_ffn_ffn_rw", "L0_ffn_ffn_rb", "L0_ffn_fw1", "L0_ffn_fw2"]


def kernel(**inputs):
    import numpy as _np
    import concourse.bacc as _bacc
    from concourse import mybir as _mybir
    from concourse.bass_utils import run_bass_kernel_spmd as _run

    nc = _bacc.Bacc("TRN2", target_bir_lowering=False, num_devices=1)
    arrays, args = {}, []
    for name in _INS:
        a = _np.ascontiguousarray(inputs[name])
        arrays[f"in_{name}"] = a
        args.append(nc.dram_tensor(f"in_{name}", a.shape, _mybir.dt.from_np(a.dtype), kind="ExternalInput").ap())
    out = nc.dram_tensor("out_0", (B, T, D), _mybir.dt.float32, kind="ExternalOutput").ap()
    build(nc, *args, out)
    r = _run(nc, [arrays], core_ids=[0])
    return r.results[0]["out_0"]
```

```python
from contextlib import ExitStack

import concourse.bass as bass
from concourse import mybir

ALU = mybir.AluOpType
ACT = mybir.ActivationFunctionType
AX = mybir.AxisListType
F32 = mybir.dt.float32
F32R = mybir.dt.float32r
U32 = mybir.dt.uint32

P = 128
B, T, D, H = 4, 512, 256, 1024
BAND = 64
NT = T // P
ND = D // P
NH = H // P
M, HEADS, KD = 2, 16, 16
NJ = M * D // P
HT = P // KD
E, TOP, F = 8, 2, 512
NF = F // P
EPS_XATTN, EPS_FFN = 1e-5, 1e-6
QUAD = 32

ROW_PARTS = 32
ROW_MAX = ROW_PARTS + 4 * KD
ROWS = ROW_MAX + 2
MAX_BANKS = 3
SCORE_BANK, SCORE_BANKS = 3, 3
RING = 3

STEPS = HT * NJ * 2
PER_ROUND = NJ * 2
LEAD = PER_ROUND + 4
LAST_STEP = STEPS + PER_ROUND
NORM_STEP, TURN_STEP, PROJECT_STEP, QUERY_STEP = 53, 57, 61, 69
EARLY_TILES = (slice(0, 2), slice(2, 3))
EARLY = 4
ROUTE_STEP = 5

VECTORS = [("bq", ND), ("bk", ND), ("bv", ND), ("gamma", ND), ("beta", ND), ("b1", NH),
           ("ln1_g", ND), ("ln1_b", ND), ("ln2_g", ND), ("ln2_b", ND),
           ("mbq", NJ), ("mbk", NJ), ("mbv", NJ)]
COL = {}
for _name, _n in VECTORS:
    COL[_name] = sum(n for _, n in VECTORS[:len(COL)])
NCOLS = sum(n for _, n in VECTORS)

DVE_LINKS = 45
FRONT_LINKS = 10
CHOICE_LINKS = 8
POOL_LINKS = 1


class Count:

    def __init__(self, sem, per):
        self.sem, self.per = sem, per

    def at(self, b, n):
        return b * self.per + n


def build(nc, x, ctx_in, g_xattn, g_ffn, wq, bq, wk, bk, wv, bv, wo, bo, pos_bias, gamma, beta, w1, b1,
          w2, b2, ln1_g, ln1_b, ln2_g, ln2_b, mha_wq, mha_bq, mha_wk, mha_bk, mha_wv, mha_bv, mha_wo,
          mha_bo, mha_rw, mha_rb, ffn_rw, ffn_rb, fw1, fw2, out):
    stack = ExitStack()
    with stack:
        place = [(nc.sbuf_base + 31) // 32 * 32]

        def at(name, offset, shape, dt=F32):
            return nc.alloc_sbuf_tensor_at(name, shape, dt, offset=offset)

        def sb(name, shape, dt=F32):
            size = 4
            for n in shape[1:]:
                size *= n
            offset = place[0]
            place[0] += (size + 31) // 32 * 32
            return at(name, offset, shape, dt)

        def region(size):
            offset = place[0]
            place[0] += size
            return offset

        WQ = sb("WQ", [P, ND, D])
        WK = sb("WK", [P, ND, D])
        WV = sb("WV", [P, ND, D])
        WO = sb("WO", [P, ND, D])
        W1 = sb("W1", [P, ND, H])
        W2 = sb("W2", [P, NH, D])
        MWQ = sb("MWQ", [P, M, ND, D])
        MWK = sb("MWK", [P, M, ND, D])
        MWV = sb("MWV", [P, ND, M, D])
        MWO = sb("MWO", [P, NJ, D])
        RW = sb("RW", [P, ND, M])
        RB = sb("RB", [P, M])
        FRW = sb("FRW", [P, ND, E])
        FRB = sb("FRB", [P, E])
        EWT = sb("EWT", [P, NT, T])
        bo_row = sb("bo_row", [P, D])
        gamma_row = sb("gamma_row", [P, D])
        beta_b2_row = sb("beta_b2_row", [P, D])
        gated_gamma_row = sb("gated_gamma_row", [P, D])
        gated_beta_row = sb("gated_beta_row", [P, D])
        mbo_row = sb("mbo_row", [P, M, D])
        ident = sb("ident", [P, P])
        ones = sb("ones", [P, P])
        COLS = sb("COLS", [P, NCOLS])
        neg_bq = sb("neg_bq", [P, ND])
        gates = sb("gates", [P, 2])
        minus_half = sb("minus_half", [P, 4])

        stats = sb("stats", [P, NT, 6])
        mean_var = sb("mean_var", [P, NT, 2])
        var_eps = sb("var_eps", [P, 2, 4])
        rstd = sb("rstd", [P, 2, 4])
        token_sum = sb("token_sum", [P, ND])
        half_sum = sb("half_sum", [P, ND, 2])
        logits = sb("logits", [P, E])
        small = sb("small", [P, 8])
        mprob = sb("mprob", [P, M])
        mix_bo = sb("mix_bo", [P, D])
        eprob = sb("eprob", [P, E])
        top_p = sb("top_p", [P, 8])
        top_i = sb("top_i", [P, 8], U32)
        out_w = sb("out_w", [P, TOP])
        neg_max = sb("neg_max", [P, 2, NT * NJ])
        max_parts = sb("max_parts", [P, 2, 2 * NT * NJ])
        rm = region(2 * P * 4)
        max_rows = at("max_rows", rm, [2 * NT * NJ, 2, P])
        sum_wide = at("sum_wide", rm, [P, ND, P])
        denom = sb("denom", [P, NT, NJ])

        xs = sb("xs", [P, NT, D])
        emb = sb("emb", [P, NT, D])
        res = sb("res", [P, NT, D])
        rn = region(NT * NJ * P * 4)
        nat = at("nat", rn, [P, NT, D])
        CN = at("CN", rn, [P, NT, NJ * P])

        X12 = sb("X12", [P, NT, D])
        ra = region(4 * NJ * T * 4)
        embT = at("embT", ra, [P, ND, T])
        q_exp = at("q_exp", ra + 4096, [P, ND, T])
        ekT = at("ekT", ra + 8192, [P, ND, T])
        EK = at("EK", ra + 12288, [P, NT, D])
        EKV = at("EKV", ra + 16384, [P, NT, D])
        den = at("den", ra + 20480, [P, ND, T])
        x_in = at("x_in", ra + 24576, [P, NT, D])
        z_in = at("z_in", ra + 28672, [P, NT, D])
        k_max = at("k_max", ra + 28672, [P, ND])
        k_shift = at("k_shift", ra + 28704, [P, ND])
        yT = at("yT", ra + 24576, [P, ND, T])
        y_den = at("y_den", ra + 28672, [P, ND, T])
        q_hi = at("q_hi", ra, [P, NJ, T], F32R)
        q_lo = at("q_lo", ra + 8192, [P, NJ, T], F32R)
        k_parts = at("k_parts", ra + 16384, [P, 2, NJ, T], F32R)
        k_hi, k_lo = k_parts[:, 0, :, :], k_parts[:, 1, :, :]
        rv = region(NT * NJ * HT * (KD + 1) * 4)
        V = at("V", rv, [P, NT, NJ * HT, KD + 1])
        rb = region(2 * NJ * 2 * T * 4)
        hT = at("hT", rb, [P, NH, T])
        PROB = at("PROB", rb, [P, 2, NJ, 2, T])
        n2T = at("n2T", rb + 20480, [P, ND, T])
        geluT = at("geluT", rb + 24576, [P, NF, T])
        actT = at("actT", rb + 4 * NH * T, [P, ND, T])
        rc = region(2 * T * 4)
        C = at("C", rc, [P, 2, T])
        QS = sb("QS", [P, RING, NJ, T], F32R)
        KS = sb("KS", [P, RING, NJ, T], F32R)
        EW1 = [at("EW1a", rv, [P, ND, F]), at("EW1b", rv + 4096, [P, ND, F])]
        EW2 = [at("EW2a", rc, [P, NF, D]), at("EW2b", rn + 4096, [P, NF, D])]
        ctxT = at("ctxT", ra + 16384, [P, NJ, T])
        POS = at("POS", rb, [P, NT, T])
        EWN = at("EWN", rb + 8192, [P, NT, T])
        pos_max = at("pos_max", rb + 22528, [P, NT])
        vec_rows = at("vec_rows", rb + 16384, [NCOLS, P])
        beta_row = at("beta_row", rb + 20480, [P, D])
        assert place[0] <= nc.sbuf_top, (place[0], nc.sbuf_top)

        PS = stack.enter_context(nc.psum_tensor("PS", [P, 8, 512], F32))

        def sem(name):
            return stack.enter_context(nc.semaphore(name))

        def count(name, per):
            return Count(sem(name), per)

        rows_loaded = sem("rows_loaded")
        vectors_loaded = [sem("vectors_loaded0"), sem("vectors_loaded1")]
        xattn_loaded = sem("xattn_loaded")
        pos_loaded = sem("pos_loaded")
        mlp_loaded = sem("mlp_loaded")
        mha_loaded = sem("mha_loaded")
        gates_loaded = sem("gates_loaded")
        consts_made = sem("consts_made")
        ident_made = sem("ident_made")
        exponent_made = sem("exponent_made")
        pos_masked = sem("pos_masked")
        pos_max_made = sem("pos_max_made")
        pos_exp_made = sem("pos_exp_made")
        pos_turned = sem("pos_turned")
        pos_copied = sem("pos_copied")
        vectors_turned = sem("vectors_turned")
        vectors_copied = sem("vectors_copied")
        gates_made = sem("gates_made")
        rows_made = sem("rows_made")
        setup_link = sem("setup_link")
        wait_carrier = sem("wait_carrier")

        x_loaded = count("x_loaded", 16)
        context_loaded = count("context_loaded", 16)
        x_var_made = count("x_var_made", 2)
        x_rstd_made = count("x_rstd_made", 2)
        var_made = count("var_made", 8)
        rstd_made = count("rstd_made", 8)
        emb_turned = count("emb_turned", 2)
        embT_made = count("embT_made", 2)
        emb_made = count("emb_made", 2)
        emb_bo_made = count("emb_bo_made", 1)
        xs_beta_made = count("xs_beta_made", 1)
        z_made = count("z_made", 6)
        turned = count("turned", 6)
        actT_made = count("actT_made", 3)
        q_done = count("q_done", ND)
        k_done = count("k_done", ND)
        v_done = count("v_done", 2)
        k_max_made = count("k_max_made", ND)
        q_exp_made = count("q_exp_made", ND)
        ekT_made = count("ekT_made", ND)
        ek_turned = count("ek_turned", 2)
        ek_copied = count("ek_copied", 2)
        ekv_made = count("ekv_made", 2)
        den_done = count("den_done", ND)
        num_done = count("num_done", ND)
        den_copied = count("den_copied", ND)
        y_made = count("y_made", ND)
        attn_done = count("attn_done", 2)
        attn_added = count("attn_added", 2)
        a_res_made = count("a_res_made", 1)
        h_done = count("h_done", NH)
        h_even = count("h_even", NH // 2)
        h_odd = count("h_odd", NH // 2)
        ff_done = count("ff_done", 2)
        ff_added = count("ff_added", 2)
        xf_made = count("xf_made", 2)
        sum_wide_made = count("sum_wide_made", 2)
        route_done = count("route_done", 2)
        logits_made = count("logits_made", 2)
        probs_exp = count("probs_exp", 2)
        res2_made = count("res2_made", 1)
        mix_bo_made = count("mix_bo_made", 1)
        qk_done = count("qk_done", 2 * NJ)
        qk_hi = count("qk_hi", 2 * NJ)
        qk_lo = count("qk_lo", 2 * NJ)
        mv_done = count("mv_done", NT)
        mv_copied = count("mv_copied", NT)
        v_ones = count("v_ones", 1)
        stacked = [count(f"stacked{s}", 4 * 16 * len(range(s, HT, RING))) for s in range(RING)]
        stacked_early = [count(f"stacked_early{i}", 4 * 16) for i in range(len(EARLY_TILES))]
        max_mm = count("max_mm", 2 * STEPS)
        max_red = count("max_red", 2 * STEPS)
        max_split = count("max_split", HT)
        max_turned = count("max_turned", HT)
        max_copied = count("max_copied", HT)
        max_stacked = [count(f"max_stacked{s}", 16 * len(range(s, HT, 2))) for s in range(2)]
        scored = count("scored", 2 * STEPS)
        exped = count("exped", 2 * STEPS)
        pv_done = count("pv_done", 2 * HT)
        c_copied = count("c_copied", HT)
        c_turned = count("c_turned", HT)
        cn_made = count("cn_made", HT)
        cn_turned = count("cn_turned", NJ)
        ctxT_made = count("ctxT_made", NJ)
        mo_done = count("mo_done", 2)
        mo_added = count("mo_added", 2)
        x12_made = count("x12_made", 1)
        chosen = count("chosen", 1)
        w1_loaded = [count(f"w1_loaded{e}", 16) for e in range(TOP)]
        w2_loaded = [count(f"w2_loaded{e}", 16) for e in range(TOP)]
        eh_done = count("eh_done", TOP * NF)
        gelu_made = count("gelu_made", TOP * NF)
        eo_done = count("eo_done", 2 * TOP)
        eo_added = count("eo_added", 2 * TOP)
        stored = count("stored", 16)
        link = count("dve_link", DVE_LINKS)
        front_link = count("front_link", FRONT_LINKS)
        choice_link = count("choice_link", CHOICE_LINKS)
        pool_link = count("pool_link", POOL_LINKS)

        x_v = x.rearrange("b (n p) d -> b p n d", p=P)
        c_v = ctx_in.rearrange("b (n p) d -> b p n d", p=P)
        o_v = out.rearrange("b (n p) d -> b p n d", p=P)
        fw1_v = fw1.rearrange("e (k p) f -> e p k f", p=P)
        fw2_v = fw2.rearrange("e (k p) d -> e p k d", p=P)

        def row(v):
            return v.rearrange("(a d) -> a d", a=1)

        block = stack.enter_context(nc.Block())

        HALVES = ((0, 2), (2, 4))
        HW = 2 * P

        def qk_bank(n):
            return 2 + n if n < NJ else SCORE_BANK + (n - NJ) % SCORE_BANKS

        def col(name, i):
            return COLS[:, COL[name] + i:COL[name] + i + 1]

        def load_vectors(eng, vectors, done):
            sources = {"bq": bq, "bk": bk, "bv": bv, "gamma": gamma, "beta": beta, "b1": b1,
                       "ln1_g": ln1_g, "ln1_b": ln1_b, "ln2_g": ln2_g, "ln2_b": ln2_b}
            mha_sources = {"mbq": mha_bq, "mbk": mha_bk, "mbv": mha_bv}
            for name, n in vectors:
                if name in sources:
                    src = sources[name].rearrange("(k p) -> k p", p=P)
                else:
                    src = mha_sources[name].rearrange("m h k -> (m h k)").rearrange("(j p) -> j p", p=P)
                eng.dma_start(vec_rows[COL[name]:COL[name] + n, :], src).then_inc(done, 16)

        @block.sync
        def _(sp):
            def load_x(b):
                sp.dma_start(x_in[:, :, :], x_v[b, :, :, :]).then_inc(x_loaded.sem, 16)

            def load_context(b):
                sp.dma_start(emb[:, :, :], c_v[b, :, :, :]).then_inc(context_loaded.sem, 16)

            def load_experts(b):
                sp.wait_ge(chosen.sem, chosen.at(b, 1))
                sp.sem_inc(wait_carrier, 1)
                for e in range(TOP):
                    i = sp.value_load(top_i[0:1, e:e + 1], min_val=0, max_val=E - 1)
                    sp.dma_start(EW1[e][:, :, :], fw1_v[i, :, :, :]).then_inc(w1_loaded[e].sem, 16)
                    sp.dma_start(EW2[e][:, :, :], fw2_v[i, :, :, :]).then_inc(w2_loaded[e].sem, 16)

            def store(b):
                sp.wait_ge(eo_added.sem, eo_added.at(b, 2 * TOP))
                sp.dma_start(o_v[b, :, :, :], X12[:, :, :]).then_inc(stored.sem, 16)

            def stack_rounds(b, after):
                def stack_round(r, tiles=slice(0, NJ), done=None):
                    s = r % RING
                    done = done or stacked[s]
                    n = (KD, 2, (tiles.stop - tiles.start) * T)
                    k = k_parts[KD * r:KD * r + KD, :, tiles, :].rearrange("p a j t -> p a (j t)")
                    for block, q_part in enumerate((q_hi, q_lo)):
                        q = q_part[KD * r:KD * r + KD, tiles, :].rearrange("p (a j) t -> p a (j t)", a=1).broadcast_to(n)
                        for dst, src in ((QS, q), (KS, k)):
                            at0 = ROW_PARTS + 2 * KD * block
                            dst = dst[at0:at0 + 2 * KD, s, tiles, :].rearrange("p j t -> p (j t)")
                            sp.dma_start(dst.bitcast(F32), src.bitcast(F32)).then_inc(done.sem, 16)

                def stack_max(r):
                    s = r % RING
                    sp.wait_ge(max_copied.sem, max_copied.at(b, r + 1))
                    dst = QS[ROW_MAX:ROWS, s, :, :].bitcast(F32)
                    sp.dma_start(dst.rearrange("a j (n c) -> a (j n) c", c=P), max_rows[:, r % 2, :]).then_inc(max_stacked[r % 2].sem, 16)

                for tiles, done in zip(EARLY_TILES, stacked_early):
                    sp.wait_ge(qk_lo.sem, qk_lo.at(b, 2 * tiles.stop))
                    sp.wait_ge(qk_hi.sem, qk_hi.at(b, 2 * tiles.stop))
                    stack_round(0, tiles, done)
                sp.wait_ge(qk_lo.sem, qk_lo.at(b, 2 * NJ))
                sp.wait_ge(qk_hi.sem, qk_hi.at(b, 2 * NJ))
                stack_round(0, slice(EARLY_TILES[-1].stop, NJ))
                for r in range(1, RING):
                    stack_round(r)
                for r in range(HT):
                    if r == HT - 1 and after is not None:
                        sp.wait_ge(res2_made.sem, res2_made.at(b, 1))
                        load_context(after)
                        for slot in stacked:
                            sp.wait_ge(slot.sem, slot.at(b, slot.per))
                            sp.sem_inc(wait_carrier, 1)
                        load_x(after)
                    stack_max(r)
                    if r + 2 >= RING and r + 2 < HT:
                        sp.wait_ge(scored.sem, scored.at(b, 2 * PER_ROUND * (r + 3 - RING)))
                        stack_round(r + 2)

            load_x(0)
            load_context(0)
            sp.dma_start(POS[:, :, :], pos_bias.rearrange("(n p) j -> p n j", p=P)).then_inc(pos_loaded, 16)
            for dst, src in ((WK, wk), (WQ, wq), (WV, wv), (WO, wo)):
                sp.dma_start(dst[:, :, :], src.rearrange("(k p) n -> p k n", p=P)).then_inc(xattn_loaded, 16)
            for dst, src in ((bo_row, row(bo)), (gamma_row, row(gamma)), (beta_row, row(beta)),
                             (beta_b2_row, row(b2)), (RB, row(mha_rb)), (FRB, row(ffn_rb))):
                sp.dma_start(dst[:, :], src.broadcast_to([P, src.shape[1]])).then_inc(rows_loaded, 16)
            for m in range(M):
                sp.dma_start(mbo_row[:, m, :], mha_bo[m:m + 1, :].broadcast_to([P, D])).then_inc(rows_loaded, 16)
            sp.dma_start(W1[:, :, :], w1.rearrange("(k p) n -> p k n", p=P)).then_inc(mlp_loaded, 16)
            sp.dma_start(W2[:, :, :], w2.rearrange("(k p) n -> p k n", p=P)).then_inc(mlp_loaded, 16)
            for m in range(M):
                for dst, src in ((MWQ[:, m, :, :], mha_wq), (MWK[:, m, :, :], mha_wk), (MWV[:, :, m, :], mha_wv)):
                    v = src.rearrange("m (k p) h d -> m p k (h d)", p=P)
                    sp.dma_start(dst, v[m, :, :, :]).then_inc(mha_loaded, 16)
            sp.dma_start(MWO[:, :, :], mha_wo.rearrange("m h k d -> (m h k) d")
                         .rearrange("(j p) d -> p j d", p=P)).then_inc(mha_loaded, 16)
            sp.dma_start(RW[:, :, :], mha_rw.rearrange("(k p) m -> p k m", p=P)).then_inc(mha_loaded, 16)
            sp.dma_start(FRW[:, :, :], ffn_rw.rearrange("(k p) m -> p k m", p=P)).then_inc(mha_loaded, 16)

            stack_rounds(0, 1)
            with sp.Fori(1, B - 1) as b:
                load_experts(b - 1)
                store(b - 1)
                stack_rounds(b, b + 1)
            load_experts(B - 2)
            store(B - 2)
            stack_rounds(B - 1, None)
            load_experts(B - 1)
            store(B - 1)
            sp.wait_ge(stored.sem, stored.at(B - 1, 16))

        @block.gpsimd
        def _(pool):
            nc.gpsimd.memset(ident[:, :], 0.0).then_inc(ident_made, 1)
            pool.wait_ge(ident_made, 1)
            nc.gpsimd.affine_select(out=ident[:, :], in_=ident[:, :], compare_op=ALU.not_equal, fill=1.0,
                                    base=0, pattern=[[-1, P]], channel_multiplier=1).then_inc(ident_made, 1)
            nc.gpsimd.memset(minus_half[:, :], -0.5).then_inc(exponent_made, 1)
            load_vectors(pool, VECTORS[1::2], vectors_loaded[1])

            def roots(b, n):
                made, done, first = (x_var_made, x_rstd_made, 0) if n == 0 else (var_made, rstd_made, 2 * (n - 1))
                for h in range(2):
                    pool.wait_ge(made.sem, made.at(b, first + h + 1))
                    w = 4 if n == 3 else 2
                    nc.gpsimd.tensor_tensor(rstd[:, h, 0:w], var_eps[:, h, 0:w], minus_half[:, 0:w], ALU.pow).then_inc(done.sem, 1)

            def wide(v):
                return v[:, :].rearrange("p (a d) -> p a d", a=1).broadcast_to([P, NT, D])

            def residuals(b, before):
                if before is not None:
                    pool.wait_ge(x12_made.sem, x12_made.at(before, 1))
                pool.wait_ge(emb_made.sem, emb_made.at(b, 2))
                nc.gpsimd.tensor_tensor(xs[:, :, :], x_in[:, :, :], wide(gated_beta_row), ALU.add).then_inc(xs_beta_made.sem, 1)
                if before is not None:
                    pool.wait_ge(z_made.sem, z_made.at(before, 6))
                nc.gpsimd.tensor_tensor(res[:, :, :], emb[:, :, :], wide(bo_row), ALU.add).then_inc(emb_bo_made.sem, 1)

            def batch_row(b, after):
                roots(b, 1)
                pool.wait_ge(z_made.sem, z_made.at(b, 2))
                nc.gpsimd.tensor_tensor(res[:, :, :], nat[:, :, :], wide(gamma_row), ALU.mult).then_inc(pool_link.sem, 1)
                pool.wait_ge(pool_link.sem, pool_link.at(b, 1))
                nc.gpsimd.tensor_tensor(res[:, :, :], res[:, :, :], wide(beta_b2_row), ALU.add).then_inc(a_res_made.sem, 1)
                roots(b, 2)
                roots(b, 3)
                pool.wait_ge(mix_bo_made.sem, mix_bo_made.at(b, 1))
                nc.gpsimd.tensor_tensor(res[:, :, :], emb[:, :, :], wide(mix_bo), ALU.add).then_inc(res2_made.sem, 1)
                if after is not None:
                    roots(after, 0)
                roots(b, 4)
                if after is not None:
                    residuals(after, b)

            pool.wait_ge(exponent_made, 1)
            roots(0, 0)
            pool.wait_ge(pos_loaded, 16)
            for n in range(NT):
                nc.gpsimd.affine_select(out=POS[:, n, :], in_=POS[:, n, :], compare_op=ALU.is_ge, fill=0.0,
                                        base=BAND - 1 - n * P, pattern=[[1, T]],
                                        channel_multiplier=-1).then_inc(pos_masked, 1)
            pool.wait_ge(pos_masked, NT)
            for n in range(NT):
                nc.gpsimd.affine_select(out=POS[:, n, :], in_=POS[:, n, :], compare_op=ALU.is_ge, fill=0.0,
                                        base=BAND - 1 + n * P, pattern=[[-1, T]],
                                        channel_multiplier=1).then_inc(pos_masked, 1)
            pool.wait_ge(rows_loaded, 16 * 8)
            nc.gpsimd.tensor_tensor(beta_b2_row[:, :], beta_b2_row[:, :], beta_row[:, :], ALU.add).then_inc(rows_made, 1)
            pool.wait_ge(gates_made, 1)
            nc.gpsimd.tensor_scalar(gated_gamma_row[:, :], gamma_row[:, :], gates[:, 0:1], None, ALU.mult).then_inc(rows_made, 1)
            nc.gpsimd.tensor_scalar(gated_beta_row[:, :], beta_row[:, :], gates[:, 0:1], None, ALU.mult).then_inc(rows_made, 1)
            pool.wait_ge(rows_made, 3)
            pool.wait_ge(x_loaded.sem, x_loaded.at(0, 16))
            residuals(0, None)
            batch_row(0, 1)
            with pool.Fori(1, B - 1) as b:
                batch_row(b, b + 1)
            batch_row(B - 1, None)

        @block.scalar
        def _(act):
            load_vectors(act, VECTORS[0::2], vectors_loaded[0])
            for n, g in enumerate((g_xattn, g_ffn)):
                act.dma_start(gates[:, n:n + 1], row(g).broadcast_to([P, 1])).then_inc(gates_loaded, 16)

            def gelus(b, e, tiles):
                for i in tiles:
                    act.wait_ge(eh_done.sem, eh_done.at(b, e * NF + i + 1))
                    if e > 0 and i == 0:
                        act.wait_ge(eo_done.sem, eo_done.at(b, 2 * e))
                    act.activation(geluT[:, i, :], PS[:, 6 + i % 2, :], ACT.Gelu).then_inc(gelu_made.sem, 1)

            def choose_experts(b):
                act.wait_ge(logits_made.sem, logits_made.at(b, 2))
                act.activation(eprob[:, :], logits[:, :], ACT.Exp, bias=small[:, 0:1],
                               accum_out=small[:, 1:2]).then_inc(probs_exp.sem, 1)

            def copy_emb(b):
                for h in range(2):
                    act.wait_ge(emb_turned.sem, emb_turned.at(b, h + 1))
                    act.activation(embT[:, :, h * HW:(h + 1) * HW], PS[:, h, :].rearrange("p (k t) -> p k t", k=ND),
                                   ACT.Copy).then_inc(embT_made.sem, 1)

            def exp_kq(b):
                for i in range(ND):
                    act.wait_ge(k_max_made.sem, k_max_made.at(b, i + 1))
                    act.activation(ekT[:, i, :], PS[:, i, :], ACT.Exp, bias=k_shift[:, i:i + 1]).then_inc(ekT_made.sem, 1)
                for i in range(ND):
                    act.wait_ge(q_done.sem, q_done.at(b, i + 1))
                    act.activation(q_exp[:, i, :], PS[:, 2 + i, :], ACT.Exp, bias=neg_bq[:, i:i + 1],
                                   scale=-1.0).then_inc(q_exp_made.sem, 1)

            def copy_ek(b):
                for i in range(2):
                    act.wait_ge(ek_turned.sem, ek_turned.at(b, i + 1))
                    act.activation(EK[:, 2 * i:2 * i + 2, :].rearrange("p a d -> p (a d)"), PS[:, 2 + i, :],
                                   ACT.Copy).then_inc(ek_copied.sem, 1)

            def batch_row(b, before, after):
                def affine(turn, bank, dst, scale, bias, sums):
                    for h in range(2):
                        act.wait_ge(turned.sem, turned.at(b, 2 * (turn - 1) + h + 1))
                        for i in range(ND):
                            kw = dict(accum_out=half_sum[:, i, h:h + 1]) if sums else {}
                            a = act.activation(dst[:, i, h * HW:(h + 1) * HW], PS[:, bank + h, i * HW:(i + 1) * HW],
                                               ACT.Identity, scale=col(scale, i), bias=col(bias, i), **kw)
                    a.then_inc(actT_made.sem, 1)

                for i in range(ND):
                    act.wait_ge(den_done.sem, den_done.at(b, i + 1))
                    act.activation(den[:, i, :], PS[:, i, :], ACT.Copy).then_inc(den_copied.sem, 1)
                    if i == 0 and before is not None:
                        choose_experts(before)
                if before is not None:
                    gelus(before, 0, range(NF))
                affine(1, 4, actT, "gamma", "beta", False)
                for i in range(0, NH, 2):
                    act.wait_ge(h_done.sem, h_done.at(b, i + 1))
                    act.activation(hT[:, i, :], PS[:, i % 6, :], ACT.Relu, bias=col("b1", i)).then_inc(h_even.sem, 1)
                if before is not None:
                    gelus(before, 1, range(NF))
                affine(2, 0, actT, "ln1_g", "ln1_b", True)

                def high_part(n):
                    j, bias, dst = n // 2, ("mbq", "mbk")[n % 2], (q_hi, k_hi)[n % 2]
                    act.wait_ge(qk_done.sem, qk_done.at(b, n + 1))
                    act.activation(dst[:, j, :], PS[:, qk_bank(n), :], ACT.Identity, bias=col(bias, j)).then_inc(qk_hi.sem, 1)

                def copy_values(t):
                    act.wait_ge(mv_done.sem, mv_done.at(b, t + 1))
                    act.activation(V[:, t, :, 0:KD], PS[:, 6 + t % 2, :].rearrange("p (h k) -> p h k", k=KD),
                                   ACT.Copy).then_inc(mv_copied.sem, 1)

                for n in range(NJ):
                    high_part(n)
                for t in range(2):
                    copy_values(t)
                for n in range(NJ, 2 * NJ):
                    high_part(n)
                for t in range(2, NT):
                    copy_values(t)
                act.wait_ge(logits_made.sem, logits_made.at(b, 1))
                act.activation(mprob[:, :], logits[:, 0:M], ACT.Exp, bias=small[:, 0:1],
                               accum_out=small[:, 1:2]).then_inc(probs_exp.sem, 1)

                for s in range(STEPS + PER_ROUND):
                    r, i = s // PER_ROUND, s % PER_ROUND
                    if i == 4 and r >= 1:
                        act.wait_ge(pv_done.sem, pv_done.at(b, 2 * r))
                        if r >= 3:
                            act.wait_ge(c_turned.sem, c_turned.at(b, r - 2))
                        act.activation(C[:, (r - 1) % 2, :], PS[:, 6, :], ACT.Copy).then_inc(c_copied.sem, 1)
                    if s == TURN_STEP + 1 and after is not None:
                        copy_emb(after)
                    if s < STEPS:
                        blk = s // NJ
                        for half in range(2):
                            u = 2 * s + half
                            act.wait_ge(scored.sem, scored.at(b, u + 1))
                            if blk >= 2 and half == 0 and s % NJ == 0:
                                act.wait_ge(pv_done.sem, pv_done.at(b, blk - 1))
                            act.activation(PROB[:, blk % 2, s % NJ, half, :], PS[:, SCORE_BANK + u % SCORE_BANKS, :],
                                           ACT.Exp, scale=KD ** -0.5).then_inc(exped.sem, 1)
                if after is not None:
                    exp_kq(after)
                    copy_ek(after)
                affine(3, 6, n2T, "ln2_g", "ln2_b", True)

            copy_emb(0)
            act.wait_ge(gates_loaded, 32)
            nc.scalar.activation(gates[:, :], gates[:, :], ACT.Tanh).then_inc(gates_made, 1)
            act.wait_ge(pos_max_made, 1)
            for n in range(NT):
                nc.scalar.activation(EWN[:, n, :], POS[:, n, :], ACT.Exp, bias=pos_max[:, n:n + 1]).then_inc(pos_exp_made, 1)
            act.wait_ge(vectors_copied, 2)
            exp_kq(0)
            copy_ek(0)
            batch_row(0, None, 1)
            with act.Fori(1, B - 1) as b:
                batch_row(b, b - 1, b + 1)
            batch_row(B - 1, B - 2, None)
            choose_experts(B - 1)
            for e in range(TOP):
                gelus(B - 1, e, range(NF))

        @block.vector
        def _(dve):
            nc.vector.memset(ones[:, :], 1.0).then_inc(consts_made, 1)

            def zero_slot(n):
                stacks = (QS, KS)[n % 2]
                nc.vector.memset(stacks[:, n // 2, :, :].bitcast(F32), 0.0).then_inc(setup_link, 1)

            def make_linked(b, counter, links):
                def linked(ins, alone=False):
                    links[0] += 1
                    ins.then_inc(counter.sem, 1)
                    dve.wait_ge(counter.sem, counter.at(b, links[0]))
                    if alone:
                        dve.sem_inc(wait_carrier, 1)
                return linked

            def spread_sum(linked):
                linked(nc.vector.tensor_tensor(token_sum[:, :], half_sum[:, :, 0], half_sum[:, :, 1], ALU.add))
                for i in range(ND):
                    a = nc.vector.tensor_scalar(sum_wide[:, i, :], ones[:, :], token_sum[:, i:i + 1], None, ALU.mult)
                a.then_inc(sum_wide_made.sem, 1)

            def softmax_shift(b, linked, n, width, bias):
                dve.wait_ge(route_done.sem, route_done.at(b, n + 1))
                linked(nc.vector.scalar_tensor_tensor(logits[:, 0:width], PS[:, 7, 0:width], 1.0 / T, bias[:, :],
                                                      ALU.mult, ALU.add))
                nc.vector.tensor_reduce(small[:, 0:1], logits[:, 0:width], AX.X, ALU.max,
                                        negate=True).then_inc(logits_made.sem, 1)

            def sum_for_experts(b):
                dve.wait_ge(actT_made.sem, actT_made.at(b, 3))
                spread_sum(make_linked(b, choice_link, [0]))

            def moments(b, linked, n, h, src, eps):
                t0, t1 = HALVES[h]
                for t in range(t0, t1):
                    a = nc.vector.bn_stats(stats[:, t, :], src[:, t, :])
                linked(a, alone=True)
                for t in range(t0, t1):
                    a = nc.vector.bn_aggr(mean_var[:, t, :], stats[:, t, :])
                linked(a)
                if n == 3:
                    nc.vector.tensor_scalar(var_eps[:, h, 2:4], mean_var[:, t0:t1, 1], 1 + EPS_FFN, eps * EPS_FFN,
                                            ALU.mult, ALU.add)
                nc.vector.tensor_scalar(var_eps[:, h, 0:2], mean_var[:, t0:t1, 1], eps, None,
                                        ALU.add).then_inc((var_made if n else x_var_made).sem, 1)

            def normalized(b, n, h, src, dst, at0=0):
                if n == 0:
                    dve.wait_ge(x_rstd_made.sem, x_rstd_made.at(b, h + 1))
                else:
                    dve.wait_ge(rstd_made.sem, rstd_made.at(b, 2 * (n - 1) + h + 1))
                for t in range(*HALVES[h]):
                    c = at0 + t % 2
                    a = nc.vector.tensor_scalar(dst[:, t, :], src[:, t, :], mean_var[:, t, 0:1], rstd[:, h, c:c + 1],
                                                ALU.subtract, ALU.mult)
                return a

            def half_tiles(v, h):
                return v[:, HALVES[h][0]:HALVES[h][1], :]

            def pair(bank):
                return PS[:, bank, :].rearrange("p (a d) -> p a d", a=2)

            def x_moments(b, h):
                if h == 0:
                    dve.wait_ge(x_loaded.sem, x_loaded.at(b, 16))
                moments(b, make_linked(b, front_link, [2 * h]), 0, h, x_in, EPS_XATTN)

            def make_emb(b, h):
                linked = make_linked(b, front_link, [4 + h])
                linked(normalized(b, 0, h, x_in, z_in))
                if h == 0:
                    dve.wait_ge(context_loaded.sem, context_loaded.at(b, 16))
                nc.vector.tensor_tensor(half_tiles(emb, h), half_tiles(emb, h), half_tiles(z_in, h), ALU.add).then_inc(emb_made.sem, 1)

            def shift_k(b, i):
                linked = make_linked(b, front_link, [6 + 2 * i])
                dve.wait_ge(k_done.sem, k_done.at(b, i + 1))
                linked(nc.vector.tensor_reduce(k_max[:, i:i + 1], PS[:, i, :], AX.X, ALU.max))
                linked(nc.vector.tensor_scalar(k_max[:, i:i + 1], k_max[:, i:i + 1], col("bk", i), None, ALU.add))
                nc.vector.tensor_tensor(k_shift[:, i:i + 1], col("bk", i), k_max[:, i:i + 1], ALU.subtract).then_inc(k_max_made.sem, 1)

            def make_ekv(b):
                for i in range(2):
                    dve.wait_ge(v_done.sem, v_done.at(b, i + 1))
                    dve.wait_ge(ek_copied.sem, ek_copied.at(b, i + 1))
                    nc.vector.tensor_tensor(half_tiles(EKV, i), pair(4 + i), half_tiles(EK, i), ALU.mult).then_inc(ekv_made.sem, 1)

            def choose_experts(b):
                links = [1]
                linked = make_linked(b, choice_link, links)
                softmax_shift(b, linked, 1, E, FRB)
                dve.wait_ge(probs_exp.sem, probs_exp.at(b, 2))
                linked(nc.vector.reciprocal(small[:, 2:3], small[:, 1:2]))
                linked(nc.vector.tensor_scalar(eprob[:, :], eprob[:, :], small[:, 2:3], None, ALU.mult), alone=True)
                linked(nc.vector.max(top_p[:, :], eprob[:, :]), alone=True)
                nc.vector.max_index(top_i[:, :], top_p[:, :], eprob[:, :]).then_inc(chosen.sem, 1)
                linked(nc.vector.tensor_tensor(small[:, 3:4], top_p[:, 0:1], top_p[:, 1:2], ALU.add))
                linked(nc.vector.reciprocal(small[:, 4:5], small[:, 3:4]))
                linked(nc.vector.tensor_scalar(out_w[:, :], top_p[:, 0:TOP], small[:, 4:5], gates[:, 1:2], ALU.mult, ALU.mult))
                assert links[0] == CHOICE_LINKS, links[0]

            def expert_out(b, e):
                for i in range(2):
                    dve.wait_ge(eo_done.sem, eo_done.at(b, 2 * e + i + 1))
                    if e == 0:
                        dve.wait_ge(x12_made.sem, x12_made.at(b, 1))
                    else:
                        dve.wait_ge(eo_added.sem, eo_added.at(b, i + 1))
                    rows = slice(2 * i, 2 * i + 2)
                    nc.vector.scalar_tensor_tensor(X12[:, rows, :], PS[:, 6 + i, :].rearrange("p (a d) -> p a d", a=2),
                                                   out_w[:, e:e + 1], X12[:, rows, :], ALU.mult, ALU.add).then_inc(eo_added.sem, 1)

            def batch_row(b, before, after):
                links = [0]
                linked = make_linked(b, link, links)

                if before is not None:
                    sum_for_experts(before)
                    choose_experts(before)
                dve.wait_ge(xs_beta_made.sem, xs_beta_made.at(b, 1))
                for i in range(ND):
                    dve.wait_ge(den_copied.sem, den_copied.at(b, i + 1))
                    dve.wait_ge(q_exp_made.sem, q_exp_made.at(b, i + 1))
                    linked(nc.vector.scalar_tensor_tensor(y_den[:, i, :], q_exp[:, i, :], 1.0, den[:, i, :], ALU.add, ALU.mult))
                    nc.vector.reciprocal(y_den[:, i, :], y_den[:, i, :])
                for i in range(ND):
                    dve.wait_ge(num_done.sem, num_done.at(b, i + 1))
                    linked(nc.vector.scalar_tensor_tensor(yT[:, i, :], den[:, i, :], col("bv", i), PS[:, 2 + i, :], ALU.mult, ALU.add))
                    nc.vector.tensor_tensor(yT[:, i, :], yT[:, i, :], y_den[:, i, :], ALU.mult).then_inc(y_made.sem, 1)
                dve.wait_ge(emb_bo_made.sem, emb_bo_made.at(b, 1))
                for i in range(2):
                    dve.wait_ge(attn_done.sem, attn_done.at(b, i + 1))
                    if i == 0 and before is not None:
                        dve.wait_ge(turned.sem, turned.at(before, 6))
                    nc.vector.tensor_tensor(half_tiles(nat, i), pair(4 + i), half_tiles(res, i), ALU.add).then_inc(attn_added.sem, 1)
                    dve.wait_ge(attn_added.sem, attn_added.at(b, i + 1))
                    moments(b, linked, 1, i, nat, EPS_XATTN)
                for h in range(2):
                    normalized(b, 1, h, nat, nat).then_inc(z_made.sem, 1)
                if before is not None:
                    expert_out(before, 0)
                for i in range(1, NH, 2):
                    if before is None:
                        zero_slot(2 + i // 2)
                    dve.wait_ge(h_done.sem, h_done.at(b, i + 1))
                    nc.vector.tensor_scalar(hT[:, i, :], PS[:, i % 6, :], col("b1", i), 0.0, ALU.add, ALU.max).then_inc(h_odd.sem, 1)
                if before is None:
                    dve.wait_ge(setup_link, 2 * RING)
                    for r in range(RING):
                        nc.vector.memset(KS[ROW_MAX:ROWS, r, :, :].bitcast(F32), 1.0).then_inc(consts_made, 1)
                    dve.wait_ge(rows_made, 3)
                dve.wait_ge(a_res_made.sem, a_res_made.at(b, 1))
                for i in range(2):
                    dve.wait_ge(ff_done.sem, ff_done.at(b, i + 1))
                    nc.vector.tensor_tensor(half_tiles(nat, i), pair(2 + i), half_tiles(res, i), ALU.add).then_inc(ff_added.sem, 1)
                    dve.wait_ge(ff_added.sem, ff_added.at(b, i + 1))
                    moments(b, linked, 2, i, nat, EPS_XATTN)
                for h in range(2):
                    dve.wait_ge(rstd_made.sem, rstd_made.at(b, 2 + h + 1))
                    for t in range(*HALVES[h]):
                        a = nc.vector.scalar_tensor_tensor(nat[:, t, :], nat[:, t, :], mean_var[:, t, 0:1], gated_gamma_row[:, :],
                                                           ALU.subtract, ALU.mult)
                    linked(a)
                    for t in range(*HALVES[h]):
                        a = nc.vector.scalar_tensor_tensor(xs[:, t, :], nat[:, t, :], rstd[:, h, t % 2:t % 2 + 1], xs[:, t, :],
                                                           ALU.mult, ALU.add)
                    linked(a)
                    moments(b, linked, 3, h, xs, EPS_XATTN)
                for h in range(2):
                    normalized(b, 3, h, xs, nat, 2).then_inc(z_made.sem, 1)
                for h in range(2):
                    normalized(b, 3, h, xs, emb).then_inc(xf_made.sem, 1)
                if before is not None:
                    expert_out(before, 1)
                dve.wait_ge(actT_made.sem, actT_made.at(b, 2))
                spread_sum(linked)
                def low_part(n):
                    j, bias, hi, dst = n // 2, ("mbq", "mbk")[n % 2], (q_hi, k_hi)[n % 2], (q_lo, k_lo)[n % 2]
                    dve.wait_ge(qk_hi.sem, qk_hi.at(b, n + 1))
                    nc.vector.scalar_tensor_tensor(dst[:, j, :], PS[:, qk_bank(n), :], col(bias, j), hi[:, j, :].bitcast(F32),
                                                   ALU.add, ALU.subtract).then_inc(qk_lo.sem, 1)

                def maxima(m):
                    g, i = m // PER_ROUND, m % PER_ROUND
                    for half in range(2):
                        n = 2 * m + half
                        c = (i // 2) * NT + 2 * (i % 2) + half
                        dve.wait_ge(max_mm.sem, max_mm.at(b, n + 1))
                        nc.vector.tensor_reduce(neg_max[:, g % 2, c:c + 1], PS[:, n % MAX_BANKS, :], AX.X, ALU.max,
                                                negate=True).then_inc(max_red.sem, 1)

                for n in range(NJ):
                    low_part(n)
                dve.wait_ge(mv_done.sem, mv_done.at(b, 1))
                nc.vector.memset(V[:, :, :, KD:KD + 1], 1.0).then_inc(v_ones.sem, 1)
                for m in range(EARLY):
                    low_part(NJ + m)
                    maxima(m)

                for s in range(EARLY - LEAD, LAST_STEP + 1):
                    m = s + LEAD
                    g, i = m // PER_ROUND, m % PER_ROUND
                    if i == 1 and 1 <= g <= HT:
                        dve.wait_ge(max_turned.sem, max_turned.at(b, g))
                        if g >= 3:
                            q = (g - 3) % 2
                            dve.wait_ge(max_stacked[q].sem, max_stacked[q].at(b, 16 * ((g - 3) // 2 + 1)))
                        nc.vector.tensor_copy(max_rows[:, (g - 1) % 2, :], PS[0:2 * NT * NJ, 7, 0:P]).then_inc(max_copied.sem, 1)
                    if m < STEPS:
                        maxima(m)
                        if i == PER_ROUND - 1:
                            w = NT * NJ
                            dve.wait_ge(max_red.sem, max_red.at(b, 2 * m + 2))
                            if g >= 2:
                                dve.wait_ge(max_turned.sem, max_turned.at(b, g - 1))
                            linked(nc.vector.tensor_copy(max_parts[:, g % 2, 0:w].bitcast(F32R), neg_max[:, g % 2, :]))
                            nc.vector.tensor_tensor(max_parts[:, g % 2, w:2 * w].bitcast(F32R), neg_max[:, g % 2, :],
                                                    max_parts[:, g % 2, 0:w], ALU.subtract).then_inc(max_split.sem, 1)
                    if m == ROUTE_STEP + 1:
                        softmax_shift(b, linked, 0, M, RB)
                    if m == ROUTE_STEP + 2:
                        dve.wait_ge(probs_exp.sem, probs_exp.at(b, 1))
                        linked(nc.vector.reciprocal(small[:, 2:3], small[:, 1:2]))
                        linked(nc.vector.tensor_scalar(mprob[:, :], mprob[:, :], small[:, 2:3], None, ALU.mult))
                        linked(nc.vector.tensor_scalar(mix_bo[:, :], mbo_row[:, 0, :], mprob[:, 0:1], None, ALU.mult))
                        nc.vector.scalar_tensor_tensor(mix_bo[:, :], mbo_row[:, 1, :], mprob[:, 1:2], mix_bo[:, :],
                                                       ALU.mult, ALU.add).then_inc(mix_bo_made.sem, 1)
                    if after is not None:
                        if NORM_STEP <= s < NORM_STEP + 2:
                            x_moments(after, s - NORM_STEP)
                        if NORM_STEP + 2 <= s < NORM_STEP + 4:
                            make_emb(after, s - NORM_STEP - 2)
                        if s in (PROJECT_STEP, PROJECT_STEP + 2):
                            shift_k(after, (s - PROJECT_STEP) // 2)
                    r = s // PER_ROUND - 2
                    if s % PER_ROUND == 0 and 0 <= r < HT:
                        ct = PS[:, 7, :].rearrange("p (t j c) -> p t j c", t=NT, c=QUAD)
                        dve.wait_ge(c_turned.sem, c_turned.at(b, r + 1))
                        linked(nc.vector.reciprocal(denom[:, :, :], ct[:, :, :, KD]))
                        cn = CN[:, :, :].rearrange("p t (j c) -> p t j c", c=P)[:, :, :, KD * r:KD * r + KD]
                        dn = denom[:, :, :].rearrange("p t (j a) -> p t j a", a=1).broadcast_to([P, NT, NJ, KD])
                        nc.vector.tensor_tensor(cn, ct[:, :, :, 0:KD], dn, ALU.mult).then_inc(cn_made.sem, 1)

                for j in range(NJ):
                    dve.wait_ge(cn_turned.sem, cn_turned.at(b, j + 1))
                    g = j // (NJ // M)
                    nc.vector.tensor_scalar(ctxT[:, j, :], PS[:, 4 + j, :], col("mbv", j),
                                            mprob[:, g:g + 1], ALU.add, ALU.mult).then_inc(ctxT_made.sem, 1)
                dve.wait_ge(res2_made.sem, res2_made.at(b, 1))
                for i in range(2):
                    dve.wait_ge(mo_done.sem, mo_done.at(b, i + 1))
                    nc.vector.tensor_tensor(half_tiles(res, i), PS[:, 2 * i:2 * i + 2, 0:D], half_tiles(res, i), ALU.add).then_inc(mo_added.sem, 1)
                    dve.wait_ge(mo_added.sem, mo_added.at(b, i + 1))
                    moments(b, linked, 4, i, res, EPS_FFN)
                for h in range(2):
                    normalized(b, 4, h, res, nat).then_inc(z_made.sem, 1)
                if before is not None:
                    dve.wait_ge(stored.sem, stored.at(before, 16))
                nc.vector.scalar_tensor_tensor(X12[:, :, :], res[:, :, :], gates[:, 1:2], xs[:, :, :], ALU.mult,
                                               ALU.add).then_inc(x12_made.sem, 1)
                if after is not None:
                    make_ekv(after)
                assert links[0] == DVE_LINKS, links[0]

            for h in range(2):
                x_moments(0, h)
            for h in range(2):
                make_emb(0, h)
            dve.wait_ge(vectors_turned, 1)
            nc.vector.tensor_copy(COLS[:, :], PS[:, 7, 0:NCOLS]).then_inc(vectors_copied, 1)
            dve.wait_ge(vectors_copied, 1)
            nc.vector.tensor_scalar(neg_bq[:, :], COLS[:, COL["bq"]:COL["bq"] + ND], -1.0, None,
                                    ALU.mult).then_inc(vectors_copied, 1)
            dve.wait_ge(pos_masked, 2 * NT)
            nc.vector.tensor_reduce(pos_max[:, :], POS[:, :, :], AX.X, ALU.max, negate=True).then_inc(pos_max_made, 1)
            for i in range(ND):
                shift_k(0, i)
            for n in range(NT):
                dve.wait_ge(pos_turned, n + 1)
                nc.vector.tensor_copy(EWT[:, n, :], PS[:, 4 + n, :]).then_inc(pos_copied, 1)
            for n in range(2):
                zero_slot(n)
            make_ekv(0)
            dve.wait_ge(pos_copied, NT)
            dve.wait_ge(vectors_copied, 2)
            batch_row(0, None, 1)
            with dve.Fori(1, B - 1) as b:
                batch_row(b, b - 1, b + 1)
            batch_row(B - 1, B - 2, None)
            sum_for_experts(B - 1)
            choose_experts(B - 1)
            for e in range(TOP):
                expert_out(B - 1, e)

        @block.tensor
        def _(pe):
            pe.wait_ge(ident_made, 2)
            def product(dst, lhs, rhs, n):
                for k in range(n):
                    a = pe.matmul(dst, lhs(k), rhs(k), start=(k == 0), stop=(k == n - 1))
                return a

            def tile_out(bank, t):
                return PS[:, bank + t // 2, (t % 2) * D:(t % 2) * D + D]

            def route_experts(b):
                pe.wait_ge(actT_made.sem, actT_made.at(b, 3))
                pe.wait_ge(sum_wide_made.sem, sum_wide_made.at(b, 2))
                product(PS[:, 7, 0:E], lambda k: sum_wide[:, k, :], lambda k: FRW[:, k, :], ND).then_inc(route_done.sem, 1)

            def expert_hidden(b, e, tiles):
                if 0 in tiles:
                    pe.wait_ge(w1_loaded[e].sem, w1_loaded[e].at(b, 16))
                    if e == 0:
                        pe.wait_ge(logits_made.sem, logits_made.at(b, 2))
                for i in tiles:
                    n = e * NF + i
                    if i >= 2:
                        pe.wait_ge(gelu_made.sem, gelu_made.at(b, n - 1))
                    elif e > 0:
                        pe.wait_ge(eo_added.sem, eo_added.at(b, 2 * (e - 1) + i + 1))
                    product(PS[:, 6 + i % 2, :], lambda k: EW1[e][:, k, i * P:(i + 1) * P], lambda k: n2T[:, k, :],
                            ND).then_inc(eh_done.sem, 1)

            def expert_product(b, e, tiles):
                pe.wait_ge(gelu_made.sem, gelu_made.at(b, NF * (e + 1)))
                pe.wait_ge(w2_loaded[e].sem, w2_loaded[e].at(b, 16))
                for t in tiles:
                    a = product(tile_out(6, t), lambda k: geluT[:, k, t * P:(t + 1) * P], lambda k: EW2[e][:, k, :], NF)
                    if t % 2:
                        a.then_inc(eo_done.sem, 1)

            def turn(b, bank, src, made, done):
                for h in range(2):
                    pe.wait_ge(made[0].sem, made[0].at(b, made[1] + h))
                    for k in range(ND):
                        for t in range(*HALVES[h]):
                            at0 = k * HW + (t % 2) * P
                            a = pe.transpose(PS[:, bank + h, at0:at0 + P], src[:, t, k * P:(k + 1) * P], ident[:, :])
                    a.then_inc(done.sem, 1)

            def project_k(b, i):
                if i == 0:
                    pe.wait_ge(embT_made.sem, embT_made.at(b, 2))
                product(PS[:, i, :], lambda k: WK[:, k, i * P:(i + 1) * P], lambda k: embT[:, k, :], ND).then_inc(k_done.sem, 1)

            def project_q(b, i):
                product(PS[:, 2 + i, :], lambda k: WQ[:, k, i * P:(i + 1) * P], lambda k: embT[:, k, :], ND).then_inc(q_done.sem, 1)

            def project_v(b):
                for t in range(NT):
                    a = product(tile_out(4, t), lambda k: embT[:, k, t * P:(t + 1) * P], lambda k: WV[:, k, :], ND)
                    if t % 2:
                        a.then_inc(v_done.sem, 1)

            def turn_ek(b):
                pe.wait_ge(ekT_made.sem, ekT_made.at(b, ND))
                pe.wait_ge(q_exp_made.sem, q_exp_made.at(b, ND))
                for t in range(NT):
                    for k in range(ND):
                        at0 = (t % 2) * D + k * P
                        a = pe.transpose(PS[:, 2 + t // 2, at0:at0 + P], ekT[:, k, t * P:(t + 1) * P], ident[:, :])
                    if t % 2:
                        a.then_inc(ek_turned.sem, 1)

            def batch_row(b, before, after):
                pe.wait_ge(ek_copied.sem, ek_copied.at(b, 2))
                for i in range(ND):
                    product(PS[:, i, :], lambda k: EK[:, k, i * P:(i + 1) * P], lambda k: EWT[:, k, :],
                            NT).then_inc(den_done.sem, 1)
                    if i == 0 and before is not None:
                        route_experts(before)
                pe.wait_ge(ekv_made.sem, ekv_made.at(b, 2))
                for i in range(ND):
                    product(PS[:, 2 + i, :], lambda k: EKV[:, k, i * P:(i + 1) * P], lambda k: EWT[:, k, :],
                            NT).then_inc(num_done.sem, 1)
                if before is not None:
                    expert_hidden(before, 0, range(2))
                pe.wait_ge(y_made.sem, y_made.at(b, ND))
                for t in range(NT):
                    a = product(tile_out(4, t), lambda k: yT[:, k, t * P:(t + 1) * P], lambda k: WO[:, k, :], ND)
                    if t % 2:
                        a.then_inc(attn_done.sem, 1)
                if before is not None:
                    expert_hidden(before, 0, range(2, NF))
                turn(b, 4, nat, (z_made, 1), turned)
                if before is not None:
                    expert_product(before, 0, range(NT))
                pe.wait_ge(actT_made.sem, actT_made.at(b, 1))
                if before is None:
                    pe.wait_ge(mlp_loaded, 2 * 16)
                for i in range(NH):
                    if i >= 6:
                        done = (h_even, h_odd)[i % 2]
                        pe.wait_ge(done.sem, done.at(b, (i - 6) // 2 + 1))
                    product(PS[:, i % 6, :], lambda k: W1[:, k, i * P:(i + 1) * P], lambda k: actT[:, k, :],
                            ND).then_inc(h_done.sem, 1)
                pe.wait_ge(h_even.sem, h_even.at(b, NH // 2))
                pe.wait_ge(h_odd.sem, h_odd.at(b, NH // 2))
                for t in range(NT):
                    a = product(tile_out(2, t), lambda k: hT[:, k, t * P:(t + 1) * P], lambda k: W2[:, k, :], NH)
                    if t % 2:
                        a.then_inc(ff_done.sem, 1)
                if before is not None:
                    expert_hidden(before, 1, range(NF))
                    expert_product(before, 1, range(2))
                turn(b, 0, nat, (z_made, 3), turned)
                if before is not None:
                    expert_product(before, 1, range(2, NT))
                pe.wait_ge(actT_made.sem, actT_made.at(b, 2))
                def project_qk(n):
                    j, w = n // 2, (MWQ, MWK)[n % 2]
                    m, half = j // (NJ // M), j % (NJ // M)
                    if n >= NJ:
                        last = max(k for k in range(n) if qk_bank(k) == qk_bank(n))
                        pe.wait_ge(qk_lo.sem, qk_lo.at(b, last + 1))
                    product(PS[:, qk_bank(n), :], lambda k: w[:, m, k, half * P:(half + 1) * P], lambda k: actT[:, k, :],
                            ND).then_inc(qk_done.sem, 1)

                if before is None:
                    pe.wait_ge(mha_loaded, 9 * 16)
                    pe.wait_ge(consts_made, 1 + RING)
                for n in range(NJ):
                    project_qk(n)
                if before is not None:
                    pe.wait_ge(eo_added.sem, eo_added.at(before, 2 * TOP))

                def values(t):
                    if t >= 2:
                        pe.wait_ge(mv_copied.sem, mv_copied.at(b, t - 1))
                    product(PS[:, 6 + t % 2, :], lambda k: actT[:, k, t * P:(t + 1) * P],
                            lambda k: MWV[:, k, :, :].rearrange("p m d -> p (m d)"), ND).then_inc(mv_done.sem, 1)

                for t in range(2):
                    values(t)

                def score_for_max(m, half):
                    g, i = m // PER_ROUND, m % PER_ROUND
                    n, t, j, slot = 2 * m + half, 2 * (i % 2) + half, i // 2, g % RING
                    if n >= MAX_BANKS:
                        pe.wait_ge(max_red.sem, max_red.at(b, n - MAX_BANKS + 1))
                    pe.matmul(PS[:, n % MAX_BANKS, :], QS[0:ROW_MAX, slot, j, t * P:(t + 1) * P], KS[0:ROW_MAX, slot, j, :],
                              start=True, stop=True).then_inc(max_mm.sem, 1)

                def score(s, half):
                    r, step, u = s // PER_ROUND, s % PER_ROUND, 2 * s + half
                    j, slot, st = step % NJ, r % RING, 2 * (step // NJ) + half
                    if u >= SCORE_BANKS:
                        pe.wait_ge(exped.sem, exped.at(b, u - SCORE_BANKS + 1))
                    pe.matmul(PS[:, SCORE_BANK + u % SCORE_BANKS, :], KS[0:ROWS, slot, j, st * P:(st + 1) * P],
                              QS[0:ROWS, slot, j, :], start=True, stop=True).then_inc(scored.sem, 1)

                for m in range(EARLY):
                    project_qk(NJ + m)
                    if m == 0:
                        pe.wait_ge(stacked_early[0].sem, stacked_early[0].at(b, 4 * 16))
                    for half in range(2):
                        score_for_max(m, half)
                for t in range(2, NT):
                    values(t)

                def value_product(blk, half):
                    if not 0 <= blk < 2 * HT:
                        return
                    st = 2 * (blk % 2) + half
                    if half == 0:
                        pe.wait_ge(exped.sem, exped.at(b, 2 * NJ * (blk + 1)))
                        if blk == 0:
                            pe.wait_ge(v_ones.sem, v_ones.at(b, 1))
                        if blk % 2 == 0 and blk >= 2:
                            pe.wait_ge(c_copied.sem, c_copied.at(b, blk // 2))
                    for j in range(NJ):
                        a = pe.matmul(PS[QUAD * j:QUAD * j + KD + 1, 6, :], V[:, st, HT * j + blk // 2, :],
                                      PROB[:, blk % 2, j, half, :], start=(st == 0), stop=(st == NT - 1))
                    if half == 1:
                        a.then_inc(pv_done.sem, 1)

                for s in range(EARLY - LEAD, LAST_STEP):
                    m, r = s + LEAD, s // PER_ROUND
                    if after is not None:
                        if s == TURN_STEP:
                            pe.wait_ge(max_red.sem, max_red.at(b, 2 * STEPS))
                            turn(after, 0, emb, (emb_made, 1), emb_turned)
                        if s in (PROJECT_STEP, PROJECT_STEP + 2):
                            project_k(after, (s - PROJECT_STEP) // 2)
                        if s in (QUERY_STEP, QUERY_STEP + 2):
                            if s > QUERY_STEP:
                                pe.wait_ge(exped.sem, exped.at(b, 2 * STEPS))
                            project_q(after, (s - QUERY_STEP) // 2)
                    g, i = m // PER_ROUND, m % PER_ROUND
                    if g == 0 and i == 2 * EARLY_TILES[1].start:
                        pe.wait_ge(stacked_early[1].sem, stacked_early[1].at(b, 4 * 16))
                    if m < STEPS and i == (0 if g else 2 * EARLY_TILES[1].stop):
                        pe.wait_ge(stacked[g % RING].sem, stacked[g % RING].at(b, 4 * 16 * (g // RING + 1)))
                    if 0 <= s < STEPS and s % PER_ROUND == 0:
                        pe.wait_ge(max_stacked[r % 2].sem, max_stacked[r % 2].at(b, 16 * (r // 2 + 1)))
                    if s >= 2 and s % 2 == 0:
                        value_product((s - 2) // NJ - 1, (s - 2) % NJ // 2)
                    for half in range(2):
                        if m < STEPS:
                            score_for_max(m, half)
                        if 0 <= s < STEPS:
                            score(s, half)
                    if m == ROUTE_STEP:
                        pe.wait_ge(mv_copied.sem, mv_copied.at(b, NT))
                        pe.wait_ge(sum_wide_made.sem, sum_wide_made.at(b, 1))
                        product(PS[:, 7, 0:M], lambda k: sum_wide[:, k, :], lambda k: RW[:, k, :], ND).then_inc(route_done.sem, 1)
                    if i == 0 and 1 <= g <= HT:
                        pe.wait_ge(max_split.sem, max_split.at(b, g))
                        if g == 1:
                            pe.wait_ge(logits_made.sem, logits_made.at(b, 1))
                        if r >= 2:
                            pe.wait_ge(cn_made.sem, cn_made.at(b, r - 1))
                        pe.transpose(PS[0:2 * NT * NJ, 7, 0:P], max_parts[:, (g - 1) % 2, :], ident[:, :]).then_inc(max_turned.sem, 1)
                    if s % PER_ROUND == PER_ROUND - 2 and r >= 1:
                        pe.wait_ge(c_copied.sem, c_copied.at(b, r))
                        if r + 1 <= HT:
                            pe.wait_ge(max_copied.sem, max_copied.at(b, min(r + 2, HT)))
                        if r >= 2:
                            pe.wait_ge(cn_made.sem, cn_made.at(b, r - 1))
                        for t in range(NT):
                            a = pe.transpose(PS[:, 7, t * P:(t + 1) * P], C[:, (r - 1) % 2, t * P:(t + 1) * P], ident[:, :])
                        a.then_inc(c_turned.sem, 1)


                pe.wait_ge(cn_made.sem, cn_made.at(b, HT))
                for j in range(NJ):
                    for t in range(NT):
                        a = pe.transpose(PS[:, 4 + j, t * P:(t + 1) * P], CN[:, t, j * P:(j + 1) * P], ident[:, :])
                    a.then_inc(cn_turned.sem, 1)
                if after is not None:
                    pe.wait_ge(ekT_made.sem, ekT_made.at(after, ND))
                    pe.wait_ge(q_exp_made.sem, q_exp_made.at(after, ND))
                for h in range(2):
                    for j in range(NJ):
                        if h == 0:
                            pe.wait_ge(ctxT_made.sem, ctxT_made.at(b, j + 1))
                        for t in range(*HALVES[h]):
                            a = pe.matmul(PS[:, t, 0:D], ctxT[:, j, t * P:(t + 1) * P], MWO[:, j, :],
                                          start=(j == 0), stop=(j == NJ - 1))
                    a.then_inc(mo_done.sem, 1)
                if after is not None:
                    project_v(after)
                    pe.wait_ge(mo_added.sem, mo_added.at(b, 2))
                    turn_ek(after)
                turn(b, 6, nat, (z_made, 5), turned)

            turn(0, 0, emb, (emb_made, 1), emb_turned)
            for i in range(2):
                pe.wait_ge(vectors_loaded[i], 16 * len(VECTORS[i::2]))
            pe.transpose(PS[:, 7, 0:NCOLS], vec_rows[:, :], ident[0:NCOLS, 0:NCOLS]).then_inc(vectors_turned, 1)
            pe.wait_ge(xattn_loaded, 4 * 16)
            for i in range(ND):
                project_k(0, i)
            for i in range(ND):
                project_q(0, i)
            pe.wait_ge(vectors_copied, 1)
            pe.wait_ge(pos_exp_made, NT)
            for j in range(NT):
                for n in range(NT):
                    a = pe.transpose(PS[:, 4 + j, n * P:(n + 1) * P], EWN[:, n, j * P:(j + 1) * P], ident[:, :])
                a.then_inc(pos_turned, 1)
            pe.wait_ge(pos_copied, NT)
            project_v(0)
            turn_ek(0)
            batch_row(0, None, 1)
            with pe.Fori(1, B - 1) as b:
                batch_row(b, b - 1, b + 1)
            batch_row(B - 1, B - 2, None)
            route_experts(B - 1)
            for e in range(TOP):
                expert_hidden(B - 1, e, range(NF))
                expert_product(B - 1, e, range(NT))


_INS = ["x", "ctx_1024", "g_xattn", "g_ffn", "L0_xattn_wq", "L0_xattn_bq", "L0_xattn_wk", "L0_xattn_bk",
        "L0_xattn_wv", "L0_xattn_bv", "L0_xattn_wo", "L0_xattn_bo", "L0_xattn_pos_bias", "L0_xattn_gamma",
        "L0_xattn_beta", "L0_xattn_w1", "L0_xattn_b1", "L0_xattn_w2", "L0_xattn_b2", "L0_ffn_ln1_g",
        "L0_ffn_ln1_b", "L0_ffn_ln2_g", "L0_ffn_ln2_b", "L0_ffn_mha_wq", "L0_ffn_mha_bq", "L0_ffn_mha_wk",
        "L0_ffn_mha_bk", "L0_ffn_mha_wv", "L0_ffn_mha_bv", "L0_ffn_mha_wo", "L0_ffn_mha_bo", "L0_ffn_mha_rw",
        "L0_ffn_mha_rb", "L0_ffn_ffn_rw", "L0_ffn_ffn_rb", "L0_ffn_fw1", "L0_ffn_fw2"]


def kernel(**inputs):
    import numpy as _np
    import concourse.bacc as _bacc
    from concourse import mybir as _mybir
    from concourse.bass_utils import run_bass_kernel_spmd as _run

    nc = _bacc.Bacc("TRN2", target_bir_lowering=False, num_devices=1)
    arrays, args = {}, []
    for name in _INS:
        a = _np.ascontiguousarray(inputs[name])
        arrays[f"in_{name}"] = a
        args.append(nc.dram_tensor(f"in_{name}", a.shape, _mybir.dt.from_np(a.dtype), kind="ExternalInput").ap())
    out = nc.dram_tensor("out_0", (B, T, D), _mybir.dt.float32, kind="ExternalOutput").ap()
    build(nc, *args, out)
    r = _run(nc, [arrays], core_ids=[0])
    return r.results[0]["out_0"]
```
